# Optimizing a Trainium2 kernel written in Bass

```python
import numpy as np
import jax
import jax.numpy as jnp

def _softmax(x, axis=-1):
    return jax.nn.softmax(x, axis=axis)

def _gelu(x):
    return jax.nn.gelu(x, approximate=True)

def _silu(x):
    return jax.nn.silu(x)

def _sigmoid(x):
    return jax.nn.sigmoid(x)

def _layernorm(x, axis=-1, eps=1e-05):
    m = jnp.mean(x, axis=axis, keepdims=True)
    v = jnp.var(x, axis=axis, keepdims=True)
    return (x - m) / jnp.sqrt(v + eps)

def _scatter_add(tgt, idx, src, axis=0):
    return tgt.at[idx].add(src)

def _segment_sum(src, seg, n):
    return jax.ops.segment_sum(src, seg, n)
kernel_name = 'mk_vit_tower_d1_tok_img256_r4_7ea13c'

def setup_inputs(seed: int=0):
    np.random.seed(seed)
    _w = jnp.asarray

    def _rec_inputs():
        import jax
        import jax.numpy as jnp
        _rk = jax.random.key(seed)
        x = -7.10856e-05 + 0.999911 * jax.random.normal(jax.random.fold_in(_rk, 1), (16, 64, 64, 64), jnp.float32)
        return x
    x = _rec_inputs()

    def _L0_tok_setup():
        import jax, jax.numpy as jnp
        import numpy as np
        GS = 8
        NH = 8
        DM = 64
        B, W, H = (4, 64, 64)
        key = jax.random.key(seed)
        ks = jax.random.split(key, 5)
        s = 0.02
        return {'x': jax.random.normal(ks[0], (B, DM, W, H), dtype=jnp.float32), 'Wq': jax.random.normal(ks[1], (DM, DM), dtype=jnp.float32) * s, 'bq': jnp.zeros((DM,), dtype=jnp.float32), 'Wk': jax.random.normal(ks[2], (DM, DM), dtype=jnp.float32) * s, 'bk': jnp.zeros((DM,), dtype=jnp.float32), 'Wv': jax.random.normal(ks[3], (DM, DM), dtype=jnp.float32) * s, 'bv': jnp.zeros((DM,), dtype=jnp.float32), 'Wo': jax.random.normal(ks[4], (DM, DM), dtype=jnp.float32) * s, 'bo': jnp.zeros((DM,), dtype=jnp.float32)}
    _L0_tok_all = _L0_tok_setup()
    _L0_tok_in = {k: v for k, v in _L0_tok_all.items() if k in ('Wq', 'bq', 'Wk', 'bk', 'Wv', 'bv', 'Wo', 'bo')}
    del _L0_tok_all

    def _L0_attn_setup():
        import jax, jax.numpy as jnp
        import numpy as np
        SEQ, BATCH, IN, HID = (512, 64, 64, 64)
        key = jax.random.key(seed)
        k1, k2, k3, k4, k5 = jax.random.split(key, 5)
        s = 1.0 / np.sqrt(HID)
        return {'x_in': jax.random.normal(k1, (SEQ, BATCH, IN), dtype=jnp.float32), 'W_ih': jax.random.uniform(k2, (HID, IN), jnp.float32, -s, s), 'W_hh': jax.random.uniform(k3, (HID, HID), jnp.float32, -s, s), 'b_ih': jax.random.uniform(k4, (HID,), jnp.float32, -s, s), 'b_hh': jax.random.uniform(k5, (HID,), jnp.float32, -s, s)}
    _L0_attn_all = _L0_attn_setup()
    _L0_attn_in = {k: v for k, v in _L0_attn_all.items() if k in ('W_ih', 'W_hh', 'b_ih', 'b_hh')}
    del _L0_attn_all

    def _L0_ffn_setup():
        import jax, jax.numpy as jnp
        import numpy as np
        DIM = 64
        H = 8
        D = 64
        G = 64
        INNER = H * D
        SCALE = D ** (-0.5)
        key = jax.random.key(seed)
        ks = jax.random.split(key, 12)
        B, N = (4, 4096)
        x = jax.random.normal(ks[0], (B, N, DIM), dtype=jnp.float32)
        s = lambda fan_in: 1.0 / np.sqrt(fan_in)
        W_fx = jax.random.normal(ks[1], (DIM, INNER), dtype=jnp.float32) * s(DIM)
        b_fx = jnp.zeros((INNER,), dtype=jnp.float32)
        W_x = jax.random.normal(ks[2], (DIM, INNER), dtype=jnp.float32) * s(DIM)
        b_x = jnp.zeros((INNER,), dtype=jnp.float32)
        A = jax.random.normal(ks[3], (G, D), dtype=jnp.float32)
        Q, _ = jnp.linalg.qr(A.T)
        W_slice = Q[:, :G].astype(jnp.float32)
        b_slice = jnp.zeros((G,), dtype=jnp.float32)
        W_q = jax.random.normal(ks[4], (D, D), dtype=jnp.float32) * s(D)
        W_k = jax.random.normal(ks[5], (D, D), dtype=jnp.float32) * s(D)
        W_v = jax.random.normal(ks[6], (D, D), dtype=jnp.float32) * s(D)
        W_out = jax.random.normal(ks[7], (INNER, DIM), dtype=jnp.float32) * s(INNER)
        b_out = jnp.zeros((DIM,), dtype=jnp.float32)
        temperature = jnp.ones((1, H, 1, 1), dtype=jnp.float32) * 0.5
        return {'x': x, 'W_fx': W_fx, 'b_fx': b_fx, 'W_x': W_x, 'b_x': b_x, 'W_slice': W_slice, 'b_slice': b_slice, 'W_q': W_q, 'W_k': W_k, 'W_v': W_v, 'W_out': W_out, 'b_out': b_out, 'temperature': temperature}
    _L0_ffn_all = _L0_ffn_setup()
    _L0_ffn_in = {k: v for k, v in _L0_ffn_all.items() if k in ('W_fx', 'b_fx', 'W_x', 'b_x', 'W_slice', 'b_slice', 'W_q', 'W_k', 'W_v', 'W_out', 'b_out', 'temperature')}
    del _L0_ffn_all
    return {'x': x, 'L0_tok_Wq': _L0_tok_in['Wq'], 'L0_tok_bq': _L0_tok_in['bq'], 'L0_tok_Wk': _L0_tok_in['Wk'], 'L0_tok_bk': _L0_tok_in['bk'], 'L0_tok_Wv': _L0_tok_in['Wv'], 'L0_tok_bv': _L0_tok_in['bv'], 'L0_tok_Wo': _L0_tok_in['Wo'], 'L0_tok_bo': _L0_tok_in['bo'], 'L0_attn_W_ih': _L0_attn_in['W_ih'], 'L0_attn_W_hh': _L0_attn_in['W_hh'], 'L0_attn_b_ih': _L0_attn_in['b_ih'], 'L0_attn_b_hh': _L0_attn_in['b_hh'], 'L0_ffn_W_fx': _L0_ffn_in['W_fx'], 'L0_ffn_b_fx': _L0_ffn_in['b_fx'], 'L0_ffn_W_x': _L0_ffn_in['W_x'], 'L0_ffn_b_x': _L0_ffn_in['b_x'], 'L0_ffn_W_slice': _L0_ffn_in['W_slice'], 'L0_ffn_b_slice': _L0_ffn_in['b_slice'], 'L0_ffn_W_q': _L0_ffn_in['W_q'], 'L0_ffn_W_k': _L0_ffn_in['W_k'], 'L0_ffn_W_v': _L0_ffn_in['W_v'], 'L0_ffn_W_out': _L0_ffn_in['W_out'], 'L0_ffn_b_out': _L0_ffn_in['b_out'], 'L0_ffn_temperature': _L0_ffn_in['temperature']}

def reference(x, L0_tok_Wq, L0_tok_bq, L0_tok_Wk, L0_tok_bk, L0_tok_Wv, L0_tok_bv, L0_tok_Wo, L0_tok_bo, L0_attn_W_ih, L0_attn_W_hh, L0_attn_b_ih, L0_attn_b_hh, L0_ffn_W_fx, L0_ffn_b_fx, L0_ffn_W_x, L0_ffn_b_x, L0_ffn_W_slice, L0_ffn_b_slice, L0_ffn_W_q, L0_ffn_W_k, L0_ffn_W_v, L0_ffn_W_out, L0_ffn_b_out, L0_ffn_temperature):
    import jax
    import jax.numpy as jnp

    def _L0_tok_ref(x, Wq, bq, Wk, bk, Wv, bv, Wo, bo):
        import jax, jax.numpy as jnp
        import numpy as np
        GS = 8
        NH = 8
        DM = 64
        B, W, H = (4, 64, 64)
        b, d, w, h = x.shape
        gw, gh = (w // GS, h // GS)
        n = gw * gh
        L = GS * GS
        dh = d // NH
        q = x.reshape(b, d, gw, GS, gh, GS).mean(axis=(3, 5))
        q = q.reshape(b, d, n).transpose(0, 2, 1).reshape(b * n, 1, d)
        kv = x.transpose(0, 2, 3, 1)
        kv = kv.reshape(b, gw, GS, gh, GS, d)
        kv = kv.transpose(0, 1, 3, 2, 4, 5).reshape(b * n, L, d)
        qp = (q @ Wq.T + bq).reshape(b * n, 1, NH, dh).transpose(0, 2, 1, 3)
        kp = (kv @ Wk.T + bk).reshape(b * n, L, NH, dh).transpose(0, 2, 1, 3)
        vp = (kv @ Wv.T + bv).reshape(b * n, L, NH, dh).transpose(0, 2, 1, 3)
        scores = jnp.einsum('bhqd,bhkd->bhqk', qp, kp) / jnp.sqrt(jnp.float32(dh))
        attn = jax.nn.softmax(scores, axis=-1)
        ctx = jnp.einsum('bhqk,bhkd->bhqd', attn, vp)
        ctx = ctx.transpose(0, 2, 1, 3).reshape(b * n, 1, d)
        attn_out = ctx @ Wo.T + bo
        out = q + attn_out
        return out.reshape(b, n, d)

    def _L0_attn_ref(x_in, W_ih, W_hh, b_ih, b_hh):
        import jax, jax.numpy as jnp
        import numpy as np
        SEQ, BATCH, IN, HID = (512, 64, 64, 64)
        xp = jnp.einsum('tbi,hi->tbh', x_in, W_ih) + b_ih + b_hh
        h0 = jnp.zeros((x_in.shape[1], W_hh.shape[0]), dtype=x_in.dtype)

        def step(h, xp_t):
            h_new = jnp.tanh(xp_t + h @ W_hh.T)
            return (h_new, h_new)
        _, hiddens = jax.lax.scan(step, h0, xp)
        return hiddens

    def _L0_ffn_ref(x, W_fx, b_fx, W_x, b_x, W_slice, b_slice, W_q, W_k, W_v, W_out, b_out, temperature):
        import jax, jax.numpy as jnp
        import numpy as np
        DIM = 64
        H = 8
        D = 64
        G = 64
        INNER = H * D
        SCALE = D ** (-0.5)
        B, N, _ = x.shape
        fx_mid = (x @ W_fx + b_fx).reshape(B, N, H, D).transpose(0, 2, 1, 3)
        x_mid = (x @ W_x + b_x).reshape(B, N, H, D).transpose(0, 2, 1, 3)
        temp = jnp.clip(temperature, 0.1, 5.0)
        slice_weights = jax.nn.softmax((x_mid @ W_slice + b_slice) / temp, axis=-1)
        slice_norm = slice_weights.sum(axis=2)
        slice_token = jnp.einsum('bhnc,bhng->bhgc', fx_mid, slice_weights)
        slice_token = slice_token / (slice_norm[..., None] + 1e-05)
        q = slice_token @ W_q
        k = slice_token @ W_k
        v = slice_token @ W_v
        attn = jax.nn.softmax(jnp.einsum('bhgc,bhkc->bhgk', q, k) * SCALE, axis=-1)
        out_slice = jnp.einsum('bhgk,bhkc->bhgc', attn, v)
        out_x = jnp.einsum('bhgc,bhng->bhnc', out_slice, slice_weights)
        out_x = out_x.transpose(0, 2, 1, 3).reshape(B, N, INNER)
        return out_x @ W_out + b_out
    h = _L0_tok_ref(x, L0_tok_Wq, L0_tok_bq, L0_tok_Wk, L0_tok_bk, L0_tok_Wv, L0_tok_bv, L0_tok_Wo, L0_tok_bo)
    h = h + _L0_attn_ref(_layernorm(h, axis=-1), L0_attn_W_ih, L0_attn_W_hh, L0_attn_b_ih, L0_attn_b_hh)
    h = h + _L0_ffn_ref(_layernorm(h, axis=-1), L0_ffn_W_fx, L0_ffn_b_fx, L0_ffn_W_x, L0_ffn_b_x, L0_ffn_W_slice, L0_ffn_b_slice, L0_ffn_W_q, L0_ffn_W_k, L0_ffn_W_v, L0_ffn_W_out, L0_ffn_b_out, L0_ffn_temperature)
    return h

_drawn_inputs = setup_inputs


def setup_inputs(seed=0):
    import zlib

    import numpy as np

    out = dict(_drawn_inputs(seed))
    spreads = {'L0_tok_bq': (0.0, 0.8),
     'L0_tok_bk': (0.0, 0.8),
     'L0_tok_bv': (0.0, 0.1),
     'L0_tok_bo': (0.0, 0.1),
     'L0_ffn_b_fx': (0.0, 0.1),
     'L0_ffn_b_x': (0.0, 0.8),
     'L0_ffn_b_slice': (0.0, 0.8),
     'L0_ffn_b_out': (0.0, 0.1),
     'L0_ffn_temperature': (0.5, 0.6)}
    factors = {'L0_tok_Wq': 8.0,
     'L0_tok_Wk': 8.0,
     'L0_tok_Wv': 5.244,
     'L0_ffn_W_q': 4.668,
     'L0_ffn_W_k': 3.969}
    for name, (base, spread) in spreads.items():
        noise = np.random.default_rng([zlib.crc32(name.encode()), seed]).standard_normal(out[name].shape)
        drawn = base * np.exp(spread * noise) if base else spread * noise
        out[name] = jnp.asarray(drawn.astype(out[name].dtype))
    for name, factor in factors.items():
        out[name] = (out[name] * factor).astype(out[name].dtype)
    return out
```

```python
import concourse.bass as bass
from concourse import mybir
from contextlib import ExitStack



def vit_tower_kernel(nc, x, tWq, tbq, tWk, tbk, tWv, tbv, tWo, tbo, W_ih, W_hh, b_ih, b_hh,
                     W_fx, b_fx, W_x, b_x, W_slice, b_slice, W_q, W_k, W_v, W_out, b_out,
                     temperature, out):
    fp32 = mybir.dt.float32
    ALU = mybir.AluOpType
    ACT = mybir.ActivationFunctionType
    AX = mybir.AxisListType

    P = 128
    B, D, HT, WD = x.shape
    GS = 8
    NH = 8
    DH = D // NH
    L = GS * GS
    N = (HT // GS) * (WD // GS)
    PIX = HT * WD
    PAIRS = B // 2
    GROUPS = 8
    CHUNKS = 32
    G = 64
    INNER = NH * D
    XW = P + 2
    AUG = D + 1
    EPS = 1e-5
    Y_ROUNDS = ((0, 3), (3, 6), (6, 8))

    x_v = x.rearrange("(t b) d w h -> t (b d) (w h)", b=2)
    out_v = out.rearrange("(t b) n c -> t (b n) c", b=2)

    ctx = ExitStack()
    with ctx:
        def sb(name, shape):
            return ctx.enter_context(nc.sbuf_tensor(name, shape, fp32))

        def bank(name, shape):
            return ctx.enter_context(nc.psum_tensor(name, shape, fp32))

        ident = sb("ident", [P, P])
        ones = sb("ones", [P, P])
        mask_gw = sb("mask_gw", [P, 2])
        mask_b = sb("mask_b", [P, 2])
        mask_img = sb("mask_img", [P, 2])
        mask_h = sb("mask_h", [P, NH])
        id_mean = sb("id_mean", [P, D])
        wq_bd = sb("wq_bd", [P, P])
        wk_bd = sb("wk_bd", [P, P])
        wv_bd = sb("wv_bd", [P, P])
        wo2 = sb("wo2", [D, P])
        wr2 = sb("wr2", [D, P])
        tokT = sb("tokT", [P, 384])
        wqT, wvT = tokT[:, 0:P], tokT[:, P:2 * P]
        woT, wrT = tokT[:, 256:320], tokT[:, 320:384]
        bq_col = sb("bq_col", [P, 1])
        bv_col = sb("bv_col", [P, 1])
        bo_row = sb("bo_row", [P, D])
        rnn_b2 = sb("rnn_b2", [P, 2])
        rnn_b = sb("rnn_b", [P, 1])
        wfx = sb("wfx", [AUG, INNER])
        wxa = sb("wxa", [AUG, INNER])
        wsl_bd = sb("wsl_bd", [P, P])
        fq_bd = sb("fq_bd", [P, P])
        fk_bd = sb("fk_bd", [P, P])
        fv_bd = sb("fv_bd", [P, P])
        wout = sb("wout", [P, 4, D])
        bout_row = sb("bout_row", [P, D])
        bsl = sb("bsl", [AUG, G])
        temp = sb("temp", [AUG, NH])
        rtemp = sb("rtemp", [AUG, NH])
        wfxT = sb("wfxT", [P, 4, 66])
        wxT = sb("wxT", [P, 4, 66])
        fqkvT = sb("fqkvT", [P, 3, P])
        mqk = sb("mqk", [P, P])
        e_bd = sb("e_bd", [P, 4, 2, 66])
        f_bd = sb("f_bd", [P, 4, 2, D])
        w_logit = sb("w_logit", [AUG, NH, G])
        w_qk = sb("w_qk", [AUG, 4, 2, 66])
        w_vo = sb("w_vo", [AUG, NH, D])

        X = sb("X", [P, 2, PIX])
        Xw = sb("Xw", [P, 4, 8, 2, 8, 8])
        XT = sb("XT", [P, 2, CHUNKS, XW])
        qsum = sb("qsum", [P, 4, 8, 2])
        qtok = sb("qtok", [P, 2, 2, 4, 2, 8])
        qp = sb("qp", [P, N])
        qpm = sb("qpm", [P, N, NH])
        U = sb("U", [P, N, 2, NH])
        St = sb("St", [P, GROUPS, L])
        Sc = sb("Sc", [P, GROUPS, L])
        Smax = sb("Smax", [P, GROUPS])
        Pm = sb("Pm", [P, GROUPS, 2, L])
        PT = sb("PT", [P, GROUPS, P])
        Yt = sb("Yt", [P, GROUPS, D])
        Ye = sb("Ye", [P, GROUPS, D])
        Yn = sb("Yn", [P, GROUPS, D])
        rsum = sb("rsum", [P, GROUPS])
        YT = sb("YT", [P, 4 * P])
        Zm = sb("Zm", [P, N, NH])
        ctxs = sb("ctxs", [P, N])
        ctxm = sb("ctxm", [P, 2, 4, 2, 2, 4])
        H = sb("H", [P, D])
        H2 = sb("H2", [P, D])
        stats = sb("stats", [P, 2, 6])
        mv = sb("mv", [P, 2, 2])
        vpe = sb("vpe", [P, 2])
        neghalf = sb("neghalf", [P, 1])
        rstd = sb("rstd", [P, 2])
        xn = sb("xn", [P, D])
        x2n = sb("x2n", [P, D])
        RX = sb("RX", [P, 4, N])
        X2T = sb("X2T", [AUG, P])
        X2B = sb("X2B", [P, 2, 66])
        R = sb("R", [P, D])
        lmax = sb("lmax", [P, NH])
        W = sb("W", [P, NH, G])
        wsum = sb("wsum", [P, NH])
        wrec = sb("wrec", [P, NH])
        Wn = sb("Wn", [P, NH, G])
        WX = sb("WX", [P, NH, 2, G])
        WT = sb("WT", [P, NH, P])
        bden = sb("bden", [P, 4, 2])
        brec = sb("brec", [P, 4, 2])
        Bn = sb("Bn", [P, 4, 2, 66])
        Bt = sb("Bt", [AUG, 4, 2, 2, G])
        T = sb("T", [AUG, NH, P])
        V = sb("V", [P, 2, 4, D])
        amax = sb("amax", [P, NH])
        A = sb("A", [P, NH, G])
        asum = sb("asum", [P, NH])
        arec = sb("arec", [P, NH])
        An = sb("An", [P, NH, G])
        M = sb("M", [P, 4, P])
        O = sb("O", [P, D])

        pX = [bank(f"pX{i}", [P, 4, P]) for i in range(2)]
        pK = [bank(f"pK{i}", [P, 512]) for i in range(2)]
        pF = bank("pF", [P, 2, 512])
        pF2 = bank("pF2", [P, 512])
        pG = bank("pG", [P, 512])

        SEMS = """
        passed x_in0 x_in1 windowed x2b_ones zeroed ident_zero consts mask_done id_mean_done xt_ones rnn_b_done
        tok_in tokT_done tokT_saved ffn_in temp_done prep_pe prep_dve
        xt_done xt_saved qsum_done qtok_done qp_done qp_saved qpm_done u_done u_saved
        s_done s_half s_whole smax_done s_shifted p_exp p_masked
        pt_done pt_saved0 pt_saved1 y_done y_half y_whole y_recip y_scaled yt_done yt_saved
        z_done z_masked ctx_done ctx_placed tok_done h_done stats_done mv_done vpe_done rstd_done
        xn_done xnt_done xnt_saved rnn_done state_done h2t_done h2_done x2n_done x2b_done
        x2t_done x2t_saved r_done
        lg_done lmax_done l_shifted w_exp wsum_done wrec_done wn_done wx_done
        b_done bden_done brec_done bn_done wt_done wt_saved bt_done bt_saved0 bt_saved1
        t_done t_saved0 t_saved1 v_done v_saved0 v_saved1
        a_done amax_done a_shifted a_exp asum_done arec_done an_done
        m_done m_saved o_done o_added stored
        """.split()
        S = {name: ctx.enter_context(nc.semaphore("s_" + name)) for name in SEMS}

        def nth(pair, k=1, per=1):
            return per * pair + k

        def ran(pair):
            return not (isinstance(pair, int) and pair < 0)

        def run_slots(engine, slot):
            slot(0, 0, True, False, False)
            slot(1, 1, True, True, False)
            with engine.Fori(2, PAIRS - 1, 2) as it:
                for j in range(2):
                    slot(it + j, j, True, True, True)
            slot(PAIRS, 0, False, True, True)
            slot(PAIRS + 1, 1, False, False, True)


        block = ctx.enter_context(nc.Block())

        TOK_LOADS = 17
        FFN_LOADS = 16
        CONSTS = 5

        @block.sync
        def _(sp):
            def load(p, j):
                if ran(p - 2):
                    sp.wait_ge(S["windowed"], nth(p - 2, 8, 8))
                    sp.sem_inc(S["passed"], 1)
                    sp.wait_ge(S["qsum_done"], nth(p - 2, 8, 8))
                    sp.sem_inc(S["passed"], 1)
                for half, name in enumerate(("x_in0", "x_in1")):
                    if ran(p - 1):
                        sp.wait_ge(S[name], 16 * p)
                        sp.sem_inc(S["passed"], 1)
                    sp.dma_start(X[:, j, half * 2048:(half + 1) * 2048],
                                 x_v[p, :, half * 2048:(half + 1) * 2048]).then_inc(S[name], 16)

            def store(p):
                sp.wait_ge(S["o_added"], nth(p))
                sp.sem_inc(S["passed"], 1)
                sp.dma_start(out_v[p, :, :], O[:, :]).then_inc(S["stored"], 16)

            sp.sem_inc(S["stored"], 16)
            load(0, 0)
            sp.wait_ge(S["zeroed"], 1)
            sp.dma_start(wfx[0:D, :], W_fx[:, :]).then_inc(S["ffn_in"], 16)
            sp.dma_start(wfx[D:AUG, :], b_fx.unsqueeze(0)).then_inc(S["ffn_in"], 16)
            sp.dma_start(wxa[0:D, :], W_x[:, :]).then_inc(S["ffn_in"], 16)
            sp.dma_start(wxa[D:AUG, :], b_x.unsqueeze(0)).then_inc(S["ffn_in"], 16)
            for h2 in range(2):
                rows = slice(64 * h2, 64 * h2 + 64)
                sp.dma_start(wsl_bd[rows, rows], W_slice[:, :]).then_inc(S["ffn_in"], 16)
                sp.dma_start(fq_bd[rows, rows], W_q[:, :]).then_inc(S["ffn_in"], 16)
                sp.dma_start(fk_bd[rows, rows], W_k[:, :]).then_inc(S["ffn_in"], 16)
                sp.dma_start(fv_bd[rows, rows], W_v[:, :]).then_inc(S["ffn_in"], 16)
            sp.dma_start(wout[:, :, :], W_out.rearrange("(a p) c -> p a c", p=P)).then_inc(S["ffn_in"], 16)
            sp.dma_start(bout_row[:, :], b_out.partition_broadcast(P)).then_inc(S["ffn_in"], 16)
            sp.dma_start(bsl[D:AUG, :], b_slice.unsqueeze(0)).then_inc(S["ffn_in"], 16)
            sp.dma_start(temp[:, :], temperature[0, :, 0, 0].partition_broadcast(AUG)).then_inc(S["ffn_in"], 16)
            for p in range(1, 4):
                load(p, p % 2)
            with sp.Fori(4, PAIRS - 1, 2) as it:
                for j in range(2):
                    load(it + j, j)
                    store(it + j - 4)
            for p in range(PAIRS - 4, PAIRS):
                store(p)
            sp.wait_ge(S["stored"], 16 * PAIRS + 16)

        @block.gpsimd
        def _(pool):
            zero = (wq_bd, wk_bd, wv_bd, wsl_bd, fq_bd, fk_bd, fv_bd)
            for t in zero:
                pool.memset(t[:, :], 0.0)
            pool.memset(neghalf[:, :], -0.5).then_inc(S["zeroed"], 1)
            pool.memset(ident[:, :], 0.0).then_inc(S["ident_zero"], 1)
            pool.wait_ge(S["ident_zero"], 1)
            pool.affine_select(out=ident[:, :], in_=ident[:, :], compare_op=ALU.not_equal, fill=1.0,
                               base=0, pattern=[[-1, P]], channel_multiplier=1).then_inc(S["consts"], 1)
            pool.memset(U[:, :, :, :], 0.0).then_inc(S["consts"], 1)
            pool.memset(ctxm[:, :, :, :, :, :], 0.0).then_inc(S["consts"], 1)
            pool.memset(e_bd[:, :, :, :], 0.0).then_inc(S["consts"], 1)
            pool.memset(f_bd[:, :, :, :], 0.0).then_inc(S["consts"], 1)
            pool.wait_ge(S["mask_done"], 4)

            def by_window(p, j, rows):
                if 0 in rows and ran(p - 1):
                    pool.wait_ge(S["s_done"], nth(p - 1, 2, 2))
                for i in rows:
                    if i == 0:
                        pool.wait_ge(S["x_in0"], nth(p, 16, 16))
                        pool.sem_inc(S["passed"], 1)
                    if i == 4:
                        pool.wait_ge(S["x_in1"], nth(p, 16, 16))
                        pool.sem_inc(S["passed"], 1)
                    pool.tensor_copy(Xw[:, i // 2, :, i % 2, :, :],
                                     X[:, j, i * 512:(i + 1) * 512].rearrange("p (r h c) -> p h r c", r=8, h=8))\
                        .then_inc(S["windowed"], 1)

            def wx(p):
                pool.wait_ge(S["wn_done"], nth(p))
                pool.sem_inc(S["passed"], 1)
                for b in range(2):
                    pool.tensor_scalar(WX[:, :, b, :], Wn[:, :, :], mask_img[:, b:b + 1], 1.0,
                                       ALU.mult, ALU.mult).then_inc(S["wx_done"], 1)

            def y_scale(p, r):
                g0, g1 = Y_ROUNDS[r]
                pool.wait_ge(S["y_whole"], nth(p, r + 1, 3))
                pool.wait_ge(S["y_recip"], nth(p, r + 1, 3))
                if r == 0 and ran(p - 1):
                    pool.wait_ge(S["yt_done"], nth(p - 1))
                pool.tensor_tensor(Yn[:, g0:g1, :], Ye[:, g0:g1, :],
                                   rsum[:, g0:g1].unsqueeze(2).to_broadcast([P, g1 - g0, D]),
                                   ALU.mult).then_inc(S["y_scaled"], 1)

            def spread_q(p, j):
                pool.wait_ge(S["qp_saved"], nth(p))
                if ran(p - 1):
                    pool.wait_ge(S["u_done"], nth(p - 1))
                pool.tensor_tensor(qpm[:, :, :], qp[:, :].unsqueeze(2).to_broadcast([P, N, NH]),
                                   mask_h[:, :].unsqueeze(1).to_broadcast([P, N, NH]),
                                   ALU.mult).then_inc(S["qpm_done"], 1)
                pool.wait_ge(S["qsum_done"], nth(p, 8, 8))
                if ran(p - 2):
                    pool.wait_ge(S["tok_done"], nth(p - 2))
                pool.sem_inc(S["passed"], 1)
                for b in range(2):
                    pool.tensor_scalar(qtok[:, j, b, :, :, :], qsum[:, :, :, :].rearrange("p a h w -> p a w h"),
                                       mask_img[:, b:b + 1], 1.0, ALU.mult, ALU.mult)\
                        .then_inc(S["qtok_done"], 1)

            def power(p, k):
                pool.wait_ge(S["vpe_done"], nth(p, k + 1, 2))
                pool.tensor_tensor(rstd[:, k:k + 1], vpe[:, k:k + 1], neghalf[:, :], ALU.pow)\
                    .then_inc(S["rstd_done"], 1)

            def mask_p(p):
                pool.wait_ge(S["p_exp"], nth(p))
                if ran(p - 1):
                    pool.wait_ge(S["pt_done"], nth(p - 1, 2, 2))
                pool.sem_inc(S["passed"], 1)
                for gw in range(2):
                    pool.tensor_scalar(Pm[:, :, gw, :], Sc[:, :, :], mask_gw[:, gw:gw + 1], 1.0,
                                       ALU.mult, ALU.mult).then_inc(S["p_masked"], 1)

            def x2_blocks(p):
                pool.wait_ge(S["x2n_done"], nth(p))
                if ran(p - 1):
                    pool.wait_ge(S["b_done"], nth(p - 1))
                pool.sem_inc(S["passed"], 1)
                for b in range(2):
                    pool.tensor_scalar(X2B[:, b, 0:D], x2n[:, :], mask_img[:, b:b + 1], 1.0,
                                       ALU.mult, ALU.mult).then_inc(S["x2b_done"], 1)
                pool.wait_ge(S["h2_done"], nth(p))
                if ran(p - 1):
                    pool.wait_ge(S["o_added"], nth(p - 1))
                pool.tensor_tensor(R[:, :], H2[:, :], bout_row[:, :], ALU.add).then_inc(S["r_done"], 1)

            def slot(s, j, a, b, d):
                if a:
                    by_window(s, j, range(0, 4))
                if d:
                    wx(s - 2)
                if a:
                    by_window(s, j, range(4, 8))
                if b:
                    for r in range(3):
                        y_scale(s - 1, r)
                if a:
                    spread_q(s, j)
                if b:
                    power(s - 1, 0)
                if a:
                    mask_p(s)
                if b:
                    power(s - 1, 1)
                    if isinstance(s, int) and s == 1:
                        pool.wait_ge(S["ffn_in"], 16 * FFN_LOADS)
                    x2_blocks(s - 1)

            run_slots(pool, slot)

        @block.tensor
        def _(pe):
            pe.wait_ge(S["consts"], 1)
            pe.wait_ge(S["tok_in"], 16 * TOK_LOADS)
            pe.transpose(pK[0][:, 0:P], wq_bd[:, :], ident[:, :])
            pe.transpose(pK[0][:, P:2 * P], wv_bd[:, :], ident[:, :])
            pe.transpose(pK[0][:, 256:320], wo2[:, :], ident[0:D, 0:D])
            pe.transpose(pK[0][:, 320:384], wr2[:, :], ident[0:D, 0:D]).then_inc(S["tokT_done"], 1)
            pe.wait_ge(S["tokT_saved"], 1)
            pe.wait_ge(S["id_mean_done"], 1)
            pe.wait_ge(S["consts"], CONSTS)

            def prepare_slices():
                pe.wait_ge(S["ffn_in"], 16 * FFN_LOADS)
                for hp in range(4):
                    pe.transpose(pF[:, 0, 66 * hp:66 * hp + AUG], wfx[:, hp * P:(hp + 1) * P],
                                 ident[0:AUG, 0:AUG])
                    pe.transpose(pF[:, 1, 66 * hp:66 * hp + AUG], wxa[:, hp * P:(hp + 1) * P],
                                 ident[0:AUG, 0:AUG])
                for k, w in enumerate((fq_bd, fk_bd, fv_bd)):
                    last = pe.transpose(pF2[:, k * P:(k + 1) * P], w[:, :], ident[:, :])
                last.then_inc(S["prep_pe"], 1)
                pe.wait_ge(S["prep_dve"], 1)
                fqT, fkT, fvT = (fqkvT[:, k, :] for k in range(3))
                pe.matmul(pF2[:, 0:P], fkT, fqT, start=True, stop=True)
                pe.matmul(pF[:, 0, 0:4 * D], fvT, wout[:, :, :].rearrange("p a c -> p (a c)"),
                          start=True, stop=True)
                for hp in range(4):
                    last = pe.matmul(pF[0:AUG, 1, hp * P:(hp + 1) * P], wxT[:, hp, 0:AUG], wsl_bd[:, :],
                                     start=True, stop=True)
                last.then_inc(S["prep_pe"], 1)
                pe.wait_ge(S["prep_dve"], 2)
                pe.matmul(pF2[:, 0:264], mqk[:, :], wfxT[:, :, :].rearrange("p a c -> p (a c)"),
                          start=True, stop=True)
                for hp in range(4):
                    last = pe.matmul(pF[0:AUG, 0, hp * P:(hp + 1) * P], wfxT[:, hp, 0:AUG],
                                     f_bd[:, hp, :, :].rearrange("p a c -> p (a c)"),
                                     start=True, stop=True)
                last.then_inc(S["prep_pe"], 1)
                pe.wait_ge(S["prep_dve"], 3)
                for hp in range(4):
                    last = pe.matmul(pF[0:AUG, hp // 2, (hp % 2) * 132:(hp % 2) * 132 + 132],
                                     wfxT[:, hp, 0:AUG], e_bd[:, hp, :, :].rearrange("p a c -> p (a c)"),
                                     start=True, stop=True)
                last.then_inc(S["prep_pe"], 1)
                pe.wait_ge(S["prep_dve"], 4)

            def transpose_x(p, j, i):
                if i % 2 == 0:
                    pe.wait_ge(S["windowed"], nth(p, i + 2, 8))
                if i >= 2 or ran(p - 1):
                    pe.wait_ge(S["xt_saved"], nth(p, i - 1, 8))
                for c in range(4):
                    last = pe.transpose(pX[i % 2][:, c, :],
                                        Xw[:, i // 2, 4 * (i % 2) + c, :, :, :].rearrange("p w r c -> p (w r c)"),
                                        ident[:, :])
                last.then_inc(S["xt_done"], 1)

            def query(p):
                pe.wait_ge(S["qsum_done"], nth(p, 8, 8))
                if ran(p - 2):
                    pe.wait_ge(S["x2t_saved"], nth(p - 2))
                pe.matmul(pG[:, 0:N], wqT, qsum[:, :, :, :].rearrange("p a h w -> p (a h w)"),
                          start=True, stop=True).then_inc(S["qp_done"], 1)

            def keys_for_query(p):
                pe.wait_ge(S["qpm_done"], nth(p))
                if ran(p - 1):
                    pe.wait_ge(S["y_whole"], nth(p - 1, 3, 3))
                    pe.wait_ge(S["y_recip"], nth(p - 1, 3, 3))
                pe.matmul(pK[0][:, :], wk_bd[:, :], qpm[:, :, :].rearrange("p w h -> p (w h)"),
                          start=True, stop=True).then_inc(S["u_done"], 1)

            def scores(p, j, half):
                if half == 0:
                    pe.wait_ge(S["u_saved"], nth(p, 2, 2))
                elif ran(p - 1):
                    pe.wait_ge(S["z_masked"], nth(p - 1))
                for g4 in range(4):
                    g = 4 * half + g4
                    for c in range(4):
                        gh = 4 * (g % 2) + c
                        k = (g // 2) * 8 + gh
                        last = pe.matmul(pK[half][32 * c:32 * c + 32, g4 * P:(g4 + 1) * P],
                                         U[:, 2 * k:2 * k + 2, :, :].rearrange("p w b h -> p (w b h)"),
                                         Xw[:, g // 2, gh, :, :, :].rearrange("p w r c -> p (w r c)"),
                                         start=True, stop=True)
                last.then_inc(S["s_done"], 1)

            def transpose_p(p, half):
                if half == 0:
                    pe.wait_ge(S["p_masked"], nth(p, 2, 2))
                for g4 in range(4):
                    last = pe.transpose(pK[half][:, g4 * P:(g4 + 1) * P],
                                        Pm[:, 4 * half + g4, :, :].rearrange("p w l -> p (w l)"), ident[:, :])
                last.then_inc(S["pt_done"], 1)

            def weighted_sum(p, j, r):
                g0, g1 = Y_ROUNDS[r]
                if r == 0:
                    pe.wait_ge(S["pt_saved0"], nth(p))
                if r == 1:
                    pe.wait_ge(S["pt_saved1"], nth(p))
                if r == 2:
                    pe.wait_ge(S["y_whole"], nth(p, 1, 3))
                    pe.wait_ge(S["y_recip"], nth(p, 1, 3))
                pe.wait_ge(S["xt_saved"], nth(p, 8, 8))
                for g in range(g0, g1):
                    for c in range(4):
                        last = pe.matmul(pK[r % 2][32 * c:32 * c + 32, (g - g0) * XW:(g - g0 + 1) * XW],
                                         PT[:, g, 32 * c:32 * c + 32],
                                         XT[:, j, 4 * g + c, :], start=True, stop=True)
                last.then_inc(S["y_done"], 1)

            def transpose_y(p):
                pe.wait_ge(S["y_scaled"], nth(p, 3, 3))
                for a in range(4):
                    last = pe.transpose(pK[1][:, a * P:(a + 1) * P],
                                        Yn[:, 2 * a:2 * a + 2, :].rearrange("p q d -> p (q d)"), ident[:, :])
                last.then_inc(S["yt_done"], 1)

            def values(p):
                pe.wait_ge(S["yt_saved"], nth(p))
                pe.matmul(pK[1][:, :], wvT, YT[:, :], start=True, stop=True).then_inc(S["z_done"], 1)

            def tokens(p, j):
                pe.wait_ge(S["ctx_placed"], nth(p, 4, 4))
                pe.wait_ge(S["qtok_done"], nth(p, 2, 2))
                if not (isinstance(p, int) and p + 1 >= PAIRS):
                    pe.wait_ge(S["qp_saved"], nth(p + 1))
                pe.matmul(pG[:, 0:D], ctxm[:, :, :, :, :, :].rearrange("p b a w q h -> p (b a w q h)"), woT,
                          start=True, stop=False)
                pe.matmul(pG[:, 0:D], qtok[:, j, :, :, :, :].rearrange("p b a w h -> p (b a w h)"), id_mean[:, :],
                          start=False, stop=True).then_inc(S["tok_done"], 1)

            def transpose_xn(p):
                pe.wait_ge(S["xn_done"], nth(p))
                pe.sem_inc(S["passed"], 1)
                pe.transpose(pG[0:D, 0:P], xn[:, :], ident[:, :]).then_inc(S["xnt_done"], 1)

            def recur(p, j, i):
                if i == 0:
                    pe.wait_ge(S["xnt_saved"], nth(p, 2, 2))
                else:
                    pe.wait_ge(S["state_done"], nth(p, 1, 2))
                pe.matmul(pG[64:128, 0:N], wrT, RX[:, (2 * j + i - 1) % 4, :],
                          start=True, stop=True).then_inc(S["rnn_done"], 1)

            def transpose_h(p, j):
                pe.wait_ge(S["state_done"], nth(p, 2, 2))
                pe.sem_inc(S["passed"], 1)
                pe.transpose(pG[:, 0:D], RX[64:128, 2 * j:2 * j + 2, :].rearrange("p t n -> p (t n)"),
                             ident[64:128, 64:128]).then_inc(S["h2t_done"], 1)

            def transpose_x2(p):
                pe.wait_ge(S["x2n_done"], nth(p))
                pe.sem_inc(S["passed"], 1)
                pe.transpose(pG[0:D, 0:P], x2n[:, :], ident[:, :]).then_inc(S["x2t_done"], 1)

            def logits(p):
                pe.wait_ge(S["x2t_saved"], nth(p))
                pe.matmul(pF[:, 0, :], X2T[:, :], w_logit[:, :, :].rearrange("p h g -> p (h g)"),
                          start=True, stop=True).then_inc(S["lg_done"], 1)

            def slice_sums(p):
                pe.wait_ge(S["wn_done"], nth(p))
                pe.wait_ge(S["x2b_done"], nth(p, 2, 2))
                for hp in range(4):
                    last = pe.matmul((pF[:, 1, 0:264] if hp < 2 else pF2[:, 0:264])[:, (hp % 2) * 132:(hp % 2) * 132 + 132],
                                     Wn[:, 2 * hp:2 * hp + 2, :].rearrange("p h g -> p (h g)"),
                                     X2B[:, :, :].rearrange("p b c -> p (b c)"), start=True, stop=True)
                last.then_inc(S["b_done"], 1)

            def transpose_w(p, half):
                if half == 0:
                    pe.wait_ge(S["wx_done"], nth(p, 2, 2))
                else:
                    pe.wait_ge(S["bn_done"], nth(p, 2, 2))
                for h in range(4 * half, 4 * half + 4):
                    last = pe.transpose(pF[:, half, (h % 4) * P:(h % 4 + 1) * P],
                                        WX[:, h, :, :].rearrange("p b g -> p (b g)"), ident[:, :])
                last.then_inc(S["wt_done"], 1)

            def transpose_b(p, half):
                if half == 0:
                    pe.wait_ge(S["bn_done"], nth(p, 2, 2))
                else:
                    pe.wait_ge(S["wt_saved"], nth(p, 1, 2))
                dst = pF2 if half == 0 else pF[:, 0, :]
                for i in range(4):
                    hp, b = 2 * half + i // 2, i % 2
                    last = pe.transpose(dst[0:AUG, i * P:(i + 1) * P], Bn[:, hp, b, 0:AUG], ident[:, :])
                last.then_inc(S["bt_done"], 1)

            def slice_keys(p, half):
                if half == 0:
                    pe.wait_ge(S["wt_saved"], nth(p, 2, 2))
                    pe.wait_ge(S["bt_saved0"], nth(p))
                else:
                    pe.wait_ge(S["bt_saved1"], nth(p))
                dst = pF[:, 1, :] if half == 0 else pF2
                for i in range(4):
                    hp, h2 = 2 * half + i // 2, i % 2
                    last = pe.matmul(dst[0:AUG, i * P:(i + 1) * P], w_qk[:, hp, h2, 0:AUG],
                                     Bt[:, hp, :, h2, :], start=True, stop=True)
                last.then_inc(S["t_done"], 1)

            def slice_values(p):
                pe.wait_ge(S["bt_saved1"], nth(p))
                pe.wait_ge(S["t_saved0"], nth(p))
                for b in range(2):
                    for hp in range(4):
                        last = pe.matmul(pF[:, b, hp * P:(hp + 1) * P], Bt[:, hp, b, :, :].rearrange("p h g -> p (h g)"),
                                         w_vo[:, 2 * hp:2 * hp + 2, :].rearrange("p h c -> p (h c)"),
                                         start=True, stop=True)
                last.then_inc(S["v_done"], 1)

            def slice_scores(p):
                pe.wait_ge(S["t_saved1"], nth(p))
                for h in range(NH):
                    for b in range(2):
                        last = pe.matmul(pF2[64 * b:64 * b + 64, h * G:(h + 1) * G],
                                         T[:, h, 64 * b:64 * b + 64], Bt[:, h // 2, b, h % 2, :],
                                         start=True, stop=True)
                last.then_inc(S["a_done"], 1)

            def weights_times_scores(p):
                pe.wait_ge(S["an_done"], nth(p))
                pe.wait_ge(S["v_saved0"], nth(p))
                pe.wait_ge(S["v_saved1"], nth(p))
                for h in range(NH):
                    rows = slice(64 * (h % 2), 64 * (h % 2) + 64)
                    last = pe.matmul(pF[rows, 0, (h // 2) * P:(h // 2 + 1) * P], An[:, h, :], WT[:, h, :],
                                     start=True, stop=True)
                last.then_inc(S["m_done"], 1)

            def project(p):
                pe.wait_ge(S["m_saved"], nth(p))
                for b in range(2):
                    for hp in range(4):
                        last = pe.matmul(pF2[64 * b:64 * b + 64, 0:D], M[:, hp, 64 * b:64 * b + 64],
                                         V[:, b, hp, :], start=(hp == 0), stop=(hp == 3))
                last.then_inc(S["o_done"], 1)

            def slot(s, j, a, b, d):
                k = 1 - j
                if d: logits(s - 2)
                if b: transpose_p(s - 1, 0); transpose_p(s - 1, 1)
                if a: transpose_x(s, j, 0); transpose_x(s, j, 1)
                if b: weighted_sum(s - 1, k, 0)
                if d: slice_sums(s - 2)
                if b: weighted_sum(s - 1, k, 1)
                if a: transpose_x(s, j, 2); transpose_x(s, j, 3)
                if b: weighted_sum(s - 1, k, 2)
                if d: transpose_w(s - 2, 0); transpose_w(s - 2, 1)
                if a: query(s)
                if d: transpose_b(s - 2, 0); transpose_b(s - 2, 1)
                if b: transpose_y(s - 1)
                if a: transpose_x(s, j, 4); keys_for_query(s)
                if d: slice_keys(s - 2, 0)
                if b: values(s - 1)
                if d: slice_keys(s - 2, 1); slice_values(s - 2)
                if b: tokens(s - 1, k)
                if a: transpose_x(s, j, 5)
                if d: slice_scores(s - 2)
                if a: scores(s, j, 0)
                if b: transpose_xn(s - 1)
                if a: transpose_x(s, j, 6); scores(s, j, 1)
                if b: recur(s - 1, k, 0)
                if d: weights_times_scores(s - 2)
                if a: transpose_x(s, j, 7)
                if b: recur(s - 1, k, 1)
                if d: project(s - 2)
                if b: transpose_h(s - 1, k); transpose_x2(s - 1)
                if isinstance(s, int) and s == 0:
                    prepare_slices()

            run_slots(pe, slot)

        @block.scalar
        def _(act):
            act.wait_ge(S["zeroed"], 1)
            for b in range(2):
                rows = slice(64 * b, 64 * b + 64)
                act.dma_start(wq_bd[rows, rows], tWq[:, :]).then_inc(S["tok_in"], 16)
                act.dma_start(wk_bd[rows, rows], tWk[:, :]).then_inc(S["tok_in"], 16)
                act.dma_start(wv_bd[rows, rows], tWv[:, :]).then_inc(S["tok_in"], 16)
                act.dma_start(wo2[:, rows], tWo[:, :]).then_inc(S["tok_in"], 16)
                act.dma_start(bq_col[rows, :], tbq.unsqueeze(1)).then_inc(S["tok_in"], 16)
                act.dma_start(bv_col[rows, :], tbv.unsqueeze(1)).then_inc(S["tok_in"], 16)
            act.dma_start(wr2[:, 0:64], W_ih[:, :]).then_inc(S["tok_in"], 16)
            act.dma_start(wr2[:, 64:128], W_hh[:, :]).then_inc(S["tok_in"], 16)
            act.dma_start(rnn_b2[64:128, 0:1], b_ih.unsqueeze(1)).then_inc(S["tok_in"], 16)
            act.dma_start(rnn_b2[64:128, 1:2], b_hh.unsqueeze(1)).then_inc(S["tok_in"], 16)
            act.dma_start(bo_row[:, :], tbo.partition_broadcast(P)).then_inc(S["tok_in"], 16)
            act.wait_ge(S["tok_in"], 16 * TOK_LOADS)
            act.wait_ge(S["consts"], CONSTS)
            act.wait_ge(S["rnn_b_done"], 1)
            act.wait_ge(S["mask_done"], 4)
            act.wait_ge(S["xt_ones"], 1)

            def save_xt(p, j, i):
                act.wait_ge(S["xt_done"], nth(p, i + 1, 8))
                if i == 0 and ran(p - 2):
                    act.wait_ge(S["y_done"], nth(p - 2, 3, 3))
                act.activation(XT[:, j, 4 * i:4 * i + 4, 0:P], pX[i % 2][:, :, :], ACT.Copy)\
                    .then_inc(S["xt_saved"], 1)

            def save_qp(p):
                act.wait_ge(S["qp_done"], nth(p))
                if ran(p - 1):
                    act.wait_ge(S["qpm_done"], nth(p - 1))
                act.activation(qp[:, :], pG[:, 0:N], ACT.Identity, bias=bq_col[:, :], scale=1.0 / L)\
                    .then_inc(S["qp_saved"], 1)

            def save_u(p):
                act.wait_ge(S["u_done"], nth(p))
                if ran(p - 1):
                    act.wait_ge(S["s_done"], nth(p - 1, 2, 2))
                for b in range(2):
                    rows = slice(64 * b, 64 * b + 64)
                    act.activation(U[rows, :, b, :], pK[0][rows, :].rearrange("p (w h) -> p w h", h=NH),
                                   ACT.Copy, scale=DH ** -0.5).then_inc(S["u_saved"], 1)

            def half_scores(p, half):
                act.wait_ge(S["s_done"], nth(p, half + 1, 2))
                if half == 0 and ran(p - 1):
                    act.wait_ge(S["s_whole"], nth(p - 1, 2, 2))
                act.activation(St[:, 4 * half:4 * half + 4, :],
                               pK[half][:, :].rearrange("p (g w l) -> p g w l", g=4, w=2)[:, :, 0, :],
                               ACT.Copy, scale=mask_gw[:, 0:1]).then_inc(S["s_half"], 1)

            def exp_p(p):
                act.wait_ge(S["s_shifted"], nth(p))
                act.activation(Sc[:, :, :], Sc[:, :, :], ACT.Exp).then_inc(S["p_exp"], 1)

            def save_pt(p):
                act.wait_ge(S["pt_done"], nth(p, 1, 2))
                if ran(p - 1):
                    act.wait_ge(S["y_done"], nth(p - 1, 3, 3))
                act.activation(PT[:, 0:4, :].rearrange("p g r -> p (g r)"), pK[0][:, :], ACT.Copy)\
                    .then_inc(S["pt_saved0"], 1)

            def half_y(p, r):
                g0, g1 = Y_ROUNDS[r]
                act.wait_ge(S["y_done"], nth(p, r + 1, 3))
                if r == 0 and ran(p - 1):
                    act.wait_ge(S["y_whole"], nth(p - 1, 3, 3))
                src = pK[r % 2][:, 0:(g1 - g0) * XW].rearrange("p (g c) -> p g c", c=XW)
                act.activation(Yt[:, g0:g1, :], src[:, :, 0:D], ACT.Copy, scale=mask_b[:, 0:1])\
                    .then_inc(S["y_half"], 1)

            def save_yt(p):
                act.wait_ge(S["yt_done"], nth(p))
                if ran(p - 1):
                    act.wait_ge(S["z_done"], nth(p - 1))
                act.activation(YT[:, :], pK[1][:, :], ACT.Copy).then_inc(S["yt_saved"], 1)

            def save_xnt(p, j):
                act.wait_ge(S["xnt_done"], nth(p))
                if ran(p - 1):
                    act.wait_ge(S["rnn_done"], nth(p - 1, 2, 2))
                for i in range(2):
                    act.activation(RX[0:D, (2 * j + i - 1) % 4, :], pG[0:D, i * N:(i + 1) * N], ACT.Copy)\
                        .then_inc(S["xnt_saved"], 1)

            def state(p, j, i):
                act.wait_ge(S["rnn_done"], nth(p, i + 1, 2))
                act.activation(RX[64:128, 2 * j + i, :], pG[64:128, 0:N], ACT.Tanh,
                               bias=rnn_b[64:128, :]).then_inc(S["state_done"], 1)

            def save_x2t(p):
                act.wait_ge(S["x2t_done"], nth(p))
                if ran(p - 1):
                    act.wait_ge(S["lg_done"], nth(p - 1))
                act.activation(X2T[0:D, :], pG[0:D, 0:P], ACT.Copy).then_inc(S["x2t_saved"], 1)

            def exp_w(p):
                act.wait_ge(S["l_shifted"], nth(p))
                act.activation(W[:, :, :], W[:, :, :], ACT.Exp).then_inc(S["w_exp"], 1)

            def save_wt(p, half):
                act.wait_ge(S["wt_done"], nth(p, half + 1, 2))
                act.activation(WT[:, 4 * half:4 * half + 4, :].rearrange("p h n -> p (h n)"),
                               pF[:, half, :], ACT.Copy).then_inc(S["wt_saved"], 1)

            def save_bt1(p):
                act.wait_ge(S["bt_done"], nth(p, 2, 2))
                act.activation(Bt[:, 2:4, :, :, :].rearrange("p a b h g -> p (a b h g)"), pF[0:AUG, 0, :],
                               ACT.Copy).then_inc(S["bt_saved1"], 1)

            def save_t0(p):
                act.wait_ge(S["t_done"], nth(p, 1, 2))
                act.activation(T[:, 0:4, :].rearrange("p h g -> p (h g)"), pF[0:AUG, 1, :], ACT.Copy)\
                    .then_inc(S["t_saved0"], 1)

            def save_v0(p):
                act.wait_ge(S["v_done"], nth(p))
                act.activation(V[0:64, :, :, :].rearrange("p b a c -> p (b a) c"),
                               pF[0:64, :, :].rearrange("p b (a h c) -> p (b a) h c", a=4, h=2)[:, :, 0, :],
                               ACT.Copy).then_inc(S["v_saved0"], 1)

            def exp_a(p):
                act.wait_ge(S["a_shifted"], nth(p))
                act.activation(A[:, :, :], A[:, :, :], ACT.Exp).then_inc(S["a_exp"], 1)

            def save_m(p):
                act.wait_ge(S["m_done"], nth(p))
                act.activation(M[:, :, :].rearrange("p a n -> p (a n)"), pF[:, 0, :], ACT.Copy)\
                    .then_inc(S["m_saved"], 1)

            def slot(s, j, a, b, d):
                k = 1 - j
                if d: exp_w(s - 2)
                if b: save_pt(s - 1)
                if a: save_xt(s, j, 0); save_xt(s, j, 1)
                if b: half_y(s - 1, 0); half_y(s - 1, 1)
                if a: save_xt(s, j, 2); save_xt(s, j, 3)
                if b: half_y(s - 1, 2)
                if d: save_wt(s - 2, 0); save_wt(s - 2, 1)
                if a: save_qp(s)
                if d: save_bt1(s - 2)
                if b: save_yt(s - 1)
                if a: save_xt(s, j, 4); save_u(s)
                if d: save_t0(s - 2); save_v0(s - 2)
                if a: save_xt(s, j, 5)
                if d: exp_a(s - 2)
                if a: half_scores(s, 0)
                if b: save_xnt(s - 1, k)
                if a: save_xt(s, j, 6); half_scores(s, 1)
                if b: state(s - 1, k, 0)
                if d: save_m(s - 2)
                if a: save_xt(s, j, 7); exp_p(s)
                if b: state(s - 1, k, 1); save_x2t(s - 1)

            run_slots(act, slot)

        @block.vector
        def _(dve):
            dve.memset(XT[:, :, :, P:XW], 1.0)
            dve.memset(X2T[D:AUG, :], 1.0)
            dve.memset(RX[64:128, 3, :], 0.0).then_inc(S["xt_ones"], 1)
            dve.wait_ge(S["consts"], 1)
            iv = ident[:, :].rearrange("p (a w c) -> p w a c", a=4, w=2)
            dve.tensor_reduce(mask_gw[:, :], iv, AX.XY, ALU.add).then_inc(S["mask_done"], 1)
            iv = ident[:, :].rearrange("p (a b c) -> p b a c", a=8, b=2)
            dve.tensor_reduce(mask_b[:, :], iv, AX.XY, ALU.add).then_inc(S["mask_done"], 1)
            iv = ident[:, :].rearrange("p (b c) -> p b c", b=2)
            dve.tensor_reduce(mask_img[:, :], iv, AX.X, ALU.add).then_inc(S["mask_done"], 1)
            iv = ident[:, :].rearrange("p (b h c) -> p h b c", b=2, h=NH)
            dve.tensor_reduce(mask_h[:, :], iv, AX.XY, ALU.add).then_inc(S["mask_done"], 1)
            for b in range(2):
                rows = slice(64 * b, 64 * b + 64)
                last = dve.tensor_scalar(id_mean[rows, :], ident[rows, rows], 1.0 / L, None, ALU.mult)
            last.then_inc(S["id_mean_done"], 1)
            dve.wait_ge(S["tok_in"], 16 * TOK_LOADS)
            dve.tensor_tensor(rnn_b[64:128, :], rnn_b2[64:128, 0:1], rnn_b2[64:128, 1:2], ALU.add)\
                .then_inc(S["rnn_b_done"], 1)
            dve.wait_ge(S["tokT_done"], 1)
            dve.tensor_copy(tokT[:, :], pK[0][:, 0:384]).then_inc(S["tokT_saved"], 1)
            dve.wait_ge(S["mask_done"], 4)
            for b in range(2):
                dve.tensor_copy(X2B[:, b, D:66], mask_img[:, b:b + 1].to_broadcast([P, 2])).then_inc(S["x2b_ones"], 1)
            dve.wait_ge(S["consts"], CONSTS)

            def prepare_slices():
                dve.wait_ge(S["ffn_in"], 16 * FFN_LOADS)
                dve.tensor_scalar(rtemp[:, :], temp[:, :], 0.1, 5.0, ALU.max, ALU.min)\
                    .then_inc(S["temp_done"], 1)
                dve.wait_ge(S["temp_done"], 1)
                dve.reciprocal(temp[:, :], rtemp[:, :]).then_inc(S["temp_done"], 1)
                dve.wait_ge(S["prep_pe"], 1)
                v66 = lambda t: t.rearrange("p (a c) -> p a c", c=66)[:, :, 0:AUG]
                dve.tensor_copy(wfxT[:, :, 0:AUG], v66(pF[:, 0, 0:264]))
                dve.tensor_copy(wxT[:, :, 0:AUG], v66(pF[:, 1, 0:264]))
                dve.memset(wfxT[:, :, AUG:66], 0.0)
                dve.tensor_copy(fqkvT[:, :, :].rearrange("p a c -> p (a c)"), pF2[:, 0:384])\
                    .then_inc(S["prep_dve"], 1)
                dve.wait_ge(S["prep_pe"], 2)
                dve.tensor_copy(mqk[:, :], pF2[:, 0:P])
                for h2 in range(2):
                    rows = slice(64 * h2, 64 * h2 + 64)
                    dve.tensor_copy(f_bd[rows, :, h2, :],
                                    pF[rows, 0, 0:4 * D].rearrange("p (a c) -> p a c", c=D))
                dve.tensor_copy(w_logit[:, :, :].rearrange("p h g -> p (h g)"), pF[0:AUG, 1, :])\
                    .then_inc(S["temp_done"], 1)
                dve.wait_ge(S["temp_done"], 3)
                dve.tensor_tensor(w_logit[D:AUG, :, :], w_logit[D:AUG, :, :],
                                  bsl[D:AUG, :].unsqueeze(1).to_broadcast([1, NH, G]), ALU.add)\
                    .then_inc(S["temp_done"], 1)
                dve.wait_ge(S["temp_done"], 4)
                dve.tensor_tensor(w_logit[:, :, :], w_logit[:, :, :],
                                  temp[:, :].unsqueeze(2).to_broadcast([AUG, NH, G]), ALU.mult)\
                    .then_inc(S["prep_dve"], 1)
                dve.wait_ge(S["prep_pe"], 3)
                for h2 in range(2):
                    rows = slice(64 * h2, 64 * h2 + 64)
                    dve.tensor_scalar(e_bd[rows, :, h2, :],
                                      pF2[rows, 0:264].rearrange("p (a c) -> p a c", c=66),
                                      float(D) ** -0.5, None, ALU.mult)
                dve.tensor_copy(w_vo[:, :, :].rearrange("p h c -> p (h c)"), pF[0:AUG, 0, :])\
                    .then_inc(S["prep_dve"], 1)
                dve.wait_ge(S["prep_pe"], 4)
                for a in range(2):
                    last = dve.tensor_copy(w_qk[:, 2 * a:2 * a + 2, :, :].rearrange("p a h c -> p (a h c)"),
                                           pF[0:AUG, a, 0:264])
                last.then_inc(S["prep_dve"], 1)

            def window_sums(p, j, i):
                if i == 0:
                    dve.wait_ge(S["x_in0"], nth(p, 16, 16))
                    if ran(p - 1):
                        dve.wait_ge(S["qp_done"], nth(p - 1))
                        dve.wait_ge(S["qtok_done"], nth(p - 1, 2, 2))
                if i == 4:
                    dve.wait_ge(S["x_in1"], nth(p, 16, 16))
                src = X[:, j, i * 512:(i + 1) * 512].rearrange("p (r h c) -> p h r c", r=8, h=8)
                dve.tensor_reduce(qsum[:, i // 2, :, i % 2], src, AX.XY, ALU.add).then_inc(S["qsum_done"], 1)

            def whole_scores(p, half):
                dve.wait_ge(S["s_half"], nth(p, half + 1, 2))
                if half == 0 and ran(p - 1):
                    dve.wait_ge(S["p_masked"], nth(p - 1, 2, 2))
                src = pK[half][:, :].rearrange("p (g w l) -> p g w l", g=4, w=2)[:, :, 1, :]
                rows = slice(4 * half, 4 * half + 4)
                dve.scalar_tensor_tensor(out=Sc[:, rows, :], in0=src, scalar=mask_gw[:, 1:2],
                                         in1=St[:, rows, :], op0=ALU.mult, op1=ALU.add)\
                    .then_inc(S["s_whole"], 1)

            def shift_scores(p):
                dve.wait_ge(S["s_whole"], nth(p, 2, 2))
                dve.tensor_reduce(Smax[:, :], Sc[:, :, :], AX.X, ALU.max).then_inc(S["smax_done"], 1)
                dve.wait_ge(S["smax_done"], nth(p))
                dve.tensor_tensor(Sc[:, :, :], Sc[:, :, :],
                                  Smax[:, :].unsqueeze(2).to_broadcast([P, GROUPS, L]), ALU.subtract)\
                    .then_inc(S["s_shifted"], 1)

            def save_pt(p):
                dve.wait_ge(S["pt_done"], nth(p, 2, 2))
                if ran(p - 1):
                    dve.wait_ge(S["y_done"], nth(p - 1, 3, 3))
                dve.tensor_copy(PT[:, 4:8, :].rearrange("p g r -> p (g r)"), pK[1][:, :])\
                    .then_inc(S["pt_saved1"], 1)

            def whole_y(p, r):
                g0, g1 = Y_ROUNDS[r]
                dve.wait_ge(S["y_half"], nth(p, r + 1, 3))
                if r == 0 and ran(p - 1):
                    dve.wait_ge(S["y_scaled"], nth(p - 1, 3, 3))
                src = pK[r % 2][:, 0:(g1 - g0) * XW].rearrange("p (g c) -> p g c", c=XW)
                dve.scalar_tensor_tensor(out=Ye[:, g0:g1, :], in0=src[:, :, D:2 * D], scalar=mask_b[:, 1:2],
                                         in1=Yt[:, g0:g1, :], op0=ALU.mult, op1=ALU.add)\
                    .then_inc(S["y_whole"], 1)
                dve.reciprocal(rsum[:, g0:g1], src[:, :, P]).then_inc(S["y_recip"], 1)

            def context(p):
                dve.wait_ge(S["z_done"], nth(p))
                dve.tensor_tensor(Zm[:, :, :], pK[1][:, :].rearrange("p (w h) -> p w h", h=NH),
                                  mask_h[:, :].unsqueeze(1).to_broadcast([P, N, NH]), ALU.mult)\
                    .then_inc(S["z_masked"], 1)
                dve.wait_ge(S["z_masked"], nth(p))
                dve.tensor_reduce(ctxs[:, :], Zm[:, :, :], AX.X, ALU.add).then_inc(S["ctx_done"], 1)
                dve.wait_ge(S["ctx_done"], nth(p))
                if ran(p - 1):
                    dve.wait_ge(S["tok_done"], nth(p - 1))
                src = ctxs[:, :].rearrange("p (a h w b) -> p b a w h", a=4, h=4, w=2)
                for q in range(2):
                    rows = slice(64 * q, 64 * q + 64)
                    for b in range(2):
                        dve.tensor_scalar(ctxm[rows, b, :, :, q, :], src[rows, b], bv_col[rows, :], None,
                                          ALU.add).then_inc(S["ctx_placed"], 1)

            def norm(p, k, h):
                dve.bn_stats(stats[:, k, :], h[:, :]).then_inc(S["stats_done"], 1)
                dve.wait_ge(S["stats_done"], nth(p, k + 1, 2))
                dve.sem_inc(S["passed"], 1)
                dve.bn_aggr(mv[:, k, :], stats[:, k, :]).then_inc(S["mv_done"], 1)
                dve.wait_ge(S["mv_done"], nth(p, k + 1, 2))
                dve.tensor_scalar(vpe[:, k:k + 1], mv[:, k, 1:2], EPS, None, ALU.add).then_inc(S["vpe_done"], 1)

            def residual(p):
                dve.wait_ge(S["tok_done"], nth(p))
                dve.tensor_tensor(H[:, :], pG[:, 0:D], bo_row[:, :], ALU.add).then_inc(S["h_done"], 1)
                dve.wait_ge(S["h_done"], nth(p))
                norm(p, 0, H)

            def normed(p):
                dve.wait_ge(S["rstd_done"], nth(p, 1, 2))
                if ran(p - 1):
                    dve.wait_ge(S["xnt_done"], nth(p - 1))
                dve.tensor_scalar(xn[:, :], H[:, :], mv[:, 0, 0:1], rstd[:, 0:1], ALU.subtract, ALU.mult)\
                    .then_inc(S["xn_done"], 1)

            def residual2(p):
                dve.wait_ge(S["h2t_done"], nth(p))
                if ran(p - 1):
                    dve.wait_ge(S["r_done"], nth(p - 1))
                dve.tensor_tensor(H2[:, :], pG[:, 0:D], H[:, :], ALU.add).then_inc(S["h2_done"], 1)
                dve.wait_ge(S["h2_done"], nth(p))
                norm(p, 1, H2)

            def normed2(p):
                dve.wait_ge(S["rstd_done"], nth(p, 2, 2))
                if ran(p - 1):
                    dve.wait_ge(S["x2t_done"], nth(p - 1))
                    dve.wait_ge(S["x2b_done"], nth(p - 1, 2, 2))
                dve.tensor_scalar(x2n[:, :], H2[:, :], mv[:, 1, 0:1], rstd[:, 1:2], ALU.subtract, ALU.mult)\
                    .then_inc(S["x2n_done"], 1)

            def shift_logits(p):
                dve.wait_ge(S["lg_done"], nth(p))
                src = pF[:, 0, :].rearrange("p (h g) -> p h g", g=G)
                dve.tensor_reduce(lmax[:, :], src, AX.X, ALU.max).then_inc(S["lmax_done"], 1)
                dve.wait_ge(S["lmax_done"], nth(p))
                dve.tensor_tensor(W[:, :, :], src, lmax[:, :].unsqueeze(2).to_broadcast([P, NH, G]),
                                  ALU.subtract).then_inc(S["l_shifted"], 1)

            def slice_weights(p):
                dve.wait_ge(S["w_exp"], nth(p))
                dve.tensor_reduce(wsum[:, :], W[:, :, :], AX.X, ALU.add).then_inc(S["wsum_done"], 1)
                dve.wait_ge(S["wsum_done"], nth(p))
                dve.reciprocal(wrec[:, :], wsum[:, :]).then_inc(S["wrec_done"], 1)
                dve.wait_ge(S["wrec_done"], nth(p))
                dve.tensor_tensor(Wn[:, :, :], W[:, :, :], wrec[:, :].unsqueeze(2).to_broadcast([P, NH, G]),
                                  ALU.mult).then_inc(S["wn_done"], 1)

            def slice_means(p):
                dve.wait_ge(S["b_done"], nth(p))
                view = lambda t: t[:, 0:264].rearrange("p (a b c) -> p a b c", a=2, b=2)
                for i, src in enumerate((view(pF[:, 1, :]), view(pF2))):
                    dve.tensor_scalar(bden[:, 2 * i:2 * i + 2, :], src[:, :, :, D], 1e-5, None, ALU.add)\
                        .then_inc(S["bden_done"], 1)
                dve.wait_ge(S["bden_done"], nth(p, 2, 2))
                dve.reciprocal(brec[:, :, :], bden[:, :, :]).then_inc(S["brec_done"], 1)
                dve.wait_ge(S["brec_done"], nth(p))
                for i, src in enumerate((view(pF[:, 1, :]), view(pF2))):
                    dve.tensor_tensor(Bn[:, 2 * i:2 * i + 2, :, :], src,
                                      brec[:, 2 * i:2 * i + 2, :].unsqueeze(3).to_broadcast([P, 2, 2, 66]),
                                      ALU.mult).then_inc(S["bn_done"], 1)

            def save_bt0(p):
                dve.wait_ge(S["bt_done"], nth(p, 1, 2))
                dve.tensor_copy(Bt[:, 0:2, :, :, :].rearrange("p a b h g -> p (a b h g)"), pF2[0:AUG, :])\
                    .then_inc(S["bt_saved0"], 1)

            def save_t1(p):
                dve.wait_ge(S["t_done"], nth(p, 2, 2))
                dve.tensor_copy(T[:, 4:8, :].rearrange("p h g -> p (h g)"), pF2[0:AUG, :])\
                    .then_inc(S["t_saved1"], 1)

            def save_v1(p):
                dve.wait_ge(S["v_done"], nth(p))
                dve.tensor_copy(V[64:128, :, :, :].rearrange("p b a c -> p (b a) c"),
                                pF[64:128, :, :].rearrange("p b (a h c) -> p (b a) h c", a=4, h=2)[:, :, 1, :])\
                    .then_inc(S["v_saved1"], 1)

            def shift_slices(p):
                dve.wait_ge(S["a_done"], nth(p))
                src = pF2[:, :].rearrange("p (h g) -> p h g", g=G)
                dve.tensor_reduce(amax[:, :], src, AX.X, ALU.max).then_inc(S["amax_done"], 1)
                dve.wait_ge(S["amax_done"], nth(p))
                dve.tensor_tensor(A[:, :, :], src, amax[:, :].unsqueeze(2).to_broadcast([P, NH, G]),
                                  ALU.subtract).then_inc(S["a_shifted"], 1)

            def slice_attention(p):
                dve.wait_ge(S["a_exp"], nth(p))
                dve.tensor_reduce(asum[:, :], A[:, :, :], AX.X, ALU.add).then_inc(S["asum_done"], 1)
                dve.wait_ge(S["asum_done"], nth(p))
                dve.reciprocal(arec[:, :], asum[:, :]).then_inc(S["arec_done"], 1)
                dve.wait_ge(S["arec_done"], nth(p))
                dve.tensor_tensor(An[:, :, :], A[:, :, :], arec[:, :].unsqueeze(2).to_broadcast([P, NH, G]),
                                  ALU.mult).then_inc(S["an_done"], 1)

            def add_out(p):
                dve.wait_ge(S["o_done"], nth(p))
                dve.wait_ge(S["r_done"], nth(p))
                dve.wait_ge(S["stored"], 16 * p + 16)
                dve.tensor_tensor(O[:, :], pF2[:, 0:D], R[:, :], ALU.add).then_inc(S["o_added"], 1)

            def slot(s, j, a, b, d):
                k = 1 - j
                if d: shift_logits(s - 2)
                if b: save_pt(s - 1)
                if d: slice_weights(s - 2)
                if a:
                    for i in range(4): window_sums(s, j, i)
                if b: whole_y(s - 1, 0)
                if d: slice_means(s - 2)
                if b: whole_y(s - 1, 1)
                if a:
                    for i in range(4, 8): window_sums(s, j, i)
                if b: whole_y(s - 1, 2)
                if d: save_bt0(s - 2)
                if b: context(s - 1)
                if d: save_t1(s - 2); save_v1(s - 2)
                if b: residual(s - 1)
                if d: shift_slices(s - 2)
                if b: normed(s - 1)
                if d: slice_attention(s - 2)
                if a: whole_scores(s, 0); whole_scores(s, 1); shift_scores(s)
                if d: add_out(s - 2)
                if b: residual2(s - 1); normed2(s - 1)
                if isinstance(s, int) and s == 0:
                    prepare_slices()

            run_slots(dve, slot)



_INS = ["x", "L0_tok_Wq", "L0_tok_bq", "L0_tok_Wk", "L0_tok_bk", "L0_tok_Wv", "L0_tok_bv", "L0_tok_Wo",
        "L0_tok_bo", "L0_attn_W_ih", "L0_attn_W_hh", "L0_attn_b_ih", "L0_attn_b_hh", "L0_ffn_W_fx",
        "L0_ffn_b_fx", "L0_ffn_W_x", "L0_ffn_b_x", "L0_ffn_W_slice", "L0_ffn_b_slice", "L0_ffn_W_q",
        "L0_ffn_W_k", "L0_ffn_W_v", "L0_ffn_W_out", "L0_ffn_b_out", "L0_ffn_temperature"]


def kernel(**inputs):
    import numpy as _np
    import concourse.bacc as _bacc
    from concourse import mybir as _mybir
    from concourse.bass_utils import run_bass_kernel_spmd as _run

    nc = _bacc.Bacc("TRN2", target_bir_lowering=False, num_devices=1)
    arrays, args = {}, []
    for name in _INS:
        a = _np.ascontiguousarray(inputs[name])
        arrays[f"in_{name}"] = a
        args.append(nc.dram_tensor(f"in_{name}", a.shape, _mybir.dt.from_np(a.dtype), kind="ExternalInput").ap())
    out = nc.dram_tensor("out_0", (16, 64, 64), _mybir.dt.float32, kind="ExternalOutput").ap()
    vit_tower_kernel(nc, *args, out)
    r = _run(nc, [arrays], core_ids=[0])
    return r.results[0]["out_0"]
```

```python
import concourse.bass as bass
from concourse import mybir
from contextlib import ExitStack



def vit_tower_kernel(nc, x, tWq, tbq, tWk, tbk, tWv, tbv, tWo, tbo, W_ih, W_hh, b_ih, b_hh,
                     W_fx, b_fx, W_x, b_x, W_slice, b_slice, W_q, W_k, W_v, W_out, b_out,
                     temperature, out):
    fp32 = mybir.dt.float32
    ALU = mybir.AluOpType
    ACT = mybir.ActivationFunctionType
    AX = mybir.AxisListType

    P = 128
    B, D, HT, WD = x.shape
    GS = 8
    NH = 8
    DH = D // NH
    L = GS * GS
    N = (HT // GS) * (WD // GS)
    PIX = HT * WD
    PAIRS = B // 2
    GROUPS = 8
    CHUNKS = 32
    G = 64
    INNER = NH * D
    XW = P + 2
    AUG = D + 1
    EPS = 1e-5
    Y_ROUNDS = ((0, 3), (3, 6), (6, 8))

    x_v = x.rearrange("(t b) d w h -> t (b d) (w h)", b=2)
    out_v = out.rearrange("(t b) n c -> t (b n) c", b=2)

    ctx = ExitStack()
    with ctx:
        def sb(name, shape):
            return ctx.enter_context(nc.sbuf_tensor(name, shape, fp32))

        def bank(name, shape):
            return ctx.enter_context(nc.psum_tensor(name, shape, fp32))

        ident = sb("ident", [P, P])
        ones = sb("ones", [P, P])
        mask_gw = sb("mask_gw", [P, 2])
        mask_w = sb("mask_w", [P, 8])
        mask_bh = sb("mask_bh", [P, 16])
        mask_b = sb("mask_b", [P, 2])
        mask_img = sb("mask_img", [P, 2])
        mask_h = sb("mask_h", [P, NH])
        id_mean = sb("id_mean", [P, D])
        wq_bd = sb("wq_bd", [P, P])
        wk_bd = sb("wk_bd", [P, P])
        wv_bd = sb("wv_bd", [P, P])
        wo2 = sb("wo2", [D, P])
        wr2 = sb("wr2", [D, P])
        tokT = sb("tokT", [P, 384])
        wqT, wvT = tokT[:, 0:P], tokT[:, P:2 * P]
        woT, wrT = tokT[:, 256:320], tokT[:, 320:384]
        bq_col = sb("bq_col", [P, 1])
        bk_col = sb("bk_col", [P, 1])
        bk_rep = sb("bk_rep", [P, P])
        bv_col = sb("bv_col", [P, 1])
        bo_row = sb("bo_row", [P, D])
        rnn_b2 = sb("rnn_b2", [P, 2])
        rnn_b = sb("rnn_b", [P, 1])
        wfx = sb("wfx", [AUG, INNER])
        wxa = sb("wxa", [AUG, INNER])
        wsl_bd = sb("wsl_bd", [P, P])
        fq_bd = sb("fq_bd", [P, P])
        fk_bd = sb("fk_bd", [P, P])
        fv_bd = sb("fv_bd", [P, P])
        wout = sb("wout", [P, 4, D])
        bout_row = sb("bout_row", [P, D])
        bsl = sb("bsl", [AUG, G])
        temp = sb("temp", [AUG, NH])
        rtemp = sb("rtemp", [AUG, NH])
        wfxT = sb("wfxT", [P, 4, 66])
        wxT = sb("wxT", [P, 4, 66])
        fqkvT = sb("fqkvT", [P, 3, P])
        mqk = sb("mqk", [P, P])
        e_bd = sb("e_bd", [P, 4, 2, 66])
        f_bd = sb("f_bd", [P, 4, 2, D])
        w_logit = sb("w_logit", [AUG, NH, G])
        w_qk = sb("w_qk", [AUG, 4, 2, 66])
        w_vo = sb("w_vo", [AUG, NH, D])

        X = sb("X", [P, 2, PIX])
        Xw = sb("Xw", [P, 2, CHUNKS, P])
        XT = sb("XT", [P, CHUNKS, XW])
        qsum = sb("qsum", [P, 4, 8, 2])
        qtok = sb("qtok", [P, 2, 2, 4, 2, 8])
        qp = sb("qp", [P, N])
        qpm = sb("qpm", [P, N, NH])
        U = sb("U", [P, N, 2, NH])
        St = sb("St", [P, GROUPS, L])
        Sc = sb("Sc", [P, GROUPS, L])
        Smax = sb("Smax", [P, GROUPS])
        full_max = sb("full_max", [P, GROUPS])
        shift = sb("shift", [P, GROUPS])
        kbw = sb("kbw", [P, GROUPS, 8])
        kb = sb("kb", [P, GROUPS])
        Pm = sb("Pm", [P, GROUPS, 2, L])
        PT = sb("PT", [P, GROUPS, P])
        Yt = sb("Yt", [P, GROUPS, D])
        Ye = sb("Ye", [P, GROUPS, D])
        Yn = sb("Yn", [P, GROUPS, D])
        rsum = sb("rsum", [P, GROUPS])
        YT = sb("YT", [P, 4 * P])
        Zm = sb("Zm", [P, N, NH])
        ctxs = sb("ctxs", [P, N])
        ctxm = sb("ctxm", [P, 2, 4, 2, 2, 4])
        H = sb("H", [P, D])
        H2 = sb("H2", [P, D])
        stats = sb("stats", [P, 2, 6])
        mv = sb("mv", [P, 2, 2])
        vpe = sb("vpe", [P, 2])
        neghalf = sb("neghalf", [P, 1])
        rstd = sb("rstd", [P, 2])
        xn = sb("xn", [P, D])
        x2n = sb("x2n", [P, D])
        RX = sb("RX", [P, 4, N])
        X2T = sb("X2T", [AUG, P])
        X2B = sb("X2B", [P, 2, 66])
        R = sb("R", [P, D])
        lmax = sb("lmax", [P, NH])
        W = sb("W", [P, NH, G])
        wsum = sb("wsum", [P, NH])
        wrec = sb("wrec", [P, NH])
        Wn = sb("Wn", [P, NH, G])
        WX = sb("WX", [P, NH, 2, G])
        WT = sb("WT", [P, NH, P])
        bden = sb("bden", [P, 4, 2])
        brec = sb("brec", [P, 4, 2])
        Bn = sb("Bn", [P, 4, 2, 66])
        Bt = sb("Bt", [AUG, 4, 2, 2, G])
        T = sb("T", [AUG, NH, P])
        V = sb("V", [P, 2, 4, D])
        amax = sb("amax", [P, NH])
        A = sb("A", [P, NH, G])
        asum = sb("asum", [P, NH])
        arec = sb("arec", [P, NH])
        An = sb("An", [P, NH, G])
        M = sb("M", [P, 4, P])
        O = sb("O", [P, D])

        pX = [bank(f"pX{i}", [P, 4, P]) for i in range(2)]
        pK = [bank(f"pK{i}", [P, 512]) for i in range(2)]
        pF = bank("pF", [P, 2, 512])
        pF2 = bank("pF2", [P, 512])
        pG = bank("pG", [P, 512])

        SEMS = """
        passed x_in0 x_in1 windowed x2b_ones tok_zeroed ffn_zeroed ident_zero consts mask_done id_mean_done ones_set rnn_b_done
        tok_in tokT_done tokT_saved ffn_in temp_done prep_pe prep_dve
        xt_done xt_saved qsum_done qtok_done qp_done qp_saved c_done c_masked kb_done bk_rep_done full_max_done shift_done qpm_done u_done u_saved
        s_done s_half s_whole smax_done s_shifted p_exp p_masked
        pt_done pt_saved0 pt_saved1 y_done y_half y_whole y_recip y_scaled yt_done yt_saved
        z_done z_masked ctx_done ctx_placed tok_done h_done stats_done0 mv_done0 vpe_done0 rstd_done0
        stats_done1 mv_done1 vpe_done1 rstd_done1
        xn_done xnt_done xnt_saved rnn_done state_done h2t_done h2_done x2n_done x2b_done
        x2t_done x2t_saved r_done
        lg_done lmax_done l_shifted w_exp wsum_done wrec_done wn_done wx_done
        b_done bden_done brec_done bn_done wt_done wt_saved bt_done bt_saved0 bt_saved1
        t_done t_saved0 t_saved1 v_done v_saved0 v_saved1
        a_done amax_done a_shifted a_exp asum_done arec_done an_done
        m_done m_saved o_done o_added stored
        """.split()
        S = {name: ctx.enter_context(nc.semaphore("s_" + name)) for name in SEMS}

        def nth(pair, k=1, per=1):
            return per * pair + k

        def has(pair):
            return not isinstance(pair, int) or 0 <= pair < PAIRS

        LAGS = 3

        FIRST = PAIRS - (PAIRS - LAGS - 1) // 2 * 2

        def run_slots(engine, steps, after_first=None):
            def slot(s, j):
                def do(lag, step, *args):
                    if has(s - lag):
                        step(s - lag, (j - lag) % 2, *args)
                steps(do)

            for s in range(FIRST):
                slot(s, s % 2)
                if s == 0 and after_first:
                    after_first()
            with engine.Fori(FIRST, PAIRS - 1, 2) as it:
                for j in range(2):
                    slot(it + j, (FIRST + j) % 2)
            for s in range(PAIRS, PAIRS + LAGS):
                slot(s, s % 2)


        block = ctx.enter_context(nc.Block())

        TOK_LOADS = 19
        FFN_LOADS = 16
        CONSTS = 5

        @block.sync
        def _(sp):
            def load(p, j):
                if has(p - 2):
                    sp.wait_ge(S["windowed"], nth(p - 2, 8, 8))
                    sp.sem_inc(S["passed"], 1)
                    sp.wait_ge(S["qsum_done"], nth(p - 2, 8, 8))
                    sp.sem_inc(S["passed"], 1)
                for half, name in enumerate(("x_in0", "x_in1")):
                    if has(p - 1):
                        sp.wait_ge(S[name], 16 * p)
                        sp.sem_inc(S["passed"], 1)
                    sp.dma_start(X[:, j, half * 2048:(half + 1) * 2048],
                                 x_v[p, :, half * 2048:(half + 1) * 2048]).then_inc(S[name], 16)

            def store(p):
                sp.wait_ge(S["o_added"], nth(p))
                sp.sem_inc(S["passed"], 1)
                sp.dma_start(out_v[p, :, :], O[:, :]).then_inc(S["stored"], 16)

            sp.sem_inc(S["stored"], 16)
            load(0, 0)
            load(1, 1)
            sp.wait_ge(S["ffn_zeroed"], 1)
            sp.wait_ge(S["tok_in"], 16 * TOK_LOADS)
            sp.dma_start(wfx[0:D, :], W_fx[:, :]).then_inc(S["ffn_in"], 16)
            sp.dma_start(wfx[D:AUG, :], b_fx.unsqueeze(0)).then_inc(S["ffn_in"], 16)
            sp.dma_start(wxa[0:D, :], W_x[:, :]).then_inc(S["ffn_in"], 16)
            sp.dma_start(wxa[D:AUG, :], b_x.unsqueeze(0)).then_inc(S["ffn_in"], 16)
            for h2 in range(2):
                rows = slice(64 * h2, 64 * h2 + 64)
                sp.dma_start(wsl_bd[rows, rows], W_slice[:, :]).then_inc(S["ffn_in"], 16)
                sp.dma_start(fq_bd[rows, rows], W_q[:, :]).then_inc(S["ffn_in"], 16)
                sp.dma_start(fk_bd[rows, rows], W_k[:, :]).then_inc(S["ffn_in"], 16)
                sp.dma_start(fv_bd[rows, rows], W_v[:, :]).then_inc(S["ffn_in"], 16)
            sp.dma_start(wout[:, :, :], W_out.rearrange("(a p) c -> p a c", p=P)).then_inc(S["ffn_in"], 16)
            sp.dma_start(bout_row[:, :], b_out.partition_broadcast(P)).then_inc(S["ffn_in"], 16)
            sp.dma_start(bsl[D:AUG, :], b_slice.unsqueeze(0)).then_inc(S["ffn_in"], 16)
            sp.dma_start(temp[:, :], temperature[0, :, 0, 0].partition_broadcast(AUG)).then_inc(S["ffn_in"], 16)
            for p in range(2, 4):
                load(p, p % 2)
            with sp.Fori(4, PAIRS - 1, 2) as it:
                for j in range(2):
                    load(it + j, j)
                    store(it + j - 4)
            for p in range(PAIRS - 4, PAIRS):
                store(p)
            sp.wait_ge(S["stored"], 16 * PAIRS + 16)

        @block.gpsimd
        def _(pool):
            pool.memset(ident[:, :], 0.0).then_inc(S["ident_zero"], 1)
            pool.wait_ge(S["ident_zero"], 1)
            pool.affine_select(out=ident[:, :], in_=ident[:, :], compare_op=ALU.not_equal, fill=1.0,
                               base=0, pattern=[[-1, P]], channel_multiplier=1).then_inc(S["consts"], 1)
            for t in (wsl_bd, fq_bd, fk_bd, fv_bd):
                pool.memset(t[:, :], 0.0)
            pool.memset(neghalf[:, :], -0.5).then_inc(S["ffn_zeroed"], 1)
            pool.memset(U[:, :, :, :], 0.0).then_inc(S["consts"], 1)
            pool.memset(ctxm[:, :, :, :, :, :], 0.0).then_inc(S["consts"], 1)
            pool.memset(e_bd[:, :, :, :], 0.0).then_inc(S["consts"], 1)
            pool.memset(f_bd[:, :, :, :], 0.0).then_inc(S["consts"], 1)
            pool.wait_ge(S["mask_done"], 6)

            def wx(p, j):
                pool.wait_ge(S["wn_done"], nth(p))
                if has(p - 1):
                    pool.wait_ge(S["wt_done"], nth(p - 1, 2, 2))
                pool.sem_inc(S["passed"], 1)
                for b in range(2):
                    pool.tensor_scalar(WX[:, :, b, :], Wn[:, :, :], mask_img[:, b:b + 1], 1.0,
                                       ALU.mult, ALU.mult).then_inc(S["wx_done"], 1)

            def y_scale(p, j, r):
                g0, g1 = Y_ROUNDS[r]
                pool.wait_ge(S["y_whole"], nth(p, r + 1, 3))
                pool.wait_ge(S["y_recip"], nth(p, r + 1, 3))
                if has(p - 1):
                    pool.wait_ge(S["yt_done"], nth(p - 1))
                pool.tensor_tensor(Yn[:, g0:g1, :], Ye[:, g0:g1, :],
                                   rsum[:, g0:g1].unsqueeze(2).to_broadcast([P, g1 - g0, D]),
                                   ALU.mult).then_inc(S["y_scaled"], 1)

            def spread_q(p, j):
                pool.wait_ge(S["qp_saved"], nth(p))
                if has(p - 1):
                    pool.wait_ge(S["u_done"], nth(p - 1))
                pool.tensor_tensor(qpm[:, :, :], qp[:, :].unsqueeze(2).to_broadcast([P, N, NH]),
                                   mask_h[:, :].unsqueeze(1).to_broadcast([P, N, NH]),
                                   ALU.mult).then_inc(S["qpm_done"], 1)

            def window_tokens(p, j):
                pool.wait_ge(S["qsum_done"], nth(p, 8, 8))
                if has(p - 2):
                    pool.wait_ge(S["tok_done"], nth(p - 2))
                pool.sem_inc(S["passed"], 1)
                for b in range(2):
                    pool.tensor_scalar(qtok[:, j, b, :, :, :], qsum[:, :, :, :].rearrange("p a h w -> p a w h"),
                                       mask_img[:, b:b + 1], 1.0, ALU.mult, ALU.mult)\
                        .then_inc(S["qtok_done"], 1)

            def power(p, j, k):
                pool.wait_ge(S[f"vpe_done{k}"], nth(p))
                pool.tensor_tensor(rstd[:, k:k + 1], vpe[:, k:k + 1], neghalf[:, :], ALU.pow)\
                    .then_inc(S[f"rstd_done{k}"], 1)

            def mask_p(p, j):
                pool.wait_ge(S["p_exp"], nth(p))
                if has(p - 1):
                    pool.wait_ge(S["pt_done"], nth(p - 1, 2, 2))
                pool.sem_inc(S["passed"], 1)
                for gw in range(2):
                    pool.tensor_scalar(Pm[:, :, gw, :], Sc[:, :, :], mask_gw[:, gw:gw + 1], 1.0,
                                       ALU.mult, ALU.mult).then_inc(S["p_masked"], 1)

            def x2_blocks(p, j):
                pool.wait_ge(S["x2n_done"], nth(p))
                if has(p - 1):
                    pool.wait_ge(S["b_done"], nth(p - 1))
                pool.sem_inc(S["passed"], 1)
                for b in range(2):
                    pool.tensor_scalar(X2B[:, b, 0:D], x2n[:, :], mask_img[:, b:b + 1], 1.0,
                                       ALU.mult, ALU.mult).then_inc(S["x2b_done"], 1)

            def residual_bias(p, j):
                if isinstance(p, int) and p == 0:
                    pool.wait_ge(S["ffn_in"], 16 * FFN_LOADS)
                pool.wait_ge(S["h2_done"], nth(p))
                if has(p - 1):
                    pool.wait_ge(S["o_added"], nth(p - 1))
                pool.tensor_tensor(R[:, :], H2[:, :], bout_row[:, :], ALU.add).then_inc(S["r_done"], 1)

            def steps(do):
                do(1, window_tokens); do(2, power, 0); do(1, mask_p); do(2, power, 1); do(2, x2_blocks)
                do(1, y_scale, 0); do(0, spread_q); do(2, wx); do(1, y_scale, 1); do(1, y_scale, 2)
                do(2, residual_bias)

            run_slots(pool, steps)

        @block.tensor
        def _(pe):
            pe.wait_ge(S["consts"], 1)
            pe.wait_ge(S["tok_in"], 16 * TOK_LOADS)
            pe.transpose(pK[0][:, 0:P], wq_bd[:, :], ident[:, :])
            pe.transpose(pK[0][:, P:2 * P], wv_bd[:, :], ident[:, :])
            pe.transpose(pK[0][:, 256:320], wo2[:, :], ident[0:D, 0:D])
            pe.transpose(pK[0][:, 320:384], wr2[:, :], ident[0:D, 0:D]).then_inc(S["tokT_done"], 1)
            pe.wait_ge(S["tokT_saved"], 1)
            pe.wait_ge(S["id_mean_done"], 1)
            pe.wait_ge(S["bk_rep_done"], 1)
            pe.wait_ge(S["consts"], CONSTS)

            def prepare_slices():
                pe.wait_ge(S["ffn_in"], 16 * FFN_LOADS)
                for hp in range(4):
                    pe.transpose(pF[:, 0, 66 * hp:66 * hp + AUG], wfx[:, hp * P:(hp + 1) * P],
                                 ident[0:AUG, 0:AUG])
                    pe.transpose(pF[:, 1, 66 * hp:66 * hp + AUG], wxa[:, hp * P:(hp + 1) * P],
                                 ident[0:AUG, 0:AUG])
                for k, w in enumerate((fq_bd, fk_bd, fv_bd)):
                    last = pe.transpose(pF2[:, k * P:(k + 1) * P], w[:, :], ident[:, :])
                last.then_inc(S["prep_pe"], 1)
                pe.wait_ge(S["prep_dve"], 1)
                fqT, fkT, fvT = (fqkvT[:, k, :] for k in range(3))
                pe.matmul(pF2[:, 0:P], fkT, fqT, start=True, stop=True)
                pe.matmul(pF[:, 0, 0:4 * D], fvT, wout[:, :, :].rearrange("p a c -> p (a c)"),
                          start=True, stop=True)
                for hp in range(4):
                    last = pe.matmul(pF[0:AUG, 1, hp * P:(hp + 1) * P], wxT[:, hp, 0:AUG], wsl_bd[:, :],
                                     start=True, stop=True)
                last.then_inc(S["prep_pe"], 1)
                pe.wait_ge(S["prep_dve"], 2)
                pe.matmul(pF2[:, 0:264], mqk[:, :], wfxT[:, :, :].rearrange("p a c -> p (a c)"),
                          start=True, stop=True)
                for hp in range(4):
                    last = pe.matmul(pF[0:AUG, 0, hp * P:(hp + 1) * P], wfxT[:, hp, 0:AUG],
                                     f_bd[:, hp, :, :].rearrange("p a c -> p (a c)"),
                                     start=True, stop=True)
                last.then_inc(S["prep_pe"], 1)
                pe.wait_ge(S["prep_dve"], 3)
                for hp in range(4):
                    last = pe.matmul(pF[0:AUG, hp // 2, (hp % 2) * 132:(hp % 2) * 132 + 132],
                                     wfxT[:, hp, 0:AUG], e_bd[:, hp, :, :].rearrange("p a c -> p (a c)"),
                                     start=True, stop=True)
                last.then_inc(S["prep_pe"], 1)
                pe.wait_ge(S["prep_dve"], 4)

            def transpose_x(p, j, i):
                if i == 0:
                    pe.wait_ge(S["s_whole"], nth(p, 1, 2))
                elif i == 1:
                    pe.wait_ge(S["s_whole"], nth(p, 2, 2))
                else:
                    pe.wait_ge(S["xt_saved"], nth(p, i - 1, 8))
                pe.wait_ge(S["windowed"], nth(p, i // 2 * 2 + 2, 8))
                for c in range(4):
                    last = pe.transpose(pX[i % 2][:, c, :],
                                        Xw[:, j, 4 * i + c, :], ident[:, :])
                last.then_inc(S["xt_done"], 1)

            def query(p, j):
                if has(p - 2):
                    pe.wait_ge(S["x2t_saved"], nth(p - 2))
                elif has(p - 1):
                    pe.wait_ge(S["c_masked"], nth(p - 1))
                pe.wait_ge(S["qsum_done"], nth(p, 8, 8))
                pe.matmul(pG[:, 0:N], wqT, qsum[:, :, :, :].rearrange("p a h w -> p (a h w)"),
                          start=True, stop=True).then_inc(S["qp_done"], 1)

            def key_bias(p, j):
                pe.wait_ge(S["qp_saved"], nth(p))
                pe.matmul(pG[:, 0:N], bk_rep[:, :], qp[:, :], start=True, stop=True).then_inc(S["c_done"], 1)

            def keys_for_query(p, j):
                if has(p - 1):
                    pe.wait_ge(S["y_whole"], nth(p - 1, 3, 3))
                    pe.wait_ge(S["y_recip"], nth(p - 1, 3, 3))
                pe.wait_ge(S["qpm_done"], nth(p))
                pe.matmul(pK[0][:, :], wk_bd[:, :], qpm[:, :, :].rearrange("p w h -> p (w h)"),
                          start=True, stop=True).then_inc(S["u_done"], 1)

            def scores(p, j, half):
                if half == 0:
                    if has(p - 1):
                        pe.wait_ge(S["xt_saved"], nth(p - 1, 7, 8))
                elif half == 1:
                    if has(p - 1):
                        pe.wait_ge(S["xt_saved"], nth(p - 1, 8, 8))
                if half == 0:
                    pe.wait_ge(S["u_saved"], nth(p, 2, 2))
                pe.wait_ge(S["windowed"], nth(p, 4 * half + 4, 8))
                for g4 in range(4):
                    g = 4 * half + g4
                    for c in range(4):
                        gh = 4 * (g % 2) + c
                        k = (g // 2) * 8 + gh
                        last = pe.matmul(pX[half][32 * c:32 * c + 32, g4, :],
                                         U[:, 2 * k:2 * k + 2, :, :].rearrange("p w b h -> p (w b h)"),
                                         Xw[:, j, k, :], start=True, stop=True)
                last.then_inc(S["s_done"], 1)

            def transpose_p(p, j, half):
                if half == 0:
                    pe.wait_ge(S["u_saved"], nth(p, 2, 2))
                elif half == 1:
                    if has(p - 1):
                        pe.wait_ge(S["z_masked"], nth(p - 1))
                pe.wait_ge(S["p_masked"], nth(p, 2, 2))
                for g4 in range(4):
                    last = pe.transpose(pK[half][:, g4 * P:(g4 + 1) * P],
                                        Pm[:, 4 * half + g4, :, :].rearrange("p w l -> p (w l)"), ident[:, :])
                last.then_inc(S["pt_done"], 1)

            def weighted_sum(p, j, r):
                if r == 0:
                    pe.wait_ge(S["pt_saved0"], nth(p))
                elif r == 1:
                    pe.wait_ge(S["pt_saved1"], nth(p))
                elif r == 2:
                    pe.wait_ge(S["y_whole"], nth(p, 1, 3))
                    pe.wait_ge(S["y_recip"], nth(p, 1, 3))
                g0, g1 = Y_ROUNDS[r]
                if r == 0:
                    pe.wait_ge(S["pt_saved0"], nth(p))
                if r == 1:
                    pe.wait_ge(S["pt_saved1"], nth(p))
                pe.wait_ge(S["xt_saved"], nth(p, g1, 8))
                for g in range(g0, g1):
                    for c in range(4):
                        last = pe.matmul(pK[r % 2][32 * c:32 * c + 32, (g - g0) * XW:(g - g0 + 1) * XW],
                                         PT[:, g, 32 * c:32 * c + 32],
                                         XT[:, 4 * g + c, :], start=True, stop=True)
                last.then_inc(S["y_done"], 1)

            def transpose_y(p, j):
                pe.wait_ge(S["y_whole"], nth(p, 2, 3))
                pe.wait_ge(S["y_recip"], nth(p, 2, 3))
                pe.wait_ge(S["y_scaled"], nth(p, 3, 3))
                for a in range(4):
                    last = pe.transpose(pK[1][:, a * P:(a + 1) * P],
                                        Yn[:, 2 * a:2 * a + 2, :].rearrange("p q d -> p (q d)"), ident[:, :])
                last.then_inc(S["yt_done"], 1)

            def values(p, j):
                pe.wait_ge(S["yt_saved"], nth(p))
                pe.matmul(pK[1][:, :], wvT, YT[:, :], start=True, stop=True).then_inc(S["z_done"], 1)

            def tokens(p, j):
                if has(p + 1):
                    pe.wait_ge(S["c_masked"], nth(p + 1))
                elif has(p - 1):
                    pe.wait_ge(S["x2t_saved"], nth(p - 1))
                else:
                    pe.wait_ge(S["c_masked"], nth(p))
                pe.wait_ge(S["ctx_placed"], nth(p, 4, 4))
                pe.wait_ge(S["qtok_done"], nth(p, 2, 2))
                pe.matmul(pG[:, 0:D], ctxm[:, :, :, :, :, :].rearrange("p b a w q h -> p (b a w q h)"), woT,
                          start=True, stop=False)
                pe.matmul(pG[:, 0:D], qtok[:, j, :, :, :, :].rearrange("p b a w h -> p (b a w h)"), id_mean[:, :],
                          start=False, stop=True).then_inc(S["tok_done"], 1)

            def transpose_xn(p, j):
                pe.wait_ge(S["h_done"], nth(p))
                pe.wait_ge(S["xn_done"], nth(p))
                pe.sem_inc(S["passed"], 1)
                pe.transpose(pG[0:D, 0:P], xn[:, :], ident[:, :]).then_inc(S["xnt_done"], 1)

            def recur(p, j, i):
                if i == 0:
                    pe.wait_ge(S["xnt_saved"], nth(p, 2, 2))
                elif i == 1:
                    pe.wait_ge(S["state_done"], nth(p, 1, 2))
                if i == 0:
                    pe.wait_ge(S["xnt_saved"], nth(p, 2, 2))
                else:
                    pe.wait_ge(S["state_done"], nth(p, 1, 2))
                pe.matmul(pG[64:128, 0:N], wrT, RX[:, (2 * j + i - 1) % 4, :],
                          start=True, stop=True).then_inc(S["rnn_done"], 1)

            def transpose_h(p, j):
                pe.wait_ge(S["state_done"], nth(p, 2, 2))
                pe.sem_inc(S["passed"], 1)
                pe.transpose(pG[:, 0:D], RX[64:128, 2 * j:2 * j + 2, :].rearrange("p t n -> p (t n)"),
                             ident[64:128, 64:128]).then_inc(S["h2t_done"], 1)

            def transpose_x2(p, j):
                pe.wait_ge(S["h2_done"], nth(p))
                pe.wait_ge(S["x2n_done"], nth(p))
                pe.sem_inc(S["passed"], 1)
                pe.transpose(pG[0:D, 0:P], x2n[:, :], ident[:, :]).then_inc(S["x2t_done"], 1)

            def logits(p, j):
                if has(p - 1):
                    pe.wait_ge(S["m_saved"], nth(p - 1))
                pe.wait_ge(S["x2t_saved"], nth(p))
                pe.matmul(pF[:, 0, :], X2T[:, :], w_logit[:, :, :].rearrange("p h g -> p (h g)"),
                          start=True, stop=True).then_inc(S["lg_done"], 1)

            def slice_sums(p, j):
                if has(p - 1):
                    pe.wait_ge(S["v_saved0"], nth(p - 1))
                    pe.wait_ge(S["v_saved1"], nth(p - 1))
                if has(p - 1):
                    pe.wait_ge(S["o_added"], nth(p - 1))
                pe.wait_ge(S["wn_done"], nth(p))
                pe.wait_ge(S["x2b_done"], nth(p, 2, 2))
                for hp in range(4):
                    last = pe.matmul((pF[:, 1, 0:264] if hp < 2 else pF2[:, 0:264])[:, (hp % 2) * 132:(hp % 2) * 132 + 132],
                                     Wn[:, 2 * hp:2 * hp + 2, :].rearrange("p h g -> p (h g)"),
                                     X2B[:, :, :].rearrange("p b c -> p (b c)"), start=True, stop=True)
                last.then_inc(S["b_done"], 1)

            def transpose_w(p, j, half):
                if half == 0:
                    pe.wait_ge(S["l_shifted"], nth(p))
                elif half == 1:
                    pe.wait_ge(S["bn_done"], nth(p, 2, 2))
                pe.wait_ge(S["wx_done"], nth(p, 2, 2))
                for h in range(4 * half, 4 * half + 4):
                    last = pe.transpose(pF[:, half, (h % 4) * P:(h % 4 + 1) * P],
                                        WX[:, h, :, :].rearrange("p b g -> p (b g)"), ident[:, :])
                last.then_inc(S["wt_done"], 1)

            def transpose_b(p, j, half):
                if half == 0:
                    pe.wait_ge(S["bn_done"], nth(p, 2, 2))
                elif half == 1:
                    pe.wait_ge(S["wt_saved"], nth(p, 1, 2))
                pe.wait_ge(S["bn_done"], nth(p, 2, 2))
                dst = pF2 if half == 0 else pF[:, 0, :]
                for i in range(4):
                    hp, b = 2 * half + i // 2, i % 2
                    last = pe.transpose(dst[0:AUG, i * P:(i + 1) * P], Bn[:, hp, b, 0:AUG], ident[:, :])
                last.then_inc(S["bt_done"], 1)

            def slice_keys(p, j, half):
                if half == 0:
                    pe.wait_ge(S["wt_saved"], nth(p, 2, 2))
                elif half == 1:
                    pe.wait_ge(S["bt_saved0"], nth(p))
                pe.wait_ge(S[("bt_saved0", "bt_saved1")[half]], nth(p))
                dst = pF[:, 1, :] if half == 0 else pF2
                for i in range(4):
                    hp, h2 = 2 * half + i // 2, i % 2
                    last = pe.matmul(dst[0:AUG, i * P:(i + 1) * P], w_qk[:, hp, h2, 0:AUG],
                                     Bt[:, hp, :, h2, :], start=True, stop=True)
                last.then_inc(S["t_done"], 1)

            def slice_values(p, j):
                pe.wait_ge(S["t_saved0"], nth(p))
                pe.wait_ge(S["bt_saved0"], nth(p))
                pe.wait_ge(S["bt_saved1"], nth(p))
                for b in range(2):
                    for hp in range(4):
                        last = pe.matmul(pF[:, b, hp * P:(hp + 1) * P], Bt[:, hp, b, :, :].rearrange("p h g -> p (h g)"),
                                         w_vo[:, 2 * hp:2 * hp + 2, :].rearrange("p h c -> p (h c)"),
                                         start=True, stop=True)
                last.then_inc(S["v_done"], 1)

            def slice_scores(p, j):
                pe.wait_ge(S["t_saved0"], nth(p))
                pe.wait_ge(S["t_saved1"], nth(p))
                for h in range(NH):
                    for b in range(2):
                        last = pe.matmul(pF2[64 * b:64 * b + 64, h * G:(h + 1) * G],
                                         T[:, h, 64 * b:64 * b + 64], Bt[:, h // 2, b, h % 2, :],
                                         start=True, stop=True)
                last.then_inc(S["a_done"], 1)

            def weights_times_scores(p, j):
                pe.wait_ge(S["v_saved0"], nth(p))
                pe.wait_ge(S["v_saved1"], nth(p))
                pe.wait_ge(S["an_done"], nth(p))
                pe.wait_ge(S["wt_saved"], nth(p, 2, 2))
                for h in range(NH):
                    rows = slice(64 * (h % 2), 64 * (h % 2) + 64)
                    last = pe.matmul(pF[rows, 0, (h // 2) * P:(h // 2 + 1) * P], An[:, h, :], WT[:, h, :],
                                     start=True, stop=True)
                last.then_inc(S["m_done"], 1)

            def project(p, j):
                pe.wait_ge(S["a_shifted"], nth(p))
                pe.wait_ge(S["m_saved"], nth(p))
                pe.wait_ge(S["v_saved0"], nth(p))
                pe.wait_ge(S["v_saved1"], nth(p))
                for b in range(2):
                    for hp in range(4):
                        last = pe.matmul(pF2[64 * b:64 * b + 64, 0:D], M[:, hp, 64 * b:64 * b + 64],
                                         V[:, b, hp, :], start=(hp == 0), stop=(hp == 3))
                last.then_inc(S["o_done"], 1)

            def steps(do):
                do(1, weighted_sum, 0); do(3, project); do(1, transpose_x, 7); do(0, query)
                do(1, weighted_sum, 1); do(1, weighted_sum, 2); do(2, slice_sums); do(0, keys_for_query)
                do(0, key_bias); do(2, transpose_w, 0); do(1, transpose_y); do(2, transpose_b, 0)
                do(2, transpose_w, 1); do(0, scores, 0); do(1, values); do(0, scores, 1); do(2, transpose_b, 1)
                do(2, slice_keys, 0); do(2, slice_keys, 1); do(1, tokens); do(2, slice_values)
                do(2, slice_scores); do(0, transpose_x, 0); do(1, transpose_xn); do(0, transpose_x, 1)
                do(1, recur, 0); do(1, recur, 1); do(0, transpose_x, 2); do(1, transpose_h)
                do(0, transpose_x, 3); do(0, transpose_x, 4); do(2, weights_times_scores)
                do(0, transpose_p, 0); do(0, transpose_p, 1); do(1, transpose_x2); do(0, transpose_x, 5)
                do(0, transpose_x, 6); do(1, logits)

            run_slots(pe, steps, prepare_slices)

        @block.scalar
        def _(act):
            act.wait_ge(S["tok_zeroed"], 1)
            for b in range(2):
                rows = slice(64 * b, 64 * b + 64)
                act.dma_start(wq_bd[rows, rows], tWq[:, :]).then_inc(S["tok_in"], 16)
                act.dma_start(wk_bd[rows, rows], tWk[:, :]).then_inc(S["tok_in"], 16)
                act.dma_start(wv_bd[rows, rows], tWv[:, :]).then_inc(S["tok_in"], 16)
                act.dma_start(wo2[:, rows], tWo[:, :]).then_inc(S["tok_in"], 16)
                act.dma_start(bq_col[rows, :], tbq.unsqueeze(1)).then_inc(S["tok_in"], 16)
                act.dma_start(bk_col[rows, :], tbk.unsqueeze(1)).then_inc(S["tok_in"], 16)
                act.dma_start(bv_col[rows, :], tbv.unsqueeze(1)).then_inc(S["tok_in"], 16)
            act.dma_start(wr2[:, 0:64], W_ih[:, :]).then_inc(S["tok_in"], 16)
            act.dma_start(wr2[:, 64:128], W_hh[:, :]).then_inc(S["tok_in"], 16)
            act.dma_start(rnn_b2[64:128, 0:1], b_ih.unsqueeze(1)).then_inc(S["tok_in"], 16)
            act.dma_start(rnn_b2[64:128, 1:2], b_hh.unsqueeze(1)).then_inc(S["tok_in"], 16)
            act.dma_start(bo_row[:, :], tbo.partition_broadcast(P)).then_inc(S["tok_in"], 16)

            def by_window(p, j, i):
                if i % 4 == 0:
                    act.wait_ge(S[("x_in0", "x_in1")[i // 4]], nth(p, 16, 16))
                if i == 0 and has(p - 2):
                    act.wait_ge(S["xt_done"], nth(p - 2, 8, 8))
                w = Xw[:, j, 8 * (i // 2):8 * (i // 2) + 8, 64 * (i % 2):64 * (i % 2) + 64]
                act.activation(w.rearrange("p h (r c) -> p h r c", c=8),
                               X[:, j, i * 512:(i + 1) * 512].rearrange("p (r h c) -> p h r c", r=8, h=8),
                               ACT.Copy).then_inc(S["windowed"], 1)

            def save_xt(p, j, i):
                act.wait_ge(S["xt_done"], nth(p, i + 1, 8))
                if i in (0, 3, 6) and has(p - 1):
                    act.wait_ge(S["y_done"], nth(p - 1, i // 3 + 1, 3))
                act.activation(XT[:, 4 * i:4 * i + 4, 0:P], pX[i % 2][:, :, :], ACT.Copy)\
                    .then_inc(S["xt_saved"], 1)

            def save_qp(p, j):
                if isinstance(p, int) and p == 0:
                    act.wait_ge(S["tok_in"], 16 * TOK_LOADS)
                    act.wait_ge(S["consts"], CONSTS)
                    act.wait_ge(S["rnn_b_done"], 1)
                    act.wait_ge(S["mask_done"], 6)
                    act.wait_ge(S["ones_set"], 1)
                act.wait_ge(S["qp_done"], nth(p))
                if has(p - 1):
                    act.wait_ge(S["c_done"], nth(p - 1))
                if has(p - 1):
                    act.wait_ge(S["qpm_done"], nth(p - 1))
                act.activation(qp[:, :], pG[:, 0:N], ACT.Identity, bias=bq_col[:, :], scale=1.0 / L)\
                    .then_inc(S["qp_saved"], 1)

            def save_u(p, j):
                act.wait_ge(S["u_done"], nth(p))
                if has(p - 1):
                    act.wait_ge(S["s_done"], nth(p - 1, 2, 2))
                for b in range(2):
                    rows = slice(64 * b, 64 * b + 64)
                    act.activation(U[rows, :, b, :], pK[0][rows, :].rearrange("p (w h) -> p w h", h=NH),
                                   ACT.Copy, scale=DH ** -0.5).then_inc(S["u_saved"], 1)

            def half_scores(p, j, half):
                act.wait_ge(S["s_done"], nth(p, half + 1, 2))
                if has(p - 1):
                    act.wait_ge(S["s_whole"], nth(p - 1, half + 1, 2))
                act.activation(St[:, 4 * half:4 * half + 4, :],
                               pX[half][:, :, 0:L],
                               ACT.Copy, scale=mask_gw[:, 0:1]).then_inc(S["s_half"], 1)

            def exp_p(p, j):
                act.wait_ge(S["s_shifted"], nth(p))
                act.activation(Sc[:, :, :], Sc[:, :, :], ACT.Exp).then_inc(S["p_exp"], 1)

            def save_pt(p, j):
                act.wait_ge(S["pt_done"], nth(p, 1, 2))
                if has(p - 1):
                    act.wait_ge(S["y_done"], nth(p - 1, 3, 3))
                act.activation(PT[:, 0:4, :].rearrange("p g r -> p (g r)"), pK[0][:, :], ACT.Copy)\
                    .then_inc(S["pt_saved0"], 1)

            def half_y(p, j, r):
                g0, g1 = Y_ROUNDS[r]
                act.wait_ge(S["y_done"], nth(p, r + 1, 3))
                if has(p - 1):
                    act.wait_ge(S["y_whole"], nth(p - 1, r + 1, 3))
                src = pK[r % 2][:, 0:(g1 - g0) * XW].rearrange("p (g c) -> p g c", c=XW)
                act.activation(Yt[:, g0:g1, :], src[:, :, 0:D], ACT.Copy, scale=mask_b[:, 0:1])\
                    .then_inc(S["y_half"], 1)

            def save_yt(p, j):
                act.wait_ge(S["yt_done"], nth(p))
                if has(p - 1):
                    act.wait_ge(S["z_done"], nth(p - 1))
                act.activation(YT[:, :], pK[1][:, :], ACT.Copy).then_inc(S["yt_saved"], 1)

            def save_xnt(p, j):
                act.wait_ge(S["xnt_done"], nth(p))
                if has(p - 1):
                    act.wait_ge(S["rnn_done"], nth(p - 1, 2, 2))
                for i in range(2):
                    act.activation(RX[0:D, (2 * j + i - 1) % 4, :], pG[0:D, i * N:(i + 1) * N], ACT.Copy)\
                        .then_inc(S["xnt_saved"], 1)

            def state(p, j, i):
                act.wait_ge(S["rnn_done"], nth(p, i + 1, 2))
                if i == 0 and has(p - 2):
                    act.wait_ge(S["h2t_done"], nth(p - 2))
                act.activation(RX[64:128, 2 * j + i, :], pG[64:128, 0:N], ACT.Tanh,
                               bias=rnn_b[64:128, :]).then_inc(S["state_done"], 1)

            def save_x2t(p, j):
                act.wait_ge(S["x2t_done"], nth(p))
                if has(p - 1):
                    act.wait_ge(S["lg_done"], nth(p - 1))
                act.activation(X2T[0:D, :], pG[0:D, 0:P], ACT.Copy).then_inc(S["x2t_saved"], 1)

            def exp_w(p, j):
                act.wait_ge(S["l_shifted"], nth(p))
                act.activation(W[:, :, :], W[:, :, :], ACT.Exp).then_inc(S["w_exp"], 1)

            def save_wt(p, j, half):
                act.wait_ge(S["wt_done"], nth(p, half + 1, 2))
                if half == 0 and has(p - 1):
                    act.wait_ge(S["m_done"], nth(p - 1))
                act.activation(WT[:, 4 * half:4 * half + 4, :].rearrange("p h n -> p (h n)"),
                               pF[:, half, :], ACT.Copy).then_inc(S["wt_saved"], 1)

            def save_bt1(p, j):
                act.wait_ge(S["bt_done"], nth(p, 2, 2))
                if has(p - 1):
                    act.wait_ge(S["a_done"], nth(p - 1))
                if has(p - 1):
                    act.wait_ge(S["v_done"], nth(p - 1))
                act.activation(Bt[:, 2:4, :, :, :].rearrange("p a b h g -> p (a b h g)"), pF[0:AUG, 0, :],
                               ACT.Copy).then_inc(S["bt_saved1"], 1)

            def save_t0(p, j):
                act.wait_ge(S["t_done"], nth(p, 1, 2))
                if has(p - 1):
                    act.wait_ge(S["a_done"], nth(p - 1))
                act.activation(T[:, 0:4, :].rearrange("p h g -> p (h g)"), pF[0:AUG, 1, :], ACT.Copy)\
                    .then_inc(S["t_saved0"], 1)

            def save_v0(p, j):
                act.wait_ge(S["v_done"], nth(p))
                if has(p - 1):
                    act.wait_ge(S["o_done"], nth(p - 1))
                act.activation(V[0:64, :, :, :].rearrange("p b a c -> p (b a) c"),
                               pF[0:64, :, :].rearrange("p b (a h c) -> p (b a) h c", a=4, h=2)[:, :, 0, :],
                               ACT.Copy).then_inc(S["v_saved0"], 1)

            def exp_a(p, j):
                act.wait_ge(S["a_shifted"], nth(p))
                act.activation(A[:, :, :], A[:, :, :], ACT.Exp).then_inc(S["a_exp"], 1)

            def save_m(p, j):
                act.wait_ge(S["m_done"], nth(p))
                if has(p - 1):
                    act.wait_ge(S["o_done"], nth(p - 1))
                act.activation(M[:, :, :].rearrange("p a n -> p (a n)"), pF[:, 0, :], ACT.Copy)\
                    .then_inc(S["m_saved"], 1)

            def steps(do):
                do(3, save_bt1); do(3, save_t0); do(0, by_window, 0); do(0, by_window, 1); do(3, save_v0)
                do(0, by_window, 2); do(2, save_xnt); do(1, save_xt, 0); do(2, state, 0); do(1, save_xt, 1)
                do(3, exp_a); do(2, state, 1); do(1, exp_p); do(1, save_xt, 2); do(0, by_window, 3)
                do(1, save_xt, 3); do(0, by_window, 4); do(1, save_xt, 4); do(3, save_m); do(2, save_x2t)
                do(0, by_window, 5); do(1, save_pt); do(1, save_xt, 5); do(1, save_xt, 6); do(1, half_y, 0)
                do(2, exp_w); do(1, save_xt, 7); do(0, save_qp); do(1, half_y, 1); do(1, half_y, 2)
                do(0, by_window, 6); do(0, save_u); do(0, by_window, 7); do(2, save_wt, 0); do(1, save_yt)
                do(0, half_scores, 0); do(2, save_wt, 1); do(0, half_scores, 1)

            run_slots(act, steps)

        @block.vector
        def _(dve):
            for t in (wq_bd, wk_bd):
                dve.memset(t[:, :], 0.0)
            dve.memset(wv_bd[:, :], 0.0).then_inc(S["tok_zeroed"], 1)
            dve.memset(XT[:, :, P:XW], 1.0)
            dve.memset(X2T[D:AUG, :], 1.0)
            dve.memset(RX[64:128, 3, :], 0.0).then_inc(S["ones_set"], 1)
            dve.wait_ge(S["consts"], 1)
            iv = ident[:, :].rearrange("p (a w c) -> p w a c", a=4, w=2)
            dve.tensor_reduce(mask_gw[:, :], iv, AX.XY, ALU.add).then_inc(S["mask_done"], 1)
            iv = ident[:, :].rearrange("p (a b c) -> p b a c", a=8, b=2)
            dve.tensor_reduce(mask_b[:, :], iv, AX.XY, ALU.add).then_inc(S["mask_done"], 1)
            iv = ident[:, :].rearrange("p (w c) -> p w c", w=8)
            dve.tensor_reduce(mask_w[:, :], iv, AX.X, ALU.add).then_inc(S["mask_done"], 1)
            iv = ident[:, :].rearrange("p (b c) -> p b c", b=16)
            dve.tensor_reduce(mask_bh[:, :], iv, AX.X, ALU.add).then_inc(S["mask_done"], 1)
            iv = ident[:, :].rearrange("p (b c) -> p b c", b=2)
            dve.tensor_reduce(mask_img[:, :], iv, AX.X, ALU.add).then_inc(S["mask_done"], 1)
            iv = ident[:, :].rearrange("p (b h c) -> p h b c", b=2, h=NH)
            dve.tensor_reduce(mask_h[:, :], iv, AX.XY, ALU.add).then_inc(S["mask_done"], 1)
            for b in range(2):
                rows = slice(64 * b, 64 * b + 64)
                last = dve.tensor_scalar(id_mean[rows, :], ident[rows, rows], 1.0 / L, None, ALU.mult)
            last.then_inc(S["id_mean_done"], 1)
            def prepare_tokens():
                dve.wait_ge(S["tok_in"], 16 * TOK_LOADS)
                dve.tensor_tensor(rnn_b[64:128, :], rnn_b2[64:128, 0:1], rnn_b2[64:128, 1:2], ALU.add)\
                    .then_inc(S["rnn_b_done"], 1)
                dve.wait_ge(S["mask_done"], 6)
                dve.tensor_scalar(bk_rep[:, :].rearrange("p (w m) -> p w m", w=8),
                                  mask_bh[:, :].unsqueeze(1).to_broadcast([P, 8, 16]), bk_col[:, :],
                                  DH ** -0.5, ALU.mult, ALU.mult).then_inc(S["bk_rep_done"], 1)
                dve.wait_ge(S["tokT_done"], 1)
                dve.tensor_copy(tokT[:, :], pK[0][:, 0:384]).then_inc(S["tokT_saved"], 1)
                for b in range(2):
                    dve.tensor_copy(X2B[:, b, D:66], mask_img[:, b:b + 1].to_broadcast([P, 2])).then_inc(S["x2b_ones"], 1)
                dve.wait_ge(S["consts"], CONSTS)

            def prepare_slices():
                dve.wait_ge(S["ffn_in"], 16 * FFN_LOADS)
                dve.tensor_scalar(rtemp[:, :], temp[:, :], 0.1, 5.0, ALU.max, ALU.min)\
                    .then_inc(S["temp_done"], 1)
                dve.wait_ge(S["temp_done"], 1)
                dve.reciprocal(temp[:, :], rtemp[:, :]).then_inc(S["temp_done"], 1)
                dve.wait_ge(S["prep_pe"], 1)
                v66 = lambda t: t.rearrange("p (a c) -> p a c", c=66)[:, :, 0:AUG]
                dve.tensor_copy(wfxT[:, :, 0:AUG], v66(pF[:, 0, 0:264]))
                dve.tensor_copy(wxT[:, :, 0:AUG], v66(pF[:, 1, 0:264]))
                dve.memset(wfxT[:, :, AUG:66], 0.0)
                dve.tensor_copy(fqkvT[:, :, :].rearrange("p a c -> p (a c)"), pF2[:, 0:384])\
                    .then_inc(S["prep_dve"], 1)
                dve.wait_ge(S["prep_pe"], 2)
                dve.tensor_copy(mqk[:, :], pF2[:, 0:P])
                for h2 in range(2):
                    rows = slice(64 * h2, 64 * h2 + 64)
                    dve.tensor_copy(f_bd[rows, :, h2, :],
                                    pF[rows, 0, 0:4 * D].rearrange("p (a c) -> p a c", c=D))
                dve.tensor_copy(w_logit[:, :, :].rearrange("p h g -> p (h g)"), pF[0:AUG, 1, :])\
                    .then_inc(S["temp_done"], 1)
                dve.wait_ge(S["temp_done"], 3)
                dve.tensor_tensor(w_logit[D:AUG, :, :], w_logit[D:AUG, :, :],
                                  bsl[D:AUG, :].unsqueeze(1).to_broadcast([1, NH, G]), ALU.add)\
                    .then_inc(S["temp_done"], 1)
                dve.wait_ge(S["temp_done"], 4)
                dve.tensor_tensor(w_logit[:, :, :], w_logit[:, :, :],
                                  temp[:, :].unsqueeze(2).to_broadcast([AUG, NH, G]), ALU.mult)\
                    .then_inc(S["prep_dve"], 1)
                dve.wait_ge(S["prep_pe"], 3)
                for h2 in range(2):
                    rows = slice(64 * h2, 64 * h2 + 64)
                    dve.tensor_scalar(e_bd[rows, :, h2, :],
                                      pF2[rows, 0:264].rearrange("p (a c) -> p a c", c=66),
                                      float(D) ** -0.5, None, ALU.mult)
                dve.tensor_copy(w_vo[:, :, :].rearrange("p h c -> p (h c)"), pF[0:AUG, 0, :])\
                    .then_inc(S["prep_dve"], 1)
                dve.wait_ge(S["prep_pe"], 4)
                for a in range(2):
                    last = dve.tensor_copy(w_qk[:, 2 * a:2 * a + 2, :, :].rearrange("p a h c -> p (a h c)"),
                                           pF[0:AUG, a, 0:264])
                last.then_inc(S["prep_dve"], 1)

            def window_sums(p, j, i):
                if i == 0:
                    dve.wait_ge(S["x_in0"], nth(p, 16, 16))
                    if has(p - 1):
                        dve.wait_ge(S["qp_done"], nth(p - 1))
                        dve.wait_ge(S["qtok_done"], nth(p - 1, 2, 2))
                if i == 4:
                    dve.wait_ge(S["x_in1"], nth(p, 16, 16))
                src = X[:, j, i * 512:(i + 1) * 512].rearrange("p (r h c) -> p h r c", r=8, h=8)
                dve.tensor_reduce(qsum[:, i // 2, :, i % 2], src, AX.XY, ALU.add).then_inc(S["qsum_done"], 1)
                if isinstance(p, int) and p == 0 and i == 7:
                    prepare_tokens()

            def own_bias(p, j):
                dve.wait_ge(S["c_done"], nth(p))
                if has(p - 1):
                    dve.wait_ge(S["kb_done"], nth(p - 1))
                dve.tensor_tensor(kbw[:, :, :], pG[:, 0:N].rearrange("p (g w) -> p g w", w=8),
                                  mask_w[:, :].unsqueeze(1).to_broadcast([P, GROUPS, 8]), ALU.mult)\
                    .then_inc(S["c_masked"], 1)

            def sum_bias(p, j):
                dve.wait_ge(S["c_masked"], nth(p))
                if has(p - 1):
                    dve.wait_ge(S["shift_done"], nth(p - 1))
                dve.tensor_reduce(kb[:, :], kbw[:, :, :], AX.X, ALU.add).then_inc(S["kb_done"], 1)

            def whole_scores(p, j, half):
                dve.wait_ge(S["s_half"], nth(p, half + 1, 2))
                if has(p - 1):
                    dve.wait_ge(S["p_masked"], nth(p - 1, 2, 2))
                src = pX[half][:, :, L:2 * L]
                rows = slice(4 * half, 4 * half + 4)
                dve.scalar_tensor_tensor(out=Sc[:, rows, :], in0=src, scalar=mask_gw[:, 1:2],
                                         in1=St[:, rows, :], op0=ALU.mult, op1=ALU.add)\
                    .then_inc(S["s_whole"], 1)

            def score_maxima(p, j):
                dve.wait_ge(S["s_whole"], nth(p, 2, 2))
                dve.tensor_reduce(Smax[:, :], Sc[:, :, :], AX.X, ALU.max).then_inc(S["smax_done"], 1)

            def full_maxima(p, j):
                dve.wait_ge(S["smax_done"], nth(p))
                dve.wait_ge(S["kb_done"], nth(p))
                dve.tensor_tensor(full_max[:, :], Smax[:, :], kb[:, :], ALU.add).then_inc(S["full_max_done"], 1)

            def score_shifts(p, j):
                dve.wait_ge(S["full_max_done"], nth(p))
                dve.tensor_tensor(shift[:, :], full_max[:, :], kb[:, :], ALU.subtract).then_inc(S["shift_done"], 1)

            def shift_scores(p, j):
                dve.wait_ge(S["shift_done"], nth(p))
                dve.tensor_tensor(Sc[:, :, :], Sc[:, :, :],
                                  shift[:, :].unsqueeze(2).to_broadcast([P, GROUPS, L]), ALU.subtract)\
                    .then_inc(S["s_shifted"], 1)

            def save_pt(p, j):
                dve.wait_ge(S["pt_done"], nth(p, 2, 2))
                if has(p - 1):
                    dve.wait_ge(S["y_done"], nth(p - 1, 3, 3))
                dve.tensor_copy(PT[:, 4:8, :].rearrange("p g r -> p (g r)"), pK[1][:, :])\
                    .then_inc(S["pt_saved1"], 1)

            def whole_y(p, j, r):
                g0, g1 = Y_ROUNDS[r]
                dve.wait_ge(S["y_half"], nth(p, r + 1, 3))
                if has(p - 1):
                    dve.wait_ge(S["y_scaled"], nth(p - 1, r + 1, 3))
                src = pK[r % 2][:, 0:(g1 - g0) * XW].rearrange("p (g c) -> p g c", c=XW)
                dve.scalar_tensor_tensor(out=Ye[:, g0:g1, :], in0=src[:, :, D:2 * D], scalar=mask_b[:, 1:2],
                                         in1=Yt[:, g0:g1, :], op0=ALU.mult, op1=ALU.add)\
                    .then_inc(S["y_whole"], 1)
                dve.reciprocal(rsum[:, g0:g1], src[:, :, P]).then_inc(S["y_recip"], 1)

            def own_heads(p, j):
                dve.wait_ge(S["z_done"], nth(p))
                if has(p - 1):
                    dve.wait_ge(S["ctx_done"], nth(p - 1))
                dve.tensor_tensor(Zm[:, :, :], pK[1][:, :].rearrange("p (w h) -> p w h", h=NH),
                                  mask_h[:, :].unsqueeze(1).to_broadcast([P, N, NH]), ALU.mult)\
                    .then_inc(S["z_masked"], 1)

            def sum_heads(p, j):
                dve.wait_ge(S["z_masked"], nth(p))
                if has(p - 1):
                    dve.wait_ge(S["ctx_placed"], nth(p - 1, 4, 4))
                dve.tensor_reduce(ctxs[:, :], Zm[:, :, :], AX.X, ALU.add).then_inc(S["ctx_done"], 1)

            def place_context(p, j):
                dve.wait_ge(S["ctx_done"], nth(p))
                if has(p - 1):
                    dve.wait_ge(S["tok_done"], nth(p - 1))
                src = ctxs[:, :].rearrange("p (a h w b) -> p b a w h", a=4, h=4, w=2)
                for q in range(2):
                    rows = slice(64 * q, 64 * q + 64)
                    for b in range(2):
                        dve.tensor_scalar(ctxm[rows, b, :, :, q, :], src[rows, b], bv_col[rows, :], None,
                                          ALU.add).then_inc(S["ctx_placed"], 1)

            def residual(p, j):
                dve.wait_ge(S["tok_done"], nth(p))
                if has(p - 1):
                    dve.wait_ge(S["h2_done"], nth(p - 1))
                dve.tensor_tensor(H[:, :], pG[:, 0:D], bo_row[:, :], ALU.add).then_inc(S["h_done"], 1)

            def residual2(p, j):
                dve.wait_ge(S["h2t_done"], nth(p))
                if has(p - 1):
                    dve.wait_ge(S["r_done"], nth(p - 1))
                    dve.wait_ge(S["x2n_done"], nth(p - 1))
                dve.tensor_tensor(H2[:, :], pG[:, 0:D], H[:, :], ALU.add).then_inc(S["h2_done"], 1)

            def norm_stats(p, j, k):
                dve.wait_ge(S[("h_done", "h2_done")[k]], nth(p))
                dve.bn_stats(stats[:, k, :], (H, H2)[k][:, :]).then_inc(S[f"stats_done{k}"], 1)

            def norm_mean(p, j, k):
                dve.wait_ge(S[f"stats_done{k}"], nth(p))
                if has(p - 1):
                    dve.wait_ge(S[("xn_done", "x2n_done")[k]], nth(p - 1))
                dve.sem_inc(S["passed"], 1)
                dve.bn_aggr(mv[:, k, :], stats[:, k, :]).then_inc(S[f"mv_done{k}"], 1)

            def norm_eps(p, j, k):
                dve.wait_ge(S[f"mv_done{k}"], nth(p))
                dve.tensor_scalar(vpe[:, k:k + 1], mv[:, k, 1:2], EPS, None, ALU.add)\
                    .then_inc(S[f"vpe_done{k}"], 1)

            def normed(p, j):
                dve.wait_ge(S["rstd_done0"], nth(p))
                if has(p - 1):
                    dve.wait_ge(S["xnt_done"], nth(p - 1))
                dve.tensor_scalar(xn[:, :], H[:, :], mv[:, 0, 0:1], rstd[:, 0:1], ALU.subtract, ALU.mult)\
                    .then_inc(S["xn_done"], 1)

            def normed2(p, j):
                dve.wait_ge(S["rstd_done1"], nth(p))
                if has(p - 1):
                    dve.wait_ge(S["x2t_done"], nth(p - 1))
                    dve.wait_ge(S["x2b_done"], nth(p - 1, 2, 2))
                dve.tensor_scalar(x2n[:, :], H2[:, :], mv[:, 1, 0:1], rstd[:, 1:2], ALU.subtract, ALU.mult)\
                    .then_inc(S["x2n_done"], 1)

            def logit_maxima(p, j):
                dve.wait_ge(S["lg_done"], nth(p))
                dve.tensor_reduce(lmax[:, :], pF[:, 0, :].rearrange("p (h g) -> p h g", g=G), AX.X, ALU.max)\
                    .then_inc(S["lmax_done"], 1)

            def shift_logits(p, j):
                dve.wait_ge(S["lmax_done"], nth(p))
                if has(p - 1):
                    dve.wait_ge(S["wn_done"], nth(p - 1))
                dve.tensor_tensor(W[:, :, :], pF[:, 0, :].rearrange("p (h g) -> p h g", g=G),
                                  lmax[:, :].unsqueeze(2).to_broadcast([P, NH, G]),
                                  ALU.subtract).then_inc(S["l_shifted"], 1)

            def weight_sums(p, j):
                dve.wait_ge(S["w_exp"], nth(p))
                dve.tensor_reduce(wsum[:, :], W[:, :, :], AX.X, ALU.add).then_inc(S["wsum_done"], 1)

            def weight_scales(p, j):
                dve.wait_ge(S["wsum_done"], nth(p))
                dve.reciprocal(wrec[:, :], wsum[:, :]).then_inc(S["wrec_done"], 1)

            def slice_weights(p, j):
                dve.wait_ge(S["wrec_done"], nth(p))
                if has(p - 1):
                    dve.wait_ge(S["b_done"], nth(p - 1))
                    dve.wait_ge(S["wx_done"], nth(p - 1, 2, 2))
                dve.tensor_tensor(Wn[:, :, :], W[:, :, :], wrec[:, :].unsqueeze(2).to_broadcast([P, NH, G]),
                                  ALU.mult).then_inc(S["wn_done"], 1)

            def slice_sizes(p, j):
                dve.wait_ge(S["b_done"], nth(p))
                for i, src in enumerate((pF[:, 1, :], pF2)):
                    dve.tensor_scalar(bden[:, 2 * i:2 * i + 2, :],
                                      src[:, 0:264].rearrange("p (a b c) -> p a b c", a=2, b=2)[:, :, :, D],
                                      1e-5, None, ALU.add).then_inc(S["bden_done"], 1)

            def slice_scales(p, j):
                dve.wait_ge(S["bden_done"], nth(p, 2, 2))
                dve.reciprocal(brec[:, :, :], bden[:, :, :]).then_inc(S["brec_done"], 1)

            def slice_means(p, j):
                dve.wait_ge(S["brec_done"], nth(p))
                if has(p - 1):
                    dve.wait_ge(S["bt_done"], nth(p - 1, 2, 2))
                for i, src in enumerate((pF[:, 1, :], pF2)):
                    dve.tensor_tensor(Bn[:, 2 * i:2 * i + 2, :, :],
                                      src[:, 0:264].rearrange("p (a b c) -> p a b c", a=2, b=2),
                                      brec[:, 2 * i:2 * i + 2, :].unsqueeze(3).to_broadcast([P, 2, 2, 66]),
                                      ALU.mult).then_inc(S["bn_done"], 1)

            def save_bt0(p, j):
                dve.wait_ge(S["bt_done"], nth(p, 1, 2))
                if has(p - 1):
                    dve.wait_ge(S["a_done"], nth(p - 1))
                if has(p - 1):
                    dve.wait_ge(S["v_done"], nth(p - 1))
                dve.tensor_copy(Bt[:, 0:2, :, :, :].rearrange("p a b h g -> p (a b h g)"), pF2[0:AUG, :])\
                    .then_inc(S["bt_saved0"], 1)

            def save_t1(p, j):
                dve.wait_ge(S["t_done"], nth(p, 2, 2))
                if has(p - 1):
                    dve.wait_ge(S["a_done"], nth(p - 1))
                dve.tensor_copy(T[:, 4:8, :].rearrange("p h g -> p (h g)"), pF2[0:AUG, :])\
                    .then_inc(S["t_saved1"], 1)

            def save_v1(p, j):
                dve.wait_ge(S["v_done"], nth(p))
                if has(p - 1):
                    dve.wait_ge(S["o_done"], nth(p - 1))
                dve.tensor_copy(V[64:128, :, :, :].rearrange("p b a c -> p (b a) c"),
                                pF[64:128, :, :].rearrange("p b (a h c) -> p (b a) h c", a=4, h=2)[:, :, 1, :])\
                    .then_inc(S["v_saved1"], 1)

            def slice_maxima(p, j):
                dve.wait_ge(S["a_done"], nth(p))
                dve.tensor_reduce(amax[:, :], pF2[:, :].rearrange("p (h g) -> p h g", g=G), AX.X, ALU.max)\
                    .then_inc(S["amax_done"], 1)

            def shift_slices(p, j):
                dve.wait_ge(S["amax_done"], nth(p))
                if has(p - 1):
                    dve.wait_ge(S["an_done"], nth(p - 1))
                dve.tensor_tensor(A[:, :, :], pF2[:, :].rearrange("p (h g) -> p h g", g=G),
                                  amax[:, :].unsqueeze(2).to_broadcast([P, NH, G]),
                                  ALU.subtract).then_inc(S["a_shifted"], 1)

            def slice_exp_sums(p, j):
                dve.wait_ge(S["a_exp"], nth(p))
                dve.tensor_reduce(asum[:, :], A[:, :, :], AX.X, ALU.add).then_inc(S["asum_done"], 1)

            def slice_exp_scales(p, j):
                dve.wait_ge(S["asum_done"], nth(p))
                dve.reciprocal(arec[:, :], asum[:, :]).then_inc(S["arec_done"], 1)

            def slice_attention(p, j):
                dve.wait_ge(S["arec_done"], nth(p))
                if has(p - 1):
                    dve.wait_ge(S["m_done"], nth(p - 1))
                dve.tensor_tensor(An[:, :, :], A[:, :, :], arec[:, :].unsqueeze(2).to_broadcast([P, NH, G]),
                                  ALU.mult).then_inc(S["an_done"], 1)

            def add_out(p, j):
                dve.wait_ge(S["o_done"], nth(p))
                dve.wait_ge(S["r_done"], nth(p))
                dve.wait_ge(S["stored"], 16 * p + 16)
                dve.tensor_tensor(O[:, :], pF2[:, 0:D], R[:, :], ALU.add).then_inc(S["o_added"], 1)

            def steps(do):
                do(0, window_sums, 0); do(3, slice_exp_sums); do(2, residual2); do(3, slice_exp_scales)
                do(2, norm_stats, 1); do(3, slice_attention); do(2, norm_mean, 1); do(2, norm_eps, 1)
                do(0, window_sums, 1); do(0, window_sums, 2); do(2, normed2); do(0, window_sums, 3)
                do(0, window_sums, 4); do(0, window_sums, 5); do(0, window_sums, 6); do(1, save_pt)
                do(2, logit_maxima); do(0, window_sums, 7); do(2, shift_logits); do(1, whole_y, 0)
                do(2, weight_sums); do(3, add_out); do(2, weight_scales); do(2, slice_weights)
                do(1, whole_y, 1); do(1, whole_y, 2); do(2, slice_sizes); do(2, slice_scales)
                do(2, slice_means); do(0, own_bias); do(2, save_bt0); do(0, whole_scores, 0); do(1, own_heads)
                do(1, sum_heads); do(1, place_context); do(0, whole_scores, 1); do(2, save_t1); do(1, residual)
                do(1, norm_stats, 0); do(1, norm_mean, 0); do(1, norm_eps, 0); do(0, sum_bias)
                do(0, score_maxima); do(2, save_v1); do(1, normed); do(0, full_maxima); do(2, slice_maxima)
                do(2, shift_slices); do(0, score_shifts); do(0, shift_scores)

            run_slots(dve, steps, prepare_slices)



_INS = ["x", "L0_tok_Wq", "L0_tok_bq", "L0_tok_Wk", "L0_tok_bk", "L0_tok_Wv", "L0_tok_bv", "L0_tok_Wo",
        "L0_tok_bo", "L0_attn_W_ih", "L0_attn_W_hh", "L0_attn_b_ih", "L0_attn_b_hh", "L0_ffn_W_fx",
        "L0_ffn_b_fx", "L0_ffn_W_x", "L0_ffn_b_x", "L0_ffn_W_slice", "L0_ffn_b_slice", "L0_ffn_W_q",
        "L0_ffn_W_k", "L0_ffn_W_v", "L0_ffn_W_out", "L0_ffn_b_out", "L0_ffn_temperature"]


def kernel(**inputs):
    import numpy as _np
    import concourse.bacc as _bacc
    from concourse import mybir as _mybir
    from concourse.bass_utils import run_bass_kernel_spmd as _run

    nc = _bacc.Bacc("TRN2", target_bir_lowering=False, num_devices=1)
    arrays, args = {}, []
    for name in _INS:
        a = _np.ascontiguousarray(inputs[name])
        arrays[f"in_{name}"] = a
        args.append(nc.dram_tensor(f"in_{name}", a.shape, _mybir.dt.from_np(a.dtype), kind="ExternalInput").ap())
    out = nc.dram_tensor("out_0", (16, 64, 64), _mybir.dt.float32, kind="ExternalOutput").ap()
    vit_tower_kernel(nc, *args, out)
    r = _run(nc, [arrays], core_ids=[0])
    return r.results[0]["out_0"]
```

```python
import concourse.bass as bass
from concourse import mybir
from contextlib import ExitStack



def vit_tower_kernel(nc, x, tWq, tbq, tWk, tbk, tWv, tbv, tWo, tbo, W_ih, W_hh, b_ih, b_hh,
                     W_fx, b_fx, W_x, b_x, W_slice, b_slice, W_q, W_k, W_v, W_out, b_out,
                     temperature, out):
    fp32 = mybir.dt.float32
    ALU = mybir.AluOpType
    ACT = mybir.ActivationFunctionType
    AX = mybir.AxisListType

    P = 128
    B, D, HT, WD = x.shape
    GS = 8
    NH = 8
    DH = D // NH
    L = GS * GS
    N = (HT // GS) * (WD // GS)
    PIX = HT * WD
    PAIRS = B // 2
    GROUPS = 8
    CHUNKS = 32
    G = 64
    INNER = NH * D
    XW = P + 2
    AUG = D + 1
    EPS = 1e-5
    Y_ROUNDS = ((0, 3), (3, 6), (6, 8))

    x_v = x.rearrange("(t b) d w h -> t (b d) (w h)", b=2)
    out_v = out.rearrange("(t b) n c -> t (b n) c", b=2)

    ctx = ExitStack()
    with ctx:
        def sb(name, shape):
            return ctx.enter_context(nc.sbuf_tensor(name, shape, fp32))

        def bank(name, shape):
            return ctx.enter_context(nc.psum_tensor(name, shape, fp32))

        ident = sb("ident", [P, P])
        ones = sb("ones", [P, P])
        mask_gw = sb("mask_gw", [P, 2])
        mask_w = sb("mask_w", [P, 8])
        mask_bh = sb("mask_bh", [P, 16])
        mask_b = sb("mask_b", [P, 2])
        mask_img = sb("mask_img", [P, 2])
        mask_h = sb("mask_h", [P, NH])
        id_mean = sb("id_mean", [P, D])
        wq_bd = sb("wq_bd", [P, P])
        wk_bd = sb("wk_bd", [P, P])
        wv_bd = sb("wv_bd", [P, P])
        wo2 = sb("wo2", [D, P])
        wr2 = sb("wr2", [D, P])
        tokT = sb("tokT", [P, 384])
        wqT, wvT = tokT[:, 0:P], tokT[:, P:2 * P]
        woT, wrT = tokT[:, 256:320], tokT[:, 320:384]
        bq_col = sb("bq_col", [P, 1])
        bk_col = sb("bk_col", [P, 1])
        bk_rep = sb("bk_rep", [P, P])
        bv_col = sb("bv_col", [P, 1])
        bo_row = sb("bo_row", [P, D])
        rnn_b2 = sb("rnn_b2", [P, 2])
        rnn_b = sb("rnn_b", [P, 1])
        wfx = sb("wfx", [AUG, INNER])
        wxa = sb("wxa", [AUG, INNER])
        wsl_bd = sb("wsl_bd", [P, P])
        fq_bd = sb("fq_bd", [P, P])
        fk_bd = sb("fk_bd", [P, P])
        fv_bd = sb("fv_bd", [P, P])
        wout = sb("wout", [P, 4, D])
        bout_row = sb("bout_row", [P, D])
        bsl = sb("bsl", [AUG, G])
        temp = sb("temp", [AUG, NH])
        rtemp = sb("rtemp", [AUG, NH])
        wfxT = sb("wfxT", [P, 4, 66])
        wxT = sb("wxT", [P, 4, 66])
        fqkvT = sb("fqkvT", [P, 3, P])
        mqk = sb("mqk", [P, P])
        e_bd = sb("e_bd", [P, 4, 2, 66])
        f_bd = sb("f_bd", [P, 4, 2, D])
        w_logit = sb("w_logit", [AUG, NH, G])
        w_qk = sb("w_qk", [AUG, 4, 2, 66])
        w_vo = sb("w_vo", [AUG, NH, D])

        X = sb("X", [P, 2, PIX])
        Xw = sb("Xw", [P, 2, CHUNKS, P])
        XT = sb("XT", [P, CHUNKS, XW])
        qsum = sb("qsum", [P, 4, 8, 2])
        qtok = sb("qtok", [P, 2, 2, 4, 2, 8])
        qp = sb("qp", [P, N])
        qpm = sb("qpm", [P, N, NH])
        U = sb("U", [P, N, 2, NH])
        St = sb("St", [P, GROUPS, L])
        Sc = sb("Sc", [P, GROUPS, L])
        Smax = sb("Smax", [P, GROUPS])
        full_max = sb("full_max", [P, GROUPS])
        shift = sb("shift", [P, GROUPS])
        kbw = sb("kbw", [P, GROUPS, 8])
        kb = sb("kb", [P, GROUPS])
        Pm = sb("Pm", [P, GROUPS, 2, L])
        PT = sb("PT", [P, GROUPS, P])
        Yt = sb("Yt", [P, GROUPS, D])
        Ye = sb("Ye", [P, GROUPS, D])
        Yn = sb("Yn", [P, GROUPS, D])
        rsum = sb("rsum", [P, GROUPS])
        YT = sb("YT", [P, 4 * P])
        Zm = sb("Zm", [P, N, NH])
        ctxs = sb("ctxs", [P, N])
        ctxm = sb("ctxm", [P, 2, 4, 2, 2, 4])
        H = sb("H", [P, D])
        H2 = sb("H2", [P, D])
        stats = sb("stats", [P, 2, 6])
        mv = sb("mv", [P, 2, 2])
        vpe = sb("vpe", [P, 2])
        neghalf = sb("neghalf", [P, 1])
        rstd = sb("rstd", [P, 2])
        xn = sb("xn", [P, D])
        x2n = sb("x2n", [P, D])
        RX = sb("RX", [P, 4, N])
        X2T = sb("X2T", [AUG, P])
        X2B = sb("X2B", [P, 2, 66])
        R = sb("R", [P, D])
        lmax = sb("lmax", [P, NH])
        W = sb("W", [P, NH, G])
        wsum = sb("wsum", [P, NH])
        wrec = sb("wrec", [P, NH])
        Wn = sb("Wn", [P, NH, G])
        WX = sb("WX", [P, NH, 2, G])
        WT = sb("WT", [P, NH, P])
        bden = sb("bden", [P, 4, 2])
        brec = sb("brec", [P, 4, 2])
        Bn = sb("Bn", [P, 4, 2, 66])
        Bt = sb("Bt", [AUG, 4, 2, 2, G])
        T = sb("T", [AUG, NH, P])
        V = sb("V", [P, 2, 4, D])
        amax = sb("amax", [P, NH])
        A = sb("A", [P, NH, G])
        asum = sb("asum", [P, NH])
        arec = sb("arec", [P, NH])
        An = sb("An", [P, NH, G])
        M = sb("M", [P, 4, P])
        O = sb("O", [P, D])

        pX = [bank(f"pX{i}", [P, 4, P]) for i in range(2)]
        pK = [bank(f"pK{i}", [P, 512]) for i in range(2)]
        pF = bank("pF", [P, 2, 512])
        pF2 = bank("pF2", [P, 512])
        pG = bank("pG", [P, 512])

        SEMS = """
        passed x_first0 x_in0 x_first1 x_in1 windowed x2b_ones tok_zeroed ffn_zeroed ident_zero consts mask_done id_mean_done ones_set rnn_b_done
        query_in wqT_done wqT_saved tok_in tokT_done tokT_saved ffn_in ffn_blocks_in temp_done prep_pe prep_dve
        xt_done xt_saved qsum_done qtok_done qp_done qp_saved c_done c_masked kb_done bk_rep_done full_max_done shift_done qpm_done u_done u_saved
        s_done s_half s_whole smax_done s_shifted p_exp p_masked
        pt_done pt_saved0 pt_saved1 y_done y_half y_whole y_recip y_scaled yt_done yt_saved
        z_done z_masked ctx_done ctx_placed tok_done h_done stats_done0 mv_done0 vpe_done0 rstd_done0
        stats_done1 mv_done1 vpe_done1 rstd_done1
        xn_done xnt_done xnt_saved rnn_done state_done h2t_done h2_done x2n_done x2b_done
        x2t_done x2t_saved r_done
        lg_done lmax_done l_shifted w_exp wsum_done wrec_done wn_done wx_done
        b_done bden_done brec_done bn_done wt_done wt_saved bt_done bt_saved0 bt_saved1
        t_done t_saved0 t_saved1 v_done v_saved
        a_done amax_done a_shifted a_exp asum_done arec_done an_done
        m_done m_saved o_done o_added stored
        """.split()
        S = {name: ctx.enter_context(nc.semaphore("s_" + name)) for name in SEMS}

        def nth(pair, k=1, per=1):
            return per * pair + k

        def has(pair):
            return not isinstance(pair, int) or 0 <= pair < PAIRS

        LAGS = 3

        FIRST = PAIRS - (PAIRS - LAGS - 1) // 2 * 2

        def run_slots(engine, steps):
            def slot(s, j):
                def do(lag, step, *args):
                    if has(s - lag):
                        step(s - lag, (j - lag) % 2, *args)

                def once(slot, step, *args):
                    if isinstance(s, int) and s == slot:
                        step(*args)
                steps(do, once)

            for s in range(FIRST):
                slot(s, s % 2)
            with engine.Fori(FIRST, PAIRS - 1, 2) as it:
                for j in range(2):
                    slot(it + j, (FIRST + j) % 2)
            for s in range(PAIRS, PAIRS + LAGS):
                slot(s, s % 2)


        block = ctx.enter_context(nc.Block())

        QUERY_LOADS = 8
        TOK_LOADS = 10
        FFN_LOADS = 10
        FFN_BLOCK_LOADS = 6
        CONSTS = 5

        @block.sync
        def _(sp):
            def load(p, j):
                if has(p - 2):
                    sp.wait_ge(S["windowed"], nth(p - 2, 8, 8))
                    sp.sem_inc(S["passed"], 1)
                    sp.wait_ge(S["qsum_done"], nth(p - 2, 8, 8))
                    sp.sem_inc(S["passed"], 1)
                for half, name in enumerate(("x_in0", "x_in1")):
                    if has(p - 1):
                        sp.wait_ge(S[name], 16 * p)
                        sp.sem_inc(S["passed"], 1)
                    sp.dma_start(X[:, j, half * 2048:(half + 1) * 2048],
                                 x_v[p, :, half * 2048:(half + 1) * 2048]).then_inc(S[name], 16)

            def store(p):
                sp.wait_ge(S["o_added"], nth(p))
                sp.sem_inc(S["passed"], 1)
                sp.dma_start(out_v[p, :, :], O[:, :]).then_inc(S["stored"], 16)

            sp.sem_inc(S["stored"], 16)
            for i, name in enumerate(("x_first0", "x_in0", "x_first1", "x_in1")):
                sp.dma_start(X[:, 0, i * 1024:(i + 1) * 1024],
                             x_v[0, :, i * 1024:(i + 1) * 1024]).then_inc(S[name], 16)
            sp.wait_ge(S["tok_zeroed"], 1)
            halves = (slice(0, 64), slice(64, 128))
            for rows in halves:
                sp.dma_start(wq_bd[rows, rows], tWq[:, :]).then_inc(S["query_in"], 16)
                sp.dma_start(bq_col[rows, :], tbq.unsqueeze(1)).then_inc(S["query_in"], 16)
                sp.dma_start(wk_bd[rows, rows], tWk[:, :]).then_inc(S["query_in"], 16)
                sp.dma_start(bk_col[rows, :], tbk.unsqueeze(1)).then_inc(S["query_in"], 16)
            for rows in halves:
                sp.dma_start(wv_bd[rows, rows], tWv[:, :]).then_inc(S["tok_in"], 16)
                sp.dma_start(bv_col[rows, :], tbv.unsqueeze(1)).then_inc(S["tok_in"], 16)
            sp.dma_start(wo2[:, :].rearrange("p (b c) -> p b c", b=2),
                         tWo.unsqueeze(1).to_broadcast([D, 2, D])).then_inc(S["tok_in"], 16)
            sp.dma_start(wr2[:, 0:64], W_ih[:, :]).then_inc(S["tok_in"], 16)
            sp.dma_start(wr2[:, 64:128], W_hh[:, :]).then_inc(S["tok_in"], 16)
            sp.dma_start(rnn_b2[64:128, 0:1], b_ih.unsqueeze(1)).then_inc(S["tok_in"], 16)
            sp.dma_start(rnn_b2[64:128, 1:2], b_hh.unsqueeze(1)).then_inc(S["tok_in"], 16)
            sp.dma_start(bo_row[:, :], tbo.partition_broadcast(P)).then_inc(S["tok_in"], 16)
            load(1, 1)
            sp.dma_start(wfx[0:D, :], W_fx[:, :]).then_inc(S["ffn_in"], 16)
            sp.dma_start(wfx[D:AUG, :], b_fx.unsqueeze(0)).then_inc(S["ffn_in"], 16)
            sp.dma_start(wxa[0:D, :], W_x[:, :]).then_inc(S["ffn_in"], 16)
            sp.dma_start(wxa[D:AUG, :], b_x.unsqueeze(0)).then_inc(S["ffn_in"], 16)
            sp.wait_ge(S["ffn_zeroed"], 1)
            for rows in halves:
                sp.dma_start(fv_bd[rows, rows], W_v[:, :]).then_inc(S["ffn_in"], 16)
            sp.dma_start(wout[:, :, :], W_out.rearrange("(a p) c -> p a c", p=P)).then_inc(S["ffn_in"], 16)
            sp.dma_start(bout_row[:, :], b_out.partition_broadcast(P)).then_inc(S["ffn_in"], 16)
            sp.dma_start(bsl[D:AUG, :], b_slice.unsqueeze(0)).then_inc(S["ffn_in"], 16)
            sp.dma_start(temp[:, :], temperature[0, :, 0, 0].partition_broadcast(AUG)).then_inc(S["ffn_in"], 16)
            for p in range(2, 4):
                load(p, p % 2)
            with sp.Fori(4, PAIRS - 1, 2) as it:
                for j in range(2):
                    load(it + j, j)
                    store(it + j - 4)
            for p in range(PAIRS - 4, PAIRS):
                store(p)
            sp.wait_ge(S["stored"], 16 * PAIRS + 16)

        @block.gpsimd
        def _(pool):
            pool.memset(ident[:, :], 0.0).then_inc(S["ident_zero"], 1)
            pool.wait_ge(S["ident_zero"], 1)
            pool.affine_select(out=ident[:, :], in_=ident[:, :], compare_op=ALU.not_equal, fill=1.0,
                               base=0, pattern=[[-1, P]], channel_multiplier=1).then_inc(S["consts"], 1)
            for t in (wsl_bd, fq_bd, fk_bd, fv_bd):
                pool.memset(t[:, :], 0.0)
            pool.memset(neghalf[:, :], -0.5).then_inc(S["ffn_zeroed"], 1)
            pool.memset(U[:, :, :, :], 0.0).then_inc(S["consts"], 1)
            pool.memset(ctxm[:, :, :, :, :, :], 0.0).then_inc(S["consts"], 1)
            pool.memset(e_bd[:, :, :, :], 0.0).then_inc(S["consts"], 1)
            pool.memset(f_bd[:, :, :, :], 0.0).then_inc(S["consts"], 1)
            pool.wait_ge(S["ffn_zeroed"], 1)
            for h2 in range(2):
                rows = slice(64 * h2, 64 * h2 + 64)
                pool.dma_start(wsl_bd[rows, rows], W_slice[:, :]).then_inc(S["ffn_blocks_in"], 16)
                pool.dma_start(fq_bd[rows, rows], W_q[:, :]).then_inc(S["ffn_blocks_in"], 16)
                pool.dma_start(fk_bd[rows, rows], W_k[:, :]).then_inc(S["ffn_blocks_in"], 16)
            pool.wait_ge(S["mask_done"], 6)

            def wx(p, j):
                pool.wait_ge(S["wn_done"], nth(p))
                if has(p - 1):
                    pool.wait_ge(S["wt_done"], nth(p - 1, 2, 2))
                pool.sem_inc(S["passed"], 1)
                for b in range(2):
                    pool.tensor_scalar(WX[:, :, b, :], Wn[:, :, :], mask_img[:, b:b + 1], 1.0,
                                       ALU.mult, ALU.mult).then_inc(S["wx_done"], 1)

            def y_scale(p, j, r):
                g0, g1 = Y_ROUNDS[r]
                pool.wait_ge(S["y_whole"], nth(p, r + 1, 3))
                pool.wait_ge(S["y_recip"], nth(p, r + 1, 3))
                if has(p - 1):
                    pool.wait_ge(S["yt_done"], nth(p - 1))
                pool.tensor_tensor(Yn[:, g0:g1, :], Ye[:, g0:g1, :],
                                   rsum[:, g0:g1].unsqueeze(2).to_broadcast([P, g1 - g0, D]),
                                   ALU.mult).then_inc(S["y_scaled"], 1)

            def spread_q(p, j):
                pool.wait_ge(S["qp_saved"], nth(p))
                if has(p - 1):
                    pool.wait_ge(S["u_done"], nth(p - 1))
                pool.tensor_tensor(qpm[:, :, :], qp[:, :].unsqueeze(2).to_broadcast([P, N, NH]),
                                   mask_h[:, :].unsqueeze(1).to_broadcast([P, N, NH]),
                                   ALU.mult).then_inc(S["qpm_done"], 1)

            def window_tokens(p, j):
                pool.wait_ge(S["qsum_done"], nth(p, 8, 8))
                if has(p - 2):
                    pool.wait_ge(S["tok_done"], nth(p - 2))
                pool.sem_inc(S["passed"], 1)
                for b in range(2):
                    pool.tensor_scalar(qtok[:, j, b, :, :, :], qsum[:, :, :, :].rearrange("p a h w -> p a w h"),
                                       mask_img[:, b:b + 1], 1.0, ALU.mult, ALU.mult)\
                        .then_inc(S["qtok_done"], 1)

            def power(p, j, k):
                pool.wait_ge(S[f"vpe_done{k}"], nth(p))
                pool.tensor_tensor(rstd[:, k:k + 1], vpe[:, k:k + 1], neghalf[:, :], ALU.pow)\
                    .then_inc(S[f"rstd_done{k}"], 1)

            def mask_p(p, j):
                pool.wait_ge(S["p_exp"], nth(p))
                if has(p - 1):
                    pool.wait_ge(S["pt_done"], nth(p - 1, 2, 2))
                pool.sem_inc(S["passed"], 1)
                for gw in range(2):
                    pool.tensor_scalar(Pm[:, :, gw, :], Sc[:, :, :], mask_gw[:, gw:gw + 1], 1.0,
                                       ALU.mult, ALU.mult).then_inc(S["p_masked"], 1)

            def x2_blocks(p, j):
                pool.wait_ge(S["x2n_done"], nth(p))
                if has(p - 1):
                    pool.wait_ge(S["b_done"], nth(p - 1))
                pool.sem_inc(S["passed"], 1)
                for b in range(2):
                    pool.tensor_scalar(X2B[:, b, 0:D], x2n[:, :], mask_img[:, b:b + 1], 1.0,
                                       ALU.mult, ALU.mult).then_inc(S["x2b_done"], 1)

            def residual_bias(p, j):
                if isinstance(p, int) and p == 0:
                    pool.wait_ge(S["ffn_in"], 16 * FFN_LOADS)
                pool.wait_ge(S["h2_done"], nth(p))
                if has(p - 1):
                    pool.wait_ge(S["o_added"], nth(p - 1))
                pool.tensor_tensor(R[:, :], H2[:, :], bout_row[:, :], ALU.add).then_inc(S["r_done"], 1)

            def steps(do, once):
                do(1, window_tokens); do(2, y_scale, 0); do(2, y_scale, 1); do(2, y_scale, 2); do(1, spread_q)
                do(3, x2_blocks); do(3, residual_bias); do(3, wx); do(2, power, 0); do(1, mask_p)
                do(2, power, 1)

            run_slots(pool, steps)

        @block.tensor
        def _(pe):
            pe.wait_ge(S["consts"], 1)
            pe.wait_ge(S["query_in"], 16 * QUERY_LOADS)
            pe.transpose(pK[0][:, 0:P], wq_bd[:, :], ident[:, :]).then_inc(S["wqT_done"], 1)
            pe.wait_ge(S["wqT_saved"], 1)
            pe.wait_ge(S["id_mean_done"], 1)
            pe.wait_ge(S["consts"], CONSTS)

            def prepare_tokens():
                pe.wait_ge(S["tok_in"], 16 * TOK_LOADS)
                pe.transpose(pF[:, 0, P:2 * P], wv_bd[:, :], ident[:, :])
                pe.transpose(pF[:, 0, 256:320], wo2[:, :], ident[0:D, 0:D])
                pe.transpose(pF[:, 0, 320:384], wr2[:, :], ident[0:D, 0:D]).then_inc(S["tokT_done"], 1)

            def prepare_slices(step):
                if step == 1:
                    pe.wait_ge(S["ffn_in"], 16 * FFN_LOADS)
                    pe.wait_ge(S["ffn_blocks_in"], 16 * FFN_BLOCK_LOADS)
                    pe.wait_ge(S["tokT_saved"], 1)
                    for hp in range(4):
                        pe.transpose(pF[:, 0, 66 * hp:66 * hp + AUG], wfx[:, hp * P:(hp + 1) * P],
                                     ident[0:AUG, 0:AUG])
                        pe.transpose(pF[:, 1, 66 * hp:66 * hp + AUG], wxa[:, hp * P:(hp + 1) * P],
                                     ident[0:AUG, 0:AUG])
                    for k, w in enumerate((fq_bd, fk_bd, fv_bd)):
                        last = pe.transpose(pF2[:, k * P:(k + 1) * P], w[:, :], ident[:, :])
                    last.then_inc(S["prep_pe"], 1)
                if step == 2:
                    pe.wait_ge(S["prep_dve"], 1)
                    fqT, fkT, fvT = (fqkvT[:, k, :] for k in range(3))
                    pe.matmul(pF2[:, 0:P], fkT, fqT, start=True, stop=True)
                    pe.matmul(pF[:, 0, 0:4 * D], fvT, wout[:, :, :].rearrange("p a c -> p (a c)"),
                              start=True, stop=True)
                    for hp in range(4):
                        last = pe.matmul(pF[0:AUG, 1, hp * P:(hp + 1) * P], wxT[:, hp, 0:AUG], wsl_bd[:, :],
                                         start=True, stop=True)
                    last.then_inc(S["prep_pe"], 1)
                if step == 3:
                    pe.wait_ge(S["prep_dve"], 2)
                    pe.matmul(pF2[:, 0:264], mqk[:, :], wfxT[:, :, :].rearrange("p a c -> p (a c)"),
                              start=True, stop=True)
                    for hp in range(4):
                        last = pe.matmul(pF[0:AUG, 0, hp * P:(hp + 1) * P], wfxT[:, hp, 0:AUG],
                                         f_bd[:, hp, :, :].rearrange("p a c -> p (a c)"),
                                         start=True, stop=True)
                    last.then_inc(S["prep_pe"], 1)
                if step == 4:
                    pe.wait_ge(S["prep_dve"], 3)
                    for hp in range(4):
                        last = pe.matmul(pF[0:AUG, hp // 2, (hp % 2) * 132:(hp % 2) * 132 + 132],
                                         wfxT[:, hp, 0:AUG], e_bd[:, hp, :, :].rearrange("p a c -> p (a c)"),
                                         start=True, stop=True)
                    last.then_inc(S["prep_pe"], 1)

            def transpose_x(p, j, i):
                if i == 0:
                    pe.wait_ge(S["s_whole"], nth(p, 1, 2))
                elif i == 1:
                    pe.wait_ge(S["s_whole"], nth(p, 2, 2))
                else:
                    pe.wait_ge(S["xt_saved"], nth(p, i - 1, 8))
                pe.wait_ge(S["windowed"], nth(p, i // 2 * 2 + 2, 8))
                for c in range(4):
                    last = pe.transpose(pX[i % 2][:, c, :],
                                        Xw[:, j, 4 * i + c, :], ident[:, :])
                last.then_inc(S["xt_done"], 1)

            def query(p, j):
                if has(p - 2):
                    pe.wait_ge(S["x2t_saved"], nth(p - 2))
                elif has(p - 1):
                    pe.wait_ge(S["c_masked"], nth(p - 1))
                pe.wait_ge(S["qsum_done"], nth(p, 8, 8))
                pe.matmul(pG[:, 0:N], wqT, qsum[:, :, :, :].rearrange("p a h w -> p (a h w)"),
                          start=True, stop=True).then_inc(S["qp_done"], 1)

            def key_bias(p, j):
                if isinstance(p, int) and p == 0:
                    pe.wait_ge(S["bk_rep_done"], 1)
                pe.wait_ge(S["qp_saved"], nth(p))
                pe.matmul(pG[:, 0:N], bk_rep[:, :], qp[:, :], start=True, stop=True).then_inc(S["c_done"], 1)

            def keys_for_query(p, j):
                if has(p - 1):
                    pe.wait_ge(S["y_whole"], nth(p - 1, 3, 3))
                    pe.wait_ge(S["y_recip"], nth(p - 1, 3, 3))
                pe.wait_ge(S["qpm_done"], nth(p))
                pe.matmul(pK[0][:, :], wk_bd[:, :], qpm[:, :, :].rearrange("p w h -> p (w h)"),
                          start=True, stop=True).then_inc(S["u_done"], 1)

            def scores(p, j, half):
                if half == 0:
                    if has(p - 1):
                        pe.wait_ge(S["xt_saved"], nth(p - 1, 7, 8))
                elif half == 1:
                    if has(p - 1):
                        pe.wait_ge(S["xt_saved"], nth(p - 1, 8, 8))
                if half == 0:
                    pe.wait_ge(S["u_saved"], nth(p, 2, 2))
                pe.wait_ge(S["windowed"], nth(p, 4 * half + 4, 8))
                for g4 in range(4):
                    g = 4 * half + g4
                    for c in range(4):
                        gh = 4 * (g % 2) + c
                        k = (g // 2) * 8 + gh
                        last = pe.matmul(pX[half][32 * c:32 * c + 32, g4, :],
                                         U[:, 2 * k:2 * k + 2, :, :].rearrange("p w b h -> p (w b h)"),
                                         Xw[:, j, k, :], start=True, stop=True)
                last.then_inc(S["s_done"], 1)

            def transpose_p(p, j, half):
                if half == 0:
                    pe.wait_ge(S["u_saved"], nth(p, 2, 2))
                elif half == 1:
                    if has(p - 1):
                        pe.wait_ge(S["z_masked"], nth(p - 1))
                pe.wait_ge(S["p_masked"], nth(p, 2, 2))
                for g4 in range(4):
                    last = pe.transpose(pK[half][:, g4 * P:(g4 + 1) * P],
                                        Pm[:, 4 * half + g4, :, :].rearrange("p w l -> p (w l)"), ident[:, :])
                last.then_inc(S["pt_done"], 1)

            def weighted_sum(p, j, r):
                if r == 0:
                    pe.wait_ge(S["pt_saved0"], nth(p))
                elif r == 1:
                    pe.wait_ge(S["pt_saved1"], nth(p))
                elif r == 2:
                    pe.wait_ge(S["y_whole"], nth(p, 1, 3))
                    pe.wait_ge(S["y_recip"], nth(p, 1, 3))
                g0, g1 = Y_ROUNDS[r]
                pe.wait_ge(S["xt_saved"], nth(p, g1, 8))
                for g in range(g0, g1):
                    for c in range(4):
                        last = pe.matmul(pK[r % 2][32 * c:32 * c + 32, (g - g0) * XW:(g - g0 + 1) * XW],
                                         PT[:, g, 32 * c:32 * c + 32],
                                         XT[:, 4 * g + c, :], start=True, stop=True)
                last.then_inc(S["y_done"], 1)

            def transpose_y(p, j):
                pe.wait_ge(S["y_whole"], nth(p, 2, 3))
                pe.wait_ge(S["y_recip"], nth(p, 2, 3))
                pe.wait_ge(S["y_scaled"], nth(p, 3, 3))
                for a in range(4):
                    last = pe.transpose(pK[1][:, a * P:(a + 1) * P],
                                        Yn[:, 2 * a:2 * a + 2, :].rearrange("p q d -> p (q d)"), ident[:, :])
                last.then_inc(S["yt_done"], 1)

            def values(p, j):
                if isinstance(p, int) and p == 0:
                    pe.wait_ge(S["tokT_saved"], 1)
                pe.wait_ge(S["yt_saved"], nth(p))
                pe.matmul(pK[1][:, :], wvT, YT[:, :], start=True, stop=True).then_inc(S["z_done"], 1)

            def tokens(p, j):
                if has(p + 1):
                    pe.wait_ge(S["c_masked"], nth(p + 1))
                elif has(p - 1):
                    pe.wait_ge(S["x2t_saved"], nth(p - 1))
                else:
                    pe.wait_ge(S["c_masked"], nth(p))
                pe.wait_ge(S["ctx_placed"], nth(p, 4, 4))
                pe.wait_ge(S["qtok_done"], nth(p, 2, 2))
                pe.matmul(pG[:, 0:D], ctxm[:, :, :, :, :, :].rearrange("p b a w q h -> p (b a w q h)"), woT,
                          start=True, stop=False)
                pe.matmul(pG[:, 0:D], qtok[:, j, :, :, :, :].rearrange("p b a w h -> p (b a w h)"), id_mean[:, :],
                          start=False, stop=True).then_inc(S["tok_done"], 1)

            def transpose_xn(p, j):
                pe.wait_ge(S["h_done"], nth(p))
                pe.wait_ge(S["xn_done"], nth(p))
                pe.sem_inc(S["passed"], 1)
                pe.transpose(pG[0:D, 0:P], xn[:, :], ident[:, :]).then_inc(S["xnt_done"], 1)

            def recur(p, j, i):
                if i == 0:
                    pe.wait_ge(S["xnt_saved"], nth(p, 2, 2))
                elif i == 1:
                    pe.wait_ge(S["state_done"], nth(p, 1, 2))
                pe.matmul(pG[64:128, 0:N], wrT, RX[:, (2 * j + i - 1) % 4, :],
                          start=True, stop=True).then_inc(S["rnn_done"], 1)

            def transpose_h(p, j):
                pe.wait_ge(S["state_done"], nth(p, 2, 2))
                pe.sem_inc(S["passed"], 1)
                pe.transpose(pG[:, 0:D], RX[64:128, 2 * j:2 * j + 2, :].rearrange("p t n -> p (t n)"),
                             ident[64:128, 64:128]).then_inc(S["h2t_done"], 1)

            def transpose_x2(p, j):
                pe.wait_ge(S["h2_done"], nth(p))
                pe.wait_ge(S["x2n_done"], nth(p))
                pe.sem_inc(S["passed"], 1)
                pe.transpose(pG[0:D, 0:P], x2n[:, :], ident[:, :]).then_inc(S["x2t_done"], 1)

            def logits(p, j):
                if has(p - 1):
                    pe.wait_ge(S["v_saved"], nth(p - 1))
                if isinstance(p, int) and p == 0:
                    pe.wait_ge(S["prep_dve"], 4)
                pe.wait_ge(S["x2t_saved"], nth(p))
                pe.matmul(pF[:, 0, :], X2T[:, :], w_logit[:, :, :].rearrange("p h g -> p (h g)"),
                          start=True, stop=True).then_inc(S["lg_done"], 1)

            def slice_sums(p, j):
                if has(p - 1):
                    pe.wait_ge(S["t_saved0"], nth(p - 1))
                if has(p - 1):
                    pe.wait_ge(S["o_added"], nth(p - 1))
                pe.wait_ge(S["wn_done"], nth(p))
                pe.wait_ge(S["x2b_done"], nth(p, 2, 2))
                for hp in range(4):
                    last = pe.matmul((pF[:, 1, 0:264] if hp < 2 else pF2[:, 0:264])[:, (hp % 2) * 132:(hp % 2) * 132 + 132],
                                     Wn[:, 2 * hp:2 * hp + 2, :].rearrange("p h g -> p (h g)"),
                                     X2B[:, :, :].rearrange("p b c -> p (b c)"), start=True, stop=True)
                last.then_inc(S["b_done"], 1)

            def transpose_w(p, j, half):
                if half == 1:
                    pe.wait_ge(S["bn_done"], nth(p, 2, 2))
                elif half == 0:
                    if has(p - 1):
                        pe.wait_ge(S["m_saved"], nth(p - 1))
                    else:
                        pe.wait_ge(S["l_shifted"], nth(p))
                pe.wait_ge(S["wx_done"], nth(p, 2, 2))
                for h in range(4 * half, 4 * half + 4):
                    last = pe.transpose(pF[:, half, (h % 4) * P:(h % 4 + 1) * P],
                                        WX[:, h, :, :].rearrange("p b g -> p (b g)"), ident[:, :])
                last.then_inc(S["wt_done"], 1)

            def transpose_b(p, j, half):
                if half == 0:
                    pe.wait_ge(S["bn_done"], nth(p, 2, 2))
                elif half == 1:
                    pe.wait_ge(S["wt_saved"], nth(p, 1, 2))
                pe.wait_ge(S["bn_done"], nth(p, 2, 2))
                dst = pF2 if half == 0 else pF[:, 0, :]
                for i in range(4):
                    hp, b = 2 * half + i // 2, i % 2
                    last = pe.transpose(dst[0:AUG, i * P:(i + 1) * P], Bn[:, hp, b, 0:AUG], ident[:, :])
                last.then_inc(S["bt_done"], 1)

            def slice_keys(p, j, half):
                if half == 0:
                    pe.wait_ge(S["wt_saved"], nth(p, 2, 2))
                elif half == 1:
                    pe.wait_ge(S["bt_saved0"], nth(p))
                pe.wait_ge(S[("bt_saved0", "bt_saved1")[half]], nth(p))
                dst = pF[:, 1, :] if half == 0 else pF2
                for i in range(4):
                    hp, h2 = 2 * half + i // 2, i % 2
                    last = pe.matmul(dst[0:AUG, i * P:(i + 1) * P], w_qk[:, hp, h2, 0:AUG],
                                     Bt[:, hp, :, h2, :], start=True, stop=True)
                last.then_inc(S["t_done"], 1)

            def slice_values(p, j):
                pe.wait_ge(S["bt_saved0"], nth(p))
                pe.wait_ge(S["bt_saved1"], nth(p))
                for b in range(2):
                    for h in range(NH):
                        hp, h2 = h // 2, h % 2
                        last = pe.matmul(pF[64 * h2:64 * h2 + 64, 0, (4 * b + hp) * D:(4 * b + hp + 1) * D],
                                         Bt[:, hp, b, h2, :], w_vo[:, h, :], start=True, stop=True)
                last.then_inc(S["v_done"], 1)

            def slice_scores(p, j):
                pe.wait_ge(S["t_saved0"], nth(p))
                pe.wait_ge(S["t_saved1"], nth(p))
                for h in range(NH):
                    for b in range(2):
                        last = pe.matmul(pF2[64 * b:64 * b + 64, h * G:(h + 1) * G],
                                         T[:, h, 64 * b:64 * b + 64], Bt[:, h // 2, b, h % 2, :],
                                         start=True, stop=True)
                last.then_inc(S["a_done"], 1)

            def weights_times_scores(p, j):
                if has(p + 1):
                    pe.wait_ge(S["l_shifted"], nth(p + 1))
                else:
                    pe.wait_ge(S["v_saved"], nth(p))
                pe.wait_ge(S["an_done"], nth(p))
                pe.wait_ge(S["wt_saved"], nth(p, 2, 2))
                for h in range(NH):
                    rows = slice(64 * (h % 2), 64 * (h % 2) + 64)
                    last = pe.matmul(pF[rows, 0, (h // 2) * P:(h // 2 + 1) * P], An[:, h, :], WT[:, h, :],
                                     start=True, stop=True)
                last.then_inc(S["m_done"], 1)

            def project(p, j):
                pe.wait_ge(S["a_shifted"], nth(p))
                pe.wait_ge(S["m_saved"], nth(p))
                pe.wait_ge(S["v_saved"], nth(p))
                for b in range(2):
                    for hp in range(4):
                        last = pe.matmul(pF2[64 * b:64 * b + 64, 0:D], M[:, hp, 64 * b:64 * b + 64],
                                         V[:, b, hp, :], start=(hp == 0), stop=(hp == 3))
                last.then_inc(S["o_done"], 1)

            def steps(do, once):
                once(2, prepare_slices, 3); do(1, transpose_x, 0); do(3, transpose_w, 1); do(3, transpose_b, 0)
                do(1, transpose_x, 1); do(3, transpose_b, 1); do(1, transpose_x, 2); once(2, prepare_slices, 4)
                do(2, transpose_xn); do(3, slice_keys, 0); do(2, recur, 0); do(3, slice_keys, 1)
                do(2, recur, 1); do(3, slice_values); do(2, transpose_h); do(1, transpose_x, 3)
                do(3, slice_scores); once(1, prepare_slices, 1); do(1, transpose_x, 4); do(1, transpose_p, 0)
                do(1, transpose_p, 1); do(1, transpose_x, 5); do(1, weighted_sum, 0); do(2, transpose_x2)
                do(1, transpose_x, 6); do(1, transpose_x, 7); do(2, logits); do(1, weighted_sum, 1)
                do(1, weighted_sum, 2); do(0, query); once(1, prepare_slices, 2); do(3, weights_times_scores)
                do(0, key_bias); do(1, transpose_y); do(3, project); do(0, keys_for_query); do(1, values)
                do(2, slice_sums); do(0, scores, 0); do(2, transpose_w, 0); once(0, prepare_tokens)
                do(0, scores, 1); do(1, tokens)

            run_slots(pe, steps)

        @block.scalar
        def _(act):
            def by_window(p, j, i):
                if isinstance(p, int) and p == 0:
                    act.wait_ge(S[("x_first0", "x_in0", "x_first1", "x_in1")[i // 2]], 16)
                elif i % 4 == 0:
                    act.wait_ge(S[("x_in0", "x_in1")[i // 4]], nth(p, 16, 16))
                if i == 0 and has(p - 2):
                    act.wait_ge(S["xt_done"], nth(p - 2, 8, 8))
                w = Xw[:, j, 8 * (i // 2):8 * (i // 2) + 8, 64 * (i % 2):64 * (i % 2) + 64]
                act.activation(w.rearrange("p h (r c) -> p h r c", c=8),
                               X[:, j, i * 512:(i + 1) * 512].rearrange("p (r h c) -> p h r c", r=8, h=8),
                               ACT.Copy).then_inc(S["windowed"], 1)

            def save_xt(p, j, i):
                act.wait_ge(S["xt_done"], nth(p, i + 1, 8))
                if i in (0, 3, 6) and has(p - 1):
                    act.wait_ge(S["y_done"], nth(p - 1, i // 3 + 1, 3))
                act.activation(XT[:, 4 * i:4 * i + 4, 0:P], pX[i % 2][:, :, :], ACT.Copy)\
                    .then_inc(S["xt_saved"], 1)

            def save_qp(p, j):
                if isinstance(p, int) and p == 0:
                    act.wait_ge(S["query_in"], 16 * QUERY_LOADS)
                    act.wait_ge(S["consts"], CONSTS)
                    act.wait_ge(S["mask_done"], 6)
                    act.wait_ge(S["ones_set"], 1)
                    act.wait_ge(S["wqT_done"], 1)
                    act.activation(wqT, pK[0][:, 0:P], ACT.Copy).then_inc(S["wqT_saved"], 1)
                act.wait_ge(S["qp_done"], nth(p))
                if has(p - 1):
                    act.wait_ge(S["c_done"], nth(p - 1))
                if has(p - 1):
                    act.wait_ge(S["qpm_done"], nth(p - 1))
                act.activation(qp[:, :], pG[:, 0:N], ACT.Identity, bias=bq_col[:, :], scale=1.0 / L)\
                    .then_inc(S["qp_saved"], 1)

            def save_u(p, j):
                act.wait_ge(S["u_done"], nth(p))
                if has(p - 1):
                    act.wait_ge(S["s_done"], nth(p - 1, 2, 2))
                for b in range(2):
                    rows = slice(64 * b, 64 * b + 64)
                    act.activation(U[rows, :, b, :], pK[0][rows, :].rearrange("p (w h) -> p w h", h=NH),
                                   ACT.Copy, scale=DH ** -0.5).then_inc(S["u_saved"], 1)

            def half_scores(p, j, half):
                act.wait_ge(S["s_done"], nth(p, half + 1, 2))
                if has(p - 1):
                    act.wait_ge(S["s_whole"], nth(p - 1, half + 1, 2))
                act.activation(St[:, 4 * half:4 * half + 4, :],
                               pX[half][:, :, 0:L],
                               ACT.Copy, scale=mask_gw[:, 0:1]).then_inc(S["s_half"], 1)

            def exp_p(p, j):
                act.wait_ge(S["s_shifted"], nth(p))
                act.activation(Sc[:, :, :], Sc[:, :, :], ACT.Exp).then_inc(S["p_exp"], 1)

            def save_pt(p, j):
                act.wait_ge(S["pt_done"], nth(p, 1, 2))
                if has(p - 1):
                    act.wait_ge(S["y_done"], nth(p - 1, 3, 3))
                act.activation(PT[:, 0:4, :].rearrange("p g r -> p (g r)"), pK[0][:, :], ACT.Copy)\
                    .then_inc(S["pt_saved0"], 1)

            def half_y(p, j, r):
                g0, g1 = Y_ROUNDS[r]
                act.wait_ge(S["y_done"], nth(p, r + 1, 3))
                if has(p - 1):
                    act.wait_ge(S["y_whole"], nth(p - 1, r + 1, 3))
                src = pK[r % 2][:, 0:(g1 - g0) * XW].rearrange("p (g c) -> p g c", c=XW)
                act.activation(Yt[:, g0:g1, :], src[:, :, 0:D], ACT.Copy, scale=mask_b[:, 0:1])\
                    .then_inc(S["y_half"], 1)

            def save_yt(p, j):
                act.wait_ge(S["yt_done"], nth(p))
                if has(p - 1):
                    act.wait_ge(S["z_done"], nth(p - 1))
                act.activation(YT[:, :], pK[1][:, :], ACT.Copy).then_inc(S["yt_saved"], 1)

            def save_xnt(p, j):
                act.wait_ge(S["xnt_done"], nth(p))
                if has(p - 1):
                    act.wait_ge(S["rnn_done"], nth(p - 1, 2, 2))
                for i in range(2):
                    act.activation(RX[0:D, (2 * j + i - 1) % 4, :], pG[0:D, i * N:(i + 1) * N], ACT.Copy)\
                        .then_inc(S["xnt_saved"], 1)

            def state(p, j, i):
                if isinstance(p, int) and p == 0 and i == 0:
                    act.wait_ge(S["rnn_b_done"], 1)
                act.wait_ge(S["rnn_done"], nth(p, i + 1, 2))
                if i == 0 and has(p - 2):
                    act.wait_ge(S["h2t_done"], nth(p - 2))
                act.activation(RX[64:128, 2 * j + i, :], pG[64:128, 0:N], ACT.Tanh,
                               bias=rnn_b[64:128, :]).then_inc(S["state_done"], 1)

            def save_x2t(p, j):
                act.wait_ge(S["x2t_done"], nth(p))
                if has(p - 1):
                    act.wait_ge(S["lg_done"], nth(p - 1))
                act.activation(X2T[0:D, :], pG[0:D, 0:P], ACT.Copy).then_inc(S["x2t_saved"], 1)

            def exp_w(p, j):
                act.wait_ge(S["l_shifted"], nth(p))
                act.activation(W[:, :, :], W[:, :, :], ACT.Exp).then_inc(S["w_exp"], 1)

            def save_wt(p, j, half):
                act.wait_ge(S["wt_done"], nth(p, half + 1, 2))
                if half == 0 and has(p - 1):
                    act.wait_ge(S["m_done"], nth(p - 1))
                act.activation(WT[:, 4 * half:4 * half + 4, :].rearrange("p h n -> p (h n)"),
                               pF[:, half, :], ACT.Copy).then_inc(S["wt_saved"], 1)

            def save_bt1(p, j):
                act.wait_ge(S["bt_done"], nth(p, 2, 2))
                if has(p - 1):
                    act.wait_ge(S["a_done"], nth(p - 1))
                if has(p - 1):
                    act.wait_ge(S["v_done"], nth(p - 1))
                act.activation(Bt[:, 2:4, :, :, :].rearrange("p a b h g -> p (a b h g)"), pF[0:AUG, 0, :],
                               ACT.Copy).then_inc(S["bt_saved1"], 1)

            def save_t0(p, j):
                act.wait_ge(S["t_done"], nth(p, 1, 2))
                if has(p - 1):
                    act.wait_ge(S["a_done"], nth(p - 1))
                act.activation(T[:, 0:4, :].rearrange("p h g -> p (h g)"), pF[0:AUG, 1, :], ACT.Copy)\
                    .then_inc(S["t_saved0"], 1)

            def save_v(p, j):
                act.wait_ge(S["v_done"], nth(p))
                if has(p - 1):
                    act.wait_ge(S["o_done"], nth(p - 1))
                act.activation(V[:, :, :, :].rearrange("p b a c -> p (b a c)"), pF[:, 0, :], ACT.Copy)\
                    .then_inc(S["v_saved"], 1)

            def save_t1(p, j):
                act.wait_ge(S["t_done"], nth(p, 2, 2))
                if has(p - 1):
                    act.wait_ge(S["a_done"], nth(p - 1))
                act.activation(T[:, 4:8, :].rearrange("p h g -> p (h g)"), pF2[0:AUG, :], ACT.Copy)\
                    .then_inc(S["t_saved1"], 1)

            def save_bt0(p, j):
                act.wait_ge(S["bt_done"], nth(p, 1, 2))
                if has(p - 1):
                    act.wait_ge(S["a_done"], nth(p - 1))
                if has(p - 1):
                    act.wait_ge(S["v_done"], nth(p - 1))
                act.activation(Bt[:, 0:2, :, :, :].rearrange("p a b h g -> p (a b h g)"), pF2[0:AUG, :], ACT.Copy)\
                    .then_inc(S["bt_saved0"], 1)

            def exp_a(p, j):
                act.wait_ge(S["a_shifted"], nth(p))
                act.activation(A[:, :, :], A[:, :, :], ACT.Exp).then_inc(S["a_exp"], 1)

            def save_m(p, j):
                act.wait_ge(S["m_done"], nth(p))
                if has(p - 1):
                    act.wait_ge(S["o_done"], nth(p - 1))
                act.activation(M[:, :, :].rearrange("p a n -> p (a n)"), pF[:, 0, :], ACT.Copy)\
                    .then_inc(S["m_saved"], 1)

            def steps(do, once):
                do(1, by_window, 5); do(2, save_yt); do(1, save_u); do(1, by_window, 6); do(1, by_window, 7)
                do(1, half_scores, 0); do(3, save_wt, 0); do(1, half_scores, 1); do(0, by_window, 0)
                do(1, save_xt, 0); do(3, save_wt, 1); do(3, save_bt0); do(3, save_bt1); do(2, save_xnt)
                do(1, save_xt, 1); do(2, state, 0); do(3, save_t0); do(1, exp_p); do(2, state, 1)
                do(1, save_xt, 2); do(3, save_t1); do(3, save_v); do(0, by_window, 1); do(1, save_xt, 3)
                do(0, by_window, 2); do(1, save_pt); do(1, save_xt, 4); do(3, exp_a); do(1, save_xt, 5)
                do(2, save_x2t); do(1, half_y, 0); do(1, save_xt, 6); do(1, save_xt, 7); do(0, by_window, 3)
                do(1, half_y, 1); do(1, half_y, 2); do(2, exp_w); do(0, save_qp); do(3, save_m)
                do(0, by_window, 4)

            run_slots(act, steps)

        @block.vector
        def _(dve):
            for t in (wq_bd, wk_bd):
                dve.memset(t[:, :], 0.0)
            dve.memset(wv_bd[:, :], 0.0).then_inc(S["tok_zeroed"], 1)
            dve.memset(XT[:, :, P:XW], 1.0)
            dve.memset(X2T[D:AUG, :], 1.0)
            dve.memset(RX[64:128, 3, :], 0.0).then_inc(S["ones_set"], 1)
            dve.wait_ge(S["consts"], 1)
            iv = ident[:, :].rearrange("p (a w c) -> p w a c", a=4, w=2)
            dve.tensor_reduce(mask_gw[:, :], iv, AX.XY, ALU.add).then_inc(S["mask_done"], 1)
            iv = ident[:, :].rearrange("p (a b c) -> p b a c", a=8, b=2)
            dve.tensor_reduce(mask_b[:, :], iv, AX.XY, ALU.add).then_inc(S["mask_done"], 1)
            iv = ident[:, :].rearrange("p (w c) -> p w c", w=8)
            dve.tensor_reduce(mask_w[:, :], iv, AX.X, ALU.add).then_inc(S["mask_done"], 1)
            iv = ident[:, :].rearrange("p (b c) -> p b c", b=16)
            dve.tensor_reduce(mask_bh[:, :], iv, AX.X, ALU.add).then_inc(S["mask_done"], 1)
            iv = ident[:, :].rearrange("p (b c) -> p b c", b=2)
            dve.tensor_reduce(mask_img[:, :], iv, AX.X, ALU.add).then_inc(S["mask_done"], 1)
            iv = ident[:, :].rearrange("p (b h c) -> p h b c", b=2, h=NH)
            dve.tensor_reduce(mask_h[:, :], iv, AX.XY, ALU.add).then_inc(S["mask_done"], 1)
            for b in range(2):
                rows = slice(64 * b, 64 * b + 64)
                last = dve.tensor_scalar(id_mean[rows, :], ident[rows, rows], 1.0 / L, None, ALU.mult)
            last.then_inc(S["id_mean_done"], 1)
            dve.wait_ge(S["mask_done"], 6)
            for b in range(2):
                dve.tensor_copy(X2B[:, b, D:66], mask_img[:, b:b + 1].to_broadcast([P, 2])).then_inc(S["x2b_ones"], 1)

            def prepare_query():
                dve.wait_ge(S["query_in"], 16 * QUERY_LOADS)
                dve.tensor_scalar(bk_rep[:, :].rearrange("p (w m) -> p w m", w=8),
                                  mask_bh[:, :].unsqueeze(1).to_broadcast([P, 8, 16]), bk_col[:, :],
                                  DH ** -0.5, ALU.mult, ALU.mult).then_inc(S["bk_rep_done"], 1)
                dve.wait_ge(S["consts"], CONSTS)

            def prepare_tokens():
                dve.wait_ge(S["tok_in"], 16 * TOK_LOADS)
                dve.tensor_tensor(rnn_b[64:128, :], rnn_b2[64:128, 0:1], rnn_b2[64:128, 1:2], ALU.add)\
                    .then_inc(S["rnn_b_done"], 1)
                dve.wait_ge(S["tokT_done"], 1)
                dve.tensor_copy(tokT[:, P:384], pF[:, 0, P:384]).then_inc(S["tokT_saved"], 1)

            def prepare_slices(step):
                if step == 1:
                    dve.wait_ge(S["ffn_in"], 16 * FFN_LOADS)
                    dve.tensor_scalar(rtemp[:, :], temp[:, :], 0.1, 5.0, ALU.max, ALU.min)\
                        .then_inc(S["temp_done"], 1)
                    dve.wait_ge(S["temp_done"], 1)
                    dve.reciprocal(temp[:, :], rtemp[:, :]).then_inc(S["temp_done"], 1)
                    dve.wait_ge(S["prep_pe"], 1)
                    v66 = lambda t: t.rearrange("p (a c) -> p a c", c=66)[:, :, 0:AUG]
                    dve.tensor_copy(wfxT[:, :, 0:AUG], v66(pF[:, 0, 0:264]))
                    dve.tensor_copy(wxT[:, :, 0:AUG], v66(pF[:, 1, 0:264]))
                    dve.memset(wfxT[:, :, AUG:66], 0.0)
                    dve.tensor_copy(fqkvT[:, :, :].rearrange("p a c -> p (a c)"), pF2[:, 0:384])\
                        .then_inc(S["prep_dve"], 1)
                if step == 2:
                    dve.wait_ge(S["prep_pe"], 2)
                    dve.tensor_copy(mqk[:, :], pF2[:, 0:P])
                    for h2 in range(2):
                        rows = slice(64 * h2, 64 * h2 + 64)
                        dve.tensor_copy(f_bd[rows, :, h2, :],
                                        pF[rows, 0, 0:4 * D].rearrange("p (a c) -> p a c", c=D))
                    dve.tensor_copy(w_logit[:, :, :].rearrange("p h g -> p (h g)"), pF[0:AUG, 1, :])\
                        .then_inc(S["temp_done"], 1)
                    dve.wait_ge(S["temp_done"], 3)
                    dve.tensor_tensor(w_logit[D:AUG, :, :], w_logit[D:AUG, :, :],
                                      bsl[D:AUG, :].unsqueeze(1).to_broadcast([1, NH, G]), ALU.add)\
                        .then_inc(S["temp_done"], 1)
                    dve.wait_ge(S["temp_done"], 4)
                    dve.tensor_tensor(w_logit[:, :, :], w_logit[:, :, :],
                                      temp[:, :].unsqueeze(2).to_broadcast([AUG, NH, G]), ALU.mult)\
                        .then_inc(S["prep_dve"], 1)
                if step == 3:
                    dve.wait_ge(S["prep_pe"], 3)
                    for h2 in range(2):
                        rows = slice(64 * h2, 64 * h2 + 64)
                        dve.tensor_scalar(e_bd[rows, :, h2, :],
                                          pF2[rows, 0:264].rearrange("p (a c) -> p a c", c=66),
                                          float(D) ** -0.5, None, ALU.mult)
                    dve.tensor_copy(w_vo[:, :, :].rearrange("p h c -> p (h c)"), pF[0:AUG, 0, :])\
                        .then_inc(S["prep_dve"], 1)
                if step == 4:
                    dve.wait_ge(S["prep_pe"], 4)
                    for a in range(2):
                        last = dve.tensor_copy(w_qk[:, 2 * a:2 * a + 2, :, :].rearrange("p a h c -> p (a h c)"),
                                               pF[0:AUG, a, 0:264])
                    last.then_inc(S["prep_dve"], 1)

            def window_sums(p, j, i):
                if isinstance(p, int) and p == 0:
                    dve.wait_ge(S[("x_first0", "x_in0", "x_first1", "x_in1")[i // 2]], 16)
                elif i % 4 == 0:
                    dve.wait_ge(S[("x_in0", "x_in1")[i // 4]], nth(p, 16, 16))
                if i == 0 and has(p - 1):
                    dve.wait_ge(S["qp_done"], nth(p - 1))
                    dve.wait_ge(S["qtok_done"], nth(p - 1, 2, 2))
                src = X[:, j, i * 512:(i + 1) * 512].rearrange("p (r h c) -> p h r c", r=8, h=8)
                dve.tensor_reduce(qsum[:, i // 2, :, i % 2], src, AX.XY, ALU.add).then_inc(S["qsum_done"], 1)
                if isinstance(p, int) and p == 0 and i == 7:
                    prepare_query()

            def own_bias(p, j):
                dve.wait_ge(S["c_done"], nth(p))
                if has(p - 1):
                    dve.wait_ge(S["kb_done"], nth(p - 1))
                dve.tensor_tensor(kbw[:, :, :], pG[:, 0:N].rearrange("p (g w) -> p g w", w=8),
                                  mask_w[:, :].unsqueeze(1).to_broadcast([P, GROUPS, 8]), ALU.mult)\
                    .then_inc(S["c_masked"], 1)

            def sum_bias(p, j):
                dve.wait_ge(S["c_masked"], nth(p))
                if has(p - 1):
                    dve.wait_ge(S["shift_done"], nth(p - 1))
                dve.tensor_reduce(kb[:, :], kbw[:, :, :], AX.X, ALU.add).then_inc(S["kb_done"], 1)

            def whole_scores(p, j, half):
                dve.wait_ge(S["s_half"], nth(p, half + 1, 2))
                if has(p - 1):
                    dve.wait_ge(S["p_masked"], nth(p - 1, 2, 2))
                src = pX[half][:, :, L:2 * L]
                rows = slice(4 * half, 4 * half + 4)
                dve.scalar_tensor_tensor(out=Sc[:, rows, :], in0=src, scalar=mask_gw[:, 1:2],
                                         in1=St[:, rows, :], op0=ALU.mult, op1=ALU.add)\
                    .then_inc(S["s_whole"], 1)

            def score_maxima(p, j):
                dve.wait_ge(S["s_whole"], nth(p, 2, 2))
                dve.tensor_reduce(Smax[:, :], Sc[:, :, :], AX.X, ALU.max).then_inc(S["smax_done"], 1)

            def full_maxima(p, j):
                dve.wait_ge(S["smax_done"], nth(p))
                dve.wait_ge(S["kb_done"], nth(p))
                dve.tensor_tensor(full_max[:, :], Smax[:, :], kb[:, :], ALU.add).then_inc(S["full_max_done"], 1)

            def score_shifts(p, j):
                dve.wait_ge(S["full_max_done"], nth(p))
                dve.tensor_tensor(shift[:, :], full_max[:, :], kb[:, :], ALU.subtract).then_inc(S["shift_done"], 1)

            def shift_scores(p, j):
                dve.wait_ge(S["shift_done"], nth(p))
                dve.tensor_tensor(Sc[:, :, :], Sc[:, :, :],
                                  shift[:, :].unsqueeze(2).to_broadcast([P, GROUPS, L]), ALU.subtract)\
                    .then_inc(S["s_shifted"], 1)

            def save_pt(p, j):
                dve.wait_ge(S["pt_done"], nth(p, 2, 2))
                if has(p - 1):
                    dve.wait_ge(S["y_done"], nth(p - 1, 3, 3))
                dve.tensor_copy(PT[:, 4:8, :].rearrange("p g r -> p (g r)"), pK[1][:, :])\
                    .then_inc(S["pt_saved1"], 1)

            def whole_y(p, j, r):
                g0, g1 = Y_ROUNDS[r]
                dve.wait_ge(S["y_half"], nth(p, r + 1, 3))
                if has(p - 1):
                    dve.wait_ge(S["y_scaled"], nth(p - 1, r + 1, 3))
                src = pK[r % 2][:, 0:(g1 - g0) * XW].rearrange("p (g c) -> p g c", c=XW)
                dve.scalar_tensor_tensor(out=Ye[:, g0:g1, :], in0=src[:, :, D:2 * D], scalar=mask_b[:, 1:2],
                                         in1=Yt[:, g0:g1, :], op0=ALU.mult, op1=ALU.add)\
                    .then_inc(S["y_whole"], 1)
                dve.reciprocal(rsum[:, g0:g1], src[:, :, P]).then_inc(S["y_recip"], 1)

            def own_heads(p, j):
                dve.wait_ge(S["z_done"], nth(p))
                if has(p - 1):
                    dve.wait_ge(S["ctx_done"], nth(p - 1))
                dve.tensor_tensor(Zm[:, :, :], pK[1][:, :].rearrange("p (w h) -> p w h", h=NH),
                                  mask_h[:, :].unsqueeze(1).to_broadcast([P, N, NH]), ALU.mult)\
                    .then_inc(S["z_masked"], 1)

            def sum_heads(p, j):
                dve.wait_ge(S["z_masked"], nth(p))
                if has(p - 1):
                    dve.wait_ge(S["ctx_placed"], nth(p - 1, 4, 4))
                dve.tensor_reduce(ctxs[:, :], Zm[:, :, :], AX.X, ALU.add).then_inc(S["ctx_done"], 1)

            def place_context(p, j):
                dve.wait_ge(S["ctx_done"], nth(p))
                if has(p - 1):
                    dve.wait_ge(S["tok_done"], nth(p - 1))
                src = ctxs[:, :].rearrange("p (a h w b) -> p b a w h", a=4, h=4, w=2)
                for q in range(2):
                    rows = slice(64 * q, 64 * q + 64)
                    for b in range(2):
                        dve.tensor_scalar(ctxm[rows, b, :, :, q, :], src[rows, b], bv_col[rows, :], None,
                                          ALU.add).then_inc(S["ctx_placed"], 1)

            def residual(p, j):
                dve.wait_ge(S["tok_done"], nth(p))
                if has(p - 1):
                    dve.wait_ge(S["h2_done"], nth(p - 1))
                dve.tensor_tensor(H[:, :], pG[:, 0:D], bo_row[:, :], ALU.add).then_inc(S["h_done"], 1)

            def residual2(p, j):
                dve.wait_ge(S["h2t_done"], nth(p))
                if has(p - 1):
                    dve.wait_ge(S["r_done"], nth(p - 1))
                    dve.wait_ge(S["x2n_done"], nth(p - 1))
                dve.tensor_tensor(H2[:, :], pG[:, 0:D], H[:, :], ALU.add).then_inc(S["h2_done"], 1)

            def norm_stats(p, j, k):
                dve.wait_ge(S[("h_done", "h2_done")[k]], nth(p))
                dve.bn_stats(stats[:, k, :], (H, H2)[k][:, :]).then_inc(S[f"stats_done{k}"], 1)

            def norm_mean(p, j, k):
                dve.wait_ge(S[f"stats_done{k}"], nth(p))
                if has(p - 1):
                    dve.wait_ge(S[("xn_done", "x2n_done")[k]], nth(p - 1))
                dve.sem_inc(S["passed"], 1)
                dve.bn_aggr(mv[:, k, :], stats[:, k, :]).then_inc(S[f"mv_done{k}"], 1)

            def norm_eps(p, j, k):
                dve.wait_ge(S[f"mv_done{k}"], nth(p))
                dve.tensor_scalar(vpe[:, k:k + 1], mv[:, k, 1:2], EPS, None, ALU.add)\
                    .then_inc(S[f"vpe_done{k}"], 1)

            def normed(p, j):
                dve.wait_ge(S["rstd_done0"], nth(p))
                if has(p - 1):
                    dve.wait_ge(S["xnt_done"], nth(p - 1))
                dve.tensor_scalar(xn[:, :], H[:, :], mv[:, 0, 0:1], rstd[:, 0:1], ALU.subtract, ALU.mult)\
                    .then_inc(S["xn_done"], 1)

            def normed2(p, j):
                dve.wait_ge(S["rstd_done1"], nth(p))
                if has(p - 1):
                    dve.wait_ge(S["x2t_done"], nth(p - 1))
                    dve.wait_ge(S["x2b_done"], nth(p - 1, 2, 2))
                dve.tensor_scalar(x2n[:, :], H2[:, :], mv[:, 1, 0:1], rstd[:, 1:2], ALU.subtract, ALU.mult)\
                    .then_inc(S["x2n_done"], 1)

            def logit_maxima(p, j):
                dve.wait_ge(S["lg_done"], nth(p))
                dve.tensor_reduce(lmax[:, :], pF[:, 0, :].rearrange("p (h g) -> p h g", g=G), AX.X, ALU.max)\
                    .then_inc(S["lmax_done"], 1)

            def shift_logits(p, j):
                dve.wait_ge(S["lmax_done"], nth(p))
                if has(p - 1):
                    dve.wait_ge(S["wn_done"], nth(p - 1))
                dve.tensor_tensor(W[:, :, :], pF[:, 0, :].rearrange("p (h g) -> p h g", g=G),
                                  lmax[:, :].unsqueeze(2).to_broadcast([P, NH, G]),
                                  ALU.subtract).then_inc(S["l_shifted"], 1)

            def weight_sums(p, j):
                dve.wait_ge(S["w_exp"], nth(p))
                dve.tensor_reduce(wsum[:, :], W[:, :, :], AX.X, ALU.add).then_inc(S["wsum_done"], 1)

            def weight_scales(p, j):
                dve.wait_ge(S["wsum_done"], nth(p))
                dve.reciprocal(wrec[:, :], wsum[:, :]).then_inc(S["wrec_done"], 1)

            def slice_weights(p, j):
                dve.wait_ge(S["wrec_done"], nth(p))
                if has(p - 1):
                    dve.wait_ge(S["b_done"], nth(p - 1))
                    dve.wait_ge(S["wx_done"], nth(p - 1, 2, 2))
                dve.tensor_tensor(Wn[:, :, :], W[:, :, :], wrec[:, :].unsqueeze(2).to_broadcast([P, NH, G]),
                                  ALU.mult).then_inc(S["wn_done"], 1)

            def slice_sizes(p, j):
                dve.wait_ge(S["b_done"], nth(p))
                for i, src in enumerate((pF[:, 1, :], pF2)):
                    dve.tensor_scalar(bden[:, 2 * i:2 * i + 2, :],
                                      src[:, 0:264].rearrange("p (a b c) -> p a b c", a=2, b=2)[:, :, :, D],
                                      1e-5, None, ALU.add).then_inc(S["bden_done"], 1)

            def slice_scales(p, j):
                dve.wait_ge(S["bden_done"], nth(p, 2, 2))
                dve.reciprocal(brec[:, :, :], bden[:, :, :]).then_inc(S["brec_done"], 1)

            def slice_means(p, j):
                dve.wait_ge(S["brec_done"], nth(p))
                if has(p - 1):
                    dve.wait_ge(S["bt_done"], nth(p - 1, 2, 2))
                for i, src in enumerate((pF[:, 1, :], pF2)):
                    dve.tensor_tensor(Bn[:, 2 * i:2 * i + 2, :, :],
                                      src[:, 0:264].rearrange("p (a b c) -> p a b c", a=2, b=2),
                                      brec[:, 2 * i:2 * i + 2, :].unsqueeze(3).to_broadcast([P, 2, 2, 66]),
                                      ALU.mult).then_inc(S["bn_done"], 1)

            def slice_maxima(p, j):
                dve.wait_ge(S["a_done"], nth(p))
                dve.tensor_reduce(amax[:, :], pF2[:, :].rearrange("p (h g) -> p h g", g=G), AX.X, ALU.max)\
                    .then_inc(S["amax_done"], 1)

            def shift_slices(p, j):
                dve.wait_ge(S["amax_done"], nth(p))
                if has(p - 1):
                    dve.wait_ge(S["an_done"], nth(p - 1))
                dve.tensor_tensor(A[:, :, :], pF2[:, :].rearrange("p (h g) -> p h g", g=G),
                                  amax[:, :].unsqueeze(2).to_broadcast([P, NH, G]),
                                  ALU.subtract).then_inc(S["a_shifted"], 1)

            def slice_exp_sums(p, j):
                dve.wait_ge(S["a_exp"], nth(p))
                dve.tensor_reduce(asum[:, :], A[:, :, :], AX.X, ALU.add).then_inc(S["asum_done"], 1)

            def slice_exp_scales(p, j):
                dve.wait_ge(S["asum_done"], nth(p))
                dve.reciprocal(arec[:, :], asum[:, :]).then_inc(S["arec_done"], 1)

            def slice_attention(p, j):
                dve.wait_ge(S["arec_done"], nth(p))
                if has(p - 1):
                    dve.wait_ge(S["m_done"], nth(p - 1))
                dve.tensor_tensor(An[:, :, :], A[:, :, :], arec[:, :].unsqueeze(2).to_broadcast([P, NH, G]),
                                  ALU.mult).then_inc(S["an_done"], 1)

            def add_out(p, j):
                dve.wait_ge(S["o_done"], nth(p))
                dve.wait_ge(S["r_done"], nth(p))
                dve.wait_ge(S["stored"], 16 * p + 16)
                dve.tensor_tensor(O[:, :], pF2[:, 0:D], R[:, :], ALU.add).then_inc(S["o_added"], 1)

            def steps(do, once):
                do(0, window_sums, 0); do(1, own_bias); once(2, prepare_slices, 2); do(1, sum_bias)
                do(2, own_heads); do(2, sum_heads); do(3, slice_sizes); do(3, slice_scales)
                do(2, place_context); once(1, prepare_tokens); do(1, whole_scores, 0); do(3, slice_means)
                do(2, residual); do(2, norm_stats, 0); do(1, whole_scores, 1); do(2, norm_mean, 0)
                do(2, norm_eps, 0); once(2, prepare_slices, 3); do(1, score_maxima); do(2, normed)
                do(1, full_maxima); do(1, score_shifts); do(1, shift_scores); do(0, window_sums, 1)
                do(0, window_sums, 2); do(0, window_sums, 3); do(0, window_sums, 4); do(0, window_sums, 5)
                do(2, residual2); do(2, norm_stats, 1); do(2, norm_mean, 1); do(2, norm_eps, 1)
                do(0, window_sums, 6); do(3, slice_maxima); do(2, normed2); once(2, prepare_slices, 4)
                do(3, shift_slices); do(1, save_pt); do(0, window_sums, 7); do(3, slice_exp_sums)
                do(3, slice_exp_scales); do(1, whole_y, 0); do(3, slice_attention); do(2, logit_maxima)
                do(2, shift_logits); once(1, prepare_slices, 1); do(1, whole_y, 1); do(1, whole_y, 2)
                do(2, weight_sums); do(2, weight_scales); do(2, slice_weights); do(3, add_out)

            run_slots(dve, steps)


_INS = ["x", "L0_tok_Wq", "L0_tok_bq", "L0_tok_Wk", "L0_tok_bk", "L0_tok_Wv", "L0_tok_bv", "L0_tok_Wo",
        "L0_tok_bo", "L0_attn_W_ih", "L0_attn_W_hh", "L0_attn_b_ih", "L0_attn_b_hh", "L0_ffn_W_fx",
        "L0_ffn_b_fx", "L0_ffn_W_x", "L0_ffn_b_x", "L0_ffn_W_slice", "L0_ffn_b_slice", "L0_ffn_W_q",
        "L0_ffn_W_k", "L0_ffn_W_v", "L0_ffn_W_out", "L0_ffn_b_out", "L0_ffn_temperature"]


def kernel(**inputs):
    import numpy as _np
    import concourse.bacc as _bacc
    from concourse import mybir as _mybir
    from concourse.bass_utils import run_bass_kernel_spmd as _run

    nc = _bacc.Bacc("TRN2", target_bir_lowering=False, num_devices=1)
    arrays, args = {}, []
    for name in _INS:
        a = _np.ascontiguousarray(inputs[name])
        arrays[f"in_{name}"] = a
        args.append(nc.dram_tensor(f"in_{name}", a.shape, _mybir.dt.from_np(a.dtype), kind="ExternalInput").ap())
    out = nc.dram_tensor("out_0", (16, 64, 64), _mybir.dt.float32, kind="ExternalOutput").ap()
    vit_tower_kernel(nc, *args, out)
    r = _run(nc, [arrays], core_ids=[0])
    return r.results[0]["out_0"]
```
